# Optimizing a Trainium2 kernel written in Bass

```python
import numpy as np
import jax
import jax.numpy as jnp

def _softmax(x, axis=-1):
    return jax.nn.softmax(x, axis=axis)

def _gelu(x):
    return jax.nn.gelu(x, approximate=True)

def _silu(x):
    return jax.nn.silu(x)

def _sigmoid(x):
    return jax.nn.sigmoid(x)

def _layernorm(x, axis=-1, eps=1e-05):
    m = jnp.mean(x, axis=axis, keepdims=True)
    v = jnp.var(x, axis=axis, keepdims=True)
    return (x - m) / jnp.sqrt(v + eps)

def _scatter_add(tgt, idx, src, axis=0):
    return tgt.at[idx].add(src)

def _segment_sum(src, seg, n):
    return jax.ops.segment_sum(src, seg, n)
kernel_name = 'mk_flamingo_gated_d1_seqx_r4_1bb2ea'

def setup_inputs(seed: int=0):
    np.random.seed(seed)
    _w = jnp.asarray

    def _rec_inputs():
        import jax
        import jax.numpy as jnp
        _rk = jax.random.key(seed)
        x = 7.22e-05 + 1 * jax.random.normal(jax.random.fold_in(_rk, 1), (4, 512, 256), jnp.float32)
        _lenS = 512 - jax.random.randint(jax.random.fold_in(_rk, 7), (4,), 0, max(1, 512 // 4) + 1, jnp.int32)
        _lenS2 = 1601 - jax.random.randint(jax.random.fold_in(_rk, 8), (4,), 0, max(1, 1601 // 4) + 1, jnp.int32)
        _ctx_1024P = jax.random.normal(jax.random.fold_in(_rk, 11), (4, 16, 256), jnp.float32)
        _ctx_1024c = jax.random.dirichlet(jax.random.fold_in(_rk, 511), 0.3 * jnp.ones((16,), jnp.float32), (4, 1601))
        _ctx_1024t = jnp.einsum('bsk,bkd->bsd', _ctx_1024c, _ctx_1024P)
        _ctx_1024t = _ctx_1024t * jax.lax.rsqrt(jnp.mean(jnp.square(_ctx_1024t)) + 1e-12) * 0.953939
        ctx_1024 = 4.13588e-05 + 0.999923 * (_ctx_1024t + 0.3 * jax.random.normal(jax.random.fold_in(_rk, 611), (4, 1601, 256), jnp.float32))
        _g = jax.random.normal(jax.random.fold_in(_rk, 9001), (2, 1), jnp.float32)
        _g = jnp.sign(_g) * jnp.maximum(jnp.abs(_g), 1.0) + (_g == 0) * 1.0
        g_xattn = _g[0]
        g_ffn = _g[1]
        return (x, ctx_1024, g_xattn, g_ffn)
    x, ctx_1024, g_xattn, g_ffn = _rec_inputs()

    def _L0_xattn_setup():
        import jax, jax.numpy as jnp
        import numpy as np
        D_MODEL = 256
        H = 16
        D_K = D_MODEL // H

        def _split_heads(x):
            b, s, d = x.shape
            return x.reshape(b, s, H, D_K).transpose(0, 2, 1, 3)
        key = jax.random.key(seed)
        ks = jax.random.split(key, 11)
        B, S = (4, 512)
        scale = 1.0 / np.sqrt(D_MODEL)
        inp = {'q': jax.random.normal(ks[0], (B, S, D_MODEL), jnp.float32), 'k': jax.random.normal(ks[1], (B, S, D_MODEL), jnp.float32), 'v': jax.random.normal(ks[2], (B, S, D_MODEL), jnp.float32), 'wq': jax.random.normal(ks[3], (D_MODEL, D_MODEL), jnp.float32) * scale, 'bq': jax.random.normal(ks[4], (D_MODEL,), jnp.float32) * 0.02, 'wk': jax.random.normal(ks[5], (D_MODEL, D_MODEL), jnp.float32) * scale, 'bk': jax.random.normal(ks[6], (D_MODEL,), jnp.float32) * 0.02, 'wv': jax.random.normal(ks[7], (D_MODEL, D_MODEL), jnp.float32) * scale, 'bv': jax.random.normal(ks[8], (D_MODEL,), jnp.float32) * 0.02, 'wo': jax.random.normal(ks[9], (D_MODEL, D_MODEL), jnp.float32) * scale, 'bo': jax.random.normal(ks[10], (D_MODEL,), jnp.float32) * 0.02}
        return inp
    _L0_xattn_all = _L0_xattn_setup()
    _L0_xattn_in = {k: v for k, v in _L0_xattn_all.items() if k in ('wq', 'bq', 'wk', 'bk', 'wv', 'bv', 'wo', 'bo')}
    del _L0_xattn_all

    def _L0_ffn_setup():
        import jax, jax.numpy as jnp
        import numpy as np
        ALPHA = 1.5
        TEMP = 1.0
        N_ITER = 25
        THRESH = 1e-09

        def entmax_bisect(X, alpha=ALPHA, n_iter=N_ITER):
            d = X.shape[-1]
            inv_am1 = 1.0 / (alpha - 1.0)
            Xs = X * (alpha - 1.0)
            max_val = jnp.max(Xs, axis=-1, keepdims=True)
            tau_lo = max_val - 1.0
            tau_hi = max_val - (1.0 / d) ** (alpha - 1.0)
            f_lo = jnp.sum(jnp.maximum(Xs - tau_lo, 0.0) ** inv_am1, axis=-1, keepdims=True) - 1.0

            def body(i, carry):
                tau_lo, dm, _ = carry
                dm = dm * 0.5
                tau_m = tau_lo + dm
                f_m = jnp.sum(jnp.maximum(Xs - tau_m, 0.0) ** inv_am1, axis=-1, keepdims=True) - 1.0
                tau_lo = jnp.where(f_m * f_lo >= 0.0, tau_m, tau_lo)
                return (tau_lo, dm, tau_m)
            dm0 = tau_hi - tau_lo
            _, _, tau_m = jax.lax.fori_loop(0, n_iter, body, (tau_lo, dm0, tau_lo))
            p = jnp.maximum(Xs - tau_m, 0.0) ** inv_am1
            return p / jnp.sum(p, axis=-1, keepdims=True)
        key = jax.random.key(seed)
        ks = jax.random.split(key, 8)
        B, S, D, E = (2, 256, 256, 8)
        F = 4 * D
        return {'x': jax.random.normal(ks[0], (B, S, D), jnp.float32), 'Wr': jax.random.normal(ks[1], (D, E), jnp.float32) * 0.02, 'br': jnp.zeros((E,), jnp.float32), 'W1': jax.random.normal(ks[2], (E, D, F), jnp.float32) * 0.02, 'b1': jnp.zeros((E, F), jnp.float32), 'W2': jax.random.normal(ks[3], (E, F, D), jnp.float32) * 0.02, 'b2': jnp.zeros((E, D), jnp.float32)}
    _L0_ffn_all = _L0_ffn_setup()
    _L0_ffn_in = {k: v for k, v in _L0_ffn_all.items() if k in ('Wr', 'br', 'W1', 'b1', 'W2', 'b2')}
    del _L0_ffn_all
    return {'x': x, 'ctx_1024': ctx_1024, 'g_xattn': g_xattn, 'g_ffn': g_ffn, 'L0_xattn_wq': _L0_xattn_in['wq'], 'L0_xattn_bq': _L0_xattn_in['bq'], 'L0_xattn_wk': _L0_xattn_in['wk'], 'L0_xattn_bk': _L0_xattn_in['bk'], 'L0_xattn_wv': _L0_xattn_in['wv'], 'L0_xattn_bv': _L0_xattn_in['bv'], 'L0_xattn_wo': _L0_xattn_in['wo'], 'L0_xattn_bo': _L0_xattn_in['bo'], 'L0_ffn_Wr': _L0_ffn_in['Wr'], 'L0_ffn_br': _L0_ffn_in['br'], 'L0_ffn_W1': _L0_ffn_in['W1'], 'L0_ffn_b1': _L0_ffn_in['b1'], 'L0_ffn_W2': _L0_ffn_in['W2'], 'L0_ffn_b2': _L0_ffn_in['b2']}

def reference(x, ctx_1024, g_xattn, g_ffn, L0_xattn_wq, L0_xattn_bq, L0_xattn_wk, L0_xattn_bk, L0_xattn_wv, L0_xattn_bv, L0_xattn_wo, L0_xattn_bo, L0_ffn_Wr, L0_ffn_br, L0_ffn_W1, L0_ffn_b1, L0_ffn_W2, L0_ffn_b2):
    import jax
    import jax.numpy as jnp

    def _L0_xattn_ref(q, k, v, wq, bq, wk, bk, wv, bv, wo, bo):
        import jax, jax.numpy as jnp
        import numpy as np
        D_MODEL = 256
        H = 16
        D_K = D_MODEL // H

        def _split_heads(x):
            b, s, d = x.shape
            return x.reshape(b, s, H, D_K).transpose(0, 2, 1, 3)
        qh = _split_heads(q @ wq + bq)
        kh = _split_heads(k @ wk + bk)
        vh = _split_heads(v @ wv + bv)
        scores = jnp.einsum('bhsk,bhtk->bhst', qh, kh) / np.sqrt(D_K)
        attn = jax.nn.softmax(scores, axis=-1)
        wv_ = jnp.einsum('bhst,bhtk->bhsk', attn, vh)
        b, h, s, dk = wv_.shape
        cv = wv_.transpose(0, 2, 1, 3).reshape(b, s, h * dk)
        return cv @ wo + bo

    def _L0_ffn_ref(x, Wr, br, W1, b1, W2, b2):
        import jax, jax.numpy as jnp
        import numpy as np
        ALPHA = 1.5
        TEMP = 1.0
        N_ITER = 25
        THRESH = 1e-09

        def entmax_bisect(X, alpha=ALPHA, n_iter=N_ITER):
            d = X.shape[-1]
            inv_am1 = 1.0 / (alpha - 1.0)
            Xs = X * (alpha - 1.0)
            max_val = jnp.max(Xs, axis=-1, keepdims=True)
            tau_lo = max_val - 1.0
            tau_hi = max_val - (1.0 / d) ** (alpha - 1.0)
            f_lo = jnp.sum(jnp.maximum(Xs - tau_lo, 0.0) ** inv_am1, axis=-1, keepdims=True) - 1.0

            def body(i, carry):
                tau_lo, dm, _ = carry
                dm = dm * 0.5
                tau_m = tau_lo + dm
                f_m = jnp.sum(jnp.maximum(Xs - tau_m, 0.0) ** inv_am1, axis=-1, keepdims=True) - 1.0
                tau_lo = jnp.where(f_m * f_lo >= 0.0, tau_m, tau_lo)
                return (tau_lo, dm, tau_m)
            dm0 = tau_hi - tau_lo
            _, _, tau_m = jax.lax.fori_loop(0, n_iter, body, (tau_lo, dm0, tau_lo))
            p = jnp.maximum(Xs - tau_m, 0.0) ** inv_am1
            return p / jnp.sum(p, axis=-1, keepdims=True)
        B, S, D = x.shape
        xt = x.reshape(B * S, D)
        logits = (xt @ Wr + br) / TEMP
        gates = entmax_bisect(logits)
        gates = jnp.where(gates > THRESH, gates, 0.0)
        h = jax.nn.relu(jnp.einsum('td,edf->etf', xt, W1) + b1[:, None, :])
        y = jnp.einsum('etf,efd->etd', h, W2) + b2[:, None, :]
        out = jnp.einsum('etd,te->td', y, gates)
        return out.reshape(B, S, D)
    x = x + jnp.tanh(g_xattn[0]) * _L0_xattn_ref(_layernorm(x, axis=-1), ctx_1024, ctx_1024, L0_xattn_wq, L0_xattn_bq, L0_xattn_wk, L0_xattn_bk, L0_xattn_wv, L0_xattn_bv, L0_xattn_wo, L0_xattn_bo)
    x = x + jnp.tanh(g_ffn[0]) * _L0_ffn_ref(_layernorm(x, axis=-1), L0_ffn_Wr, L0_ffn_br, L0_ffn_W1, L0_ffn_b1, L0_ffn_W2, L0_ffn_b2)
    return x

_drawn_inputs = setup_inputs


def setup_inputs(seed=0):
    import zlib

    import numpy as np

    out = dict(_drawn_inputs(seed))
    spreads = {'L0_ffn_br': (0.0, 0.34), 'L0_ffn_b1': (0.0, 0.432), 'L0_ffn_b2': (0.0, 0.1)}
    factors = {'L0_xattn_bq': 8.0, 'L0_xattn_bk': 8.0, 'L0_xattn_bv': 4.311, 'L0_xattn_bo': 3.861}
    for name, (base, spread) in spreads.items():
        noise = np.random.default_rng([zlib.crc32(name.encode()), seed]).standard_normal(out[name].shape)
        drawn = base * np.exp(spread * noise) if base else spread * noise
        out[name] = jnp.asarray(drawn.astype(out[name].dtype))
    for name, factor in factors.items():
        out[name] = (out[name] * factor).astype(out[name].dtype)
    return out
```

```python
import concourse.bass as bass
from concourse import mybir
from contextlib import ExitStack

fp32 = mybir.dt.float32
f32r = mybir.dt.float32r
bf16 = mybir.dt.bfloat16
ALU = mybir.AluOpType
ACT = mybir.ActivationFunctionType
AX = mybir.AxisListType


def flamingo_block(nc, x, ctx, g_xattn, g_ffn, wq, bq, wk, bk, wv, bv, wo, bo,
                   Wr, br, W1, b1, W2, b2, out):
    B, S, D = x.shape
    T = ctx.shape[1]
    H = 16
    DK = D // H
    E, F = b1.shape
    KT = D // 128
    ST = S // 128
    NT = B * ST
    TP = 124
    TN = -(-T // TP)
    CT = 4
    CW = CT * TP
    NC = -(-T // CW)
    HG = 4
    NG = H // HG
    STRIP = 32
    KPARTS = (0, 0, 1, 1, 0, 2)
    QPARTS = (0, 1, 0, 1, 2, 0)
    NB = len(KPARTS)
    KS = NB * DK
    KM = KS + 3
    HALF = 1024
    FT = F // 128
    TBS = S
    NTB = B * S // TBS
    EPS = 1e-5
    BISECT = 25
    THRESH = 1e-9

    def tile_rows(n):
        return min(TP, T - n * TP)

    def chunk_cols(c):
        return min(CW, T - c * CW)

    kd = nc.dram_tensor("k_parts_dram", (B, 3, D, T), bf16).ap()
    qd = nc.dram_tensor("q_parts_dram", (B, 3, D, S), bf16).ap()
    vd = nc.dram_tensor("v_strips_dram", (B, 128, NG * TN * HG * STRIP), fp32).ap()

    with ExitStack() as es:
        def sb(name, shape, dt=fp32):
            return es.enter_context(nc.sbuf_tensor(name, shape, dt))

        def sem(name):
            return es.enter_context(nc.semaphore(name))

        wide = es.enter_context(nc.psum_tensor("wide", [128, 4 * 512], fp32))
        ring = es.enter_context(nc.psum_tensor("ring", [128, 3 * 512], fp32))
        pv_acc = es.enter_context(nc.psum_tensor("pv_acc", [128, 512], fp32))
        bank = [wide[:, 512 * i:512 * i + 512] for i in range(4)] + \
               [ring[:, 512 * i:512 * i + 512] for i in range(3)] + [pv_acc[:, :]]

        ident = sb("ident", [128, 128])
        ident_bf = sb("ident_bf", [128, 128], bf16)
        x_all = sb("x_all", [128, NT, D])
        attn = sb("attn", [128, NT, D])
        BROWS = E * FT + 2 * KT
        bias_rows = sb("bias_rows", [BROWS, 128])
        bias_c = sb("bias_c", [128, BROWS])
        bk_c = bias_c[:, E * FT:E * FT + KT]
        bq_c = bias_c[:, E * FT + KT:BROWS]
        b1_c = bias_c[:, 0:E * FT]
        bv_b = sb("bv_b", [128, D])
        bo_b = sb("bo_b", [128, D])
        br_b = sb("br_b", [128, E])
        wr_raw = sb("wr_raw", [128, KT, E])
        wr_hi = sb("wr_hi", [128, KT, E], f32r)
        wr_lo = sb("wr_lo", [128, KT, E], f32r)
        gates_raw = sb("gates_raw", [128, 2])
        tg = sb("tg", [128, 2])
        stats = sb("stats", [128, ST, 6])
        mv = sb("mv", [128, ST, 2])
        vpe = sb("vpe", [128, ST])
        rstd = sb("rstd", [128, ST])
        neg_half = sb("neg_half", [128, ST])
        wo_hi = sb("wo_hi", [128, KT, D], f32r)
        wo_lo = sb("wo_lo", [128, KT, D], f32r)

        sems = {}

        def S_(name):
            if name not in sems:
                sems[name] = sem(name)
            return sems[name]

        def wait_apart(eng, semaphore, value):
            if not isinstance(value, int):
                value = eng.snap(eng.to_reg(value))
            eng.wait_ge(S_("consts"), 2)
            eng.wait_ge(semaphore, value)

        with ExitStack() as ph:
            def sb0(name, shape, dt=fp32):
                return ph.enter_context(nc.sbuf_tensor(name, shape, dt))

            w_raw = [sb0(f"w_raw{i}", [128, KT, D]) for i in range(4)]
            w_hi = [sb0(f"w_hi{i}", [128, KT, D], f32r) for i in range(3)] + [wo_hi]
            w_lo = [sb0(f"w_lo{i}", [128, KT, D], f32r) for i in range(3)] + [wo_lo]
            ctx_in = sb0("ctx_in", [128, TN, D])
            cT_hi = sb0("cT_hi", [128, KT, T + 1], f32r)
            cT_lo = sb0("cT_lo", [128, KT, T + 1], f32r)
            xn = sb0("xn", [128, ST, D])
            xT_hi = sb0("xT_hi", [128, KT, S], f32r)
            xT_lo = sb0("xT_lo", [128, KT, S], f32r)
            full = [sb0(f"full{m}", [128, S]) for m in range(KT)]
            rest = [sb0(f"rest{m}", [128, S]) for m in range(KT)]
            kp = [sb0(f"kp{i}", [128, 3, KT, CW], bf16) for i in range(2)]
            qp = sb0("qp", [128, 3, KT, S], bf16)
            v_out = sb0("v_out", [128, NG, TN, HG, STRIP])

            JOBS = [("k", 0), ("k", 1), ("q", 0), ("k", 2), ("k", 3)]
            NJ = 2 * len(JOBS)

            def job_cols(kind, c):
                return chunk_cols(c) if kind == "k" else S

            def job_out(kind, c, part, m):
                return kp[c % 2][:, part, m, 0:chunk_cols(c)] if kind == "k" else qp[:, part, m, :]

            job_at = {job: 2 * i for i, job in enumerate(JOBS)}

            with nc.Block() as block:
                @block.sync
                def _(eng):
                    def load_ctx(b, c):
                        tiles = [n for n in range(CT * c, min(CT * c + CT, TN))]
                        rows = tile_rows(tiles[0])
                        src = ctx[b, c * CW:c * CW + chunk_cols(c), :]
                        eng.dma_start(ctx_in[0:rows, tiles[0]:tiles[-1] + 1, :],
                                      src.rearrange("(n p) d -> p n d", p=rows)).then_inc(S_(f"ctx_in{c}"), 16)

                    def store_k(b, c):
                        for part in range(3):
                            eng.dma_start(
                                kd[b, part, :, c * CW:c * CW + chunk_cols(c)].rearrange("(m p) t -> p m t", p=128),
                                kp[c % 2][:, part, :, 0:chunk_cols(c)]).then_inc(S_(f"kp_out{c % 2}"), 16)

                    def batch(b, load_next):
                        def nxt(c):
                            if load_next:
                                eng.wait_ge(S_("ctx_tr"), b * 2 * NC + 2 * c + 2)
                                load_ctx(b + 1, c)
                        nxt(0)
                        nxt(1)
                        for kind, c in JOBS:
                            eng.wait_ge(S_("parts_made"), b * NJ + job_at[kind, c] + 2)
                            if kind == "k":
                                store_k(b, c)
                                if c in (0, 1):
                                    nxt(c + 2)
                            else:
                                for part in range(3):
                                    eng.dma_start(qd[b, part, :, :].rearrange("(m p) t -> p m t", p=128),
                                                  qp[:, part, :, :]).then_inc(S_("qp_out"), 16)
                        eng.wait_ge(S_("v_made"), TN * b + TN)
                        eng.dma_start(vd[b, :, :], v_out[:, :, :, :, :].rearrange("p g n h c -> p (g n h c)"))\
                           .then_inc(S_("v_out_done"), 16)

                    load_ctx(0, 0)
                    for i, w in enumerate((wq, wk, wv, wo)):
                        eng.dma_start(w_raw[(0, 1, 2, 3)[i]][:, :, :], w.rearrange("(k p) n -> p k n", p=128))\
                           .then_inc(S_(f"w_in{i}"), 16)
                    eng.dma_start(bias_rows[E * FT:E * FT + KT, :], bk.rearrange("(m p) -> m p", p=128))\
                       .then_inc(S_("bias_in"), 16)
                    eng.dma_start(bias_rows[E * FT + KT:BROWS, :], bq.rearrange("(m p) -> m p", p=128))\
                       .then_inc(S_("bias_in"), 16)
                    eng.dma_start(bias_rows[0:E * FT, :], b1.rearrange("e (f p) -> (e f) p", p=128))\
                       .then_inc(S_("bias_in"), 16)
                    eng.dma_start(bv_b[:, :], bv.rearrange("(a n) -> a n", a=1).broadcast_to([128, D]))\
                       .then_inc(S_("bv_in"), 16)
                    for c in range(1, NC):
                        load_ctx(0, c)
                    for b in range(B):
                        eng.dma_start(x_all[:, ST * b:ST * b + ST, :], x[b, :, :].rearrange("(i p) d -> p i d", p=128))\
                           .then_inc(S_(f"x_in{b}"), 16)
                    eng.dma_start(bo_b[:, :], bo.rearrange("(a n) -> a n", a=1).broadcast_to([128, D]))\
                       .then_inc(S_("late_in"), 16)
                    eng.dma_start(br_b[:, :], br.rearrange("(a n) -> a n", a=1).broadcast_to([128, E]))\
                       .then_inc(S_("late_in"), 16)
                    eng.dma_start(wr_raw[:, :, :], Wr.rearrange("(k p) n -> p k n", p=128)).then_inc(S_("late_in"), 16)
                    for i, g in enumerate((g_xattn, g_ffn)):
                        eng.dma_start(gates_raw[:, i:i + 1], g.rearrange("(a n) -> a n", a=1).broadcast_to([128, 1]))\
                           .then_inc(S_("late_in"), 16)
                    with eng.Fori(0, B - 1) as b:
                        batch(b, True)
                    batch(B - 1, False)
                    eng.wait_ge(S_("kp_out0"), 16 * 3 * 2 * B)
                    eng.wait_ge(S_("kp_out1"), 16 * 3 * 2 * B)
                    eng.wait_ge(S_("qp_out"), 16 * 3 * B)
                    eng.wait_ge(S_("v_out_done"), 16 * B)

                @block.gpsimd
                def _(eng):
                    eng.memset(ident[:, :], 0.0).then_inc(S_("consts"), 1)
                    eng.wait_ge(S_("consts"), 1)
                    eng.affine_select(out=ident[:, :], in_=ident[:, :], compare_op=ALU.not_equal, fill=1.0,
                                      base=0, pattern=[[-1, 128]], channel_multiplier=1).then_inc(S_("consts"), 1)
                    eng.memset(neg_half[:, :], -0.5).then_inc(S_("consts"), 1)
                    eng.wait_ge(S_("consts"), 3)
                    eng.tensor_copy(ident_bf[:, :], ident[:, :]).then_inc(S_("consts"), 1)
                    for t in (cT_hi, cT_lo):
                        eng.memset(t[:, :, T:T + 1].bitcast(fp32), 0.0).then_inc(S_("pad_zero"), 1)
                    eng.memset(v_out[:, :, :, :, :].rearrange("p g n h c -> p (g n h c)"), 0.0)\
                       .then_inc(S_("v_init"), 1)
                    eng.wait_ge(S_("v_init"), 1)
                    eng.memset(v_out[:, :, :, :, DK:DK + 1].rearrange("p g n h c -> p (g n h c)"), 1.0)\
                       .then_inc(S_("v_init"), 1)
                    with eng.Fori(0, B) as b:
                        wait_apart(eng, S_("stats_made"), b + 1)
                        wait_apart(eng, S_("rstd_made"), b)
                        eng.tensor_scalar(vpe[:, :], mv[:, :, 1], EPS, None, ALU.add).then_inc(S_("var_made"), 1)
                        eng.wait_ge(S_("var_made"), b + 1)
                        eng.tensor_tensor(rstd[:, :], vpe[:, :], neg_half[:, :], ALU.pow).then_inc(S_("rstd_made"), 1)
                        for kind, c in JOBS:
                            for m in range(KT):
                                i, w = job_at[kind, c] + m, job_cols(kind, c)
                                eng.wait_ge(S_("first_made"), b * NJ + i + 1)
                                eng.wait_ge(S_("parts_made"), b * NJ + max(i - 1, 0))
                                eng.tensor_tensor(rest[m][:, 0:w], full[m][:, 0:w], job_out(kind, c, 0, m),
                                                  ALU.subtract).then_inc(S_("rest_made"), 1)

                @block.scalar
                def _(eng):
                    for i in (1, 2, 0, 3):
                        eng.wait_ge(S_(f"w_in{i}"), 16)
                        eng.activation(w_hi[i][:, :, :], w_raw[i][:, :, :], ACT.Copy).then_inc(S_("w_hi"), 1)
                    eng.wait_ge(S_("bias_turned"), 1)
                    eng.activation(bias_c[:, :], bank[7][:, 0:BROWS], ACT.Copy).then_inc(S_("bias_made"), 1)
                    eng.wait_ge(S_("bias_made"), 1)

                    def hi(b, c, k):
                        eng.wait_ge(S_("ctx_tr"), b * 2 * NC + 2 * c + k + 1)
                        eng.activation(cT_hi[:, k, c * CW:c * CW + chunk_cols(c)], bank[k][:, 0:chunk_cols(c)],
                                       ACT.Copy).then_inc(S_("c_hi"), 1)

                    def job(b, kind, c, m):
                        i, w = job_at[kind, c] + m, job_cols(kind, c)
                        eng.wait_ge(S_("proj_made"), b * NJ + i + 1)
                        eng.wait_ge(S_("rest_made"), b * NJ + max(i - 1, 0))
                        bias = bk_c if kind == "k" else bq_c
                        src = bank[2 + m] if kind == "k" else bank[6 + m]
                        eng.activation(full[m][:, 0:w], src[:, 0:w], ACT.Identity,
                                       bias=bias[:, m:m + 1]).then_inc(S_("full_made"), 1)

                    with eng.Fori(0, B) as b:
                        for c in (0, 1):
                            for k in range(KT):
                                hi(b, c, k)
                        job(b, "k", 0, 0)
                        job(b, "k", 0, 1)
                        for k in range(KT):
                            eng.wait_ge(S_("x_tr"), b * KT + k + 1)
                            eng.activation(xT_hi[:, k, :], bank[6 + k], ACT.Copy).then_inc(S_("x_hi"), 1)
                        for k in range(KT):
                            hi(b, 2, k)
                        job(b, "k", 1, 0)
                        job(b, "k", 1, 1)
                        job(b, "q", 0, 0)
                        job(b, "q", 0, 1)
                        for k in range(KT):
                            hi(b, 3, k)
                        for c in (2, 3):
                            job(b, "k", c, 0)
                            job(b, "k", c, 1)

                @block.vector
                def _(eng):
                    for n, i in enumerate((1, 2, 0, 3)):
                        eng.wait_ge(S_("w_hi"), n + 1)
                        eng.tensor_tensor(w_lo[i][:, :, :], w_raw[i][:, :, :], w_hi[i][:, :, :].bitcast(fp32),
                                          ALU.subtract).then_inc(S_("w_lo"), 1)
                    eng.wait_ge(S_("bv_in"), 16)
                    eng.wait_ge(S_("v_init"), 2)
                    for b in range(B):
                        eng.wait_ge(S_(f"x_in{b}"), 16)

                    def lo(b, c, k):
                        cols = slice(c * CW, c * CW + chunk_cols(c))
                        eng.wait_ge(S_("c_hi"), b * 2 * NC + 2 * c + k + 1)
                        eng.tensor_tensor(cT_lo[:, k, cols], bank[k][:, 0:chunk_cols(c)],
                                          cT_hi[:, k, cols].bitcast(fp32), ALU.subtract).then_inc(S_("c_lo"), 1)

                    def first(b, kind, c, m):
                        i, w = job_at[kind, c] + m, job_cols(kind, c)
                        eng.wait_ge(S_("full_made"), b * NJ + i + 1)
                        if m == 0:
                            if kind == "k":
                                eng.wait_ge(S_(f"kp_out{c % 2}"), (b * 2 + c // 2) * 48)
                            else:
                                eng.wait_ge(S_("qp_out"), b * 48)
                        eng.tensor_copy(job_out(kind, c, 0, m), full[m][:, 0:w]).then_inc(S_("first_made"), 1)

                    def others(b, kind, c, m):
                        i, w = job_at[kind, c] + m, job_cols(kind, c)
                        eng.wait_ge(S_("rest_made"), b * NJ + i + 1)
                        eng.tensor_copy(job_out(kind, c, 1, m), rest[m][:, 0:w]).then_inc(S_("second_made"), 1)
                        eng.wait_ge(S_("second_made"), b * NJ + i + 1)
                        eng.tensor_tensor(job_out(kind, c, 2, m), rest[m][:, 0:w], job_out(kind, c, 1, m),
                                          ALU.subtract).then_inc(S_("parts_made"), 1)

                    def v_rows(b, n):
                        rows = tile_rows(n)
                        if n == 0:
                            eng.wait_ge(S_("v_out_done"), b * 16)
                        eng.wait_ge(S_("v_proj"), b * TN + n + 1)
                        eng.tensor_tensor(v_out[0:rows, :, n, :, 0:DK],
                                          bank[4 + n % 2][0:rows, 0:D].rearrange("p (g h c) -> p g h c", g=NG, h=HG),
                                          bv_b[0:rows, :].rearrange("p (g h c) -> p g h c", g=NG, h=HG),
                                          ALU.add).then_inc(S_("v_made"), 1)

                    def kv(b, c):
                        first(b, "k", c, 0)
                        first(b, "k", c, 1)
                        tiles = list(range(CT * c, min(CT * c + CT, TN)))
                        for m in range(KT):
                            for n in tiles[2 * m:2 * m + 2]:
                                v_rows(b, n)
                            others(b, "k", c, m)

                    with eng.Fori(0, B) as b:
                        for i in range(ST):
                            eng.bn_stats(stats[:, i, :], x_all[:, bass.ds(b * ST + i, 1), :]
                                         .rearrange("p a d -> p (a d)")).then_inc(S_("bn_made"), 1)
                        lo(b, 0, 0)
                        lo(b, 0, 1)
                        wait_apart(eng, S_("bn_made"), b * ST + ST)
                        for i in range(ST):
                            last = eng.bn_aggr(mv[:, i, :], stats[:, i, :])
                        last.then_inc(S_("stats_made"), 1)
                        lo(b, 1, 0)
                        lo(b, 1, 1)
                        eng.wait_ge(S_("rstd_made"), b + 1)
                        eng.wait_ge(S_("x_tr"), b * KT)
                        for i in range(ST):
                            eng.tensor_scalar(xn[:, i, :],
                                              x_all[:, bass.ds(b * ST + i, 1), :].rearrange("p a d -> p (a d)"),
                                              mv[:, i, 0:1], rstd[:, i:i + 1], ALU.subtract, ALU.mult)\
                               .then_inc(S_("xn_made"), 1)
                        kv(b, 0)
                        for k in range(KT):
                            eng.wait_ge(S_("x_hi"), b * KT + k + 1)
                            eng.tensor_tensor(xT_lo[:, k, :], bank[6 + k], xT_hi[:, k, :].bitcast(fp32),
                                              ALU.subtract).then_inc(S_("x_lo"), 1)
                        lo(b, 2, 0)
                        lo(b, 2, 1)
                        kv(b, 1)
                        first(b, "q", 0, 0)
                        first(b, "q", 0, 1)
                        lo(b, 3, 0)
                        lo(b, 3, 1)
                        others(b, "q", 0, 0)
                        others(b, "q", 0, 1)
                        kv(b, 2)
                        kv(b, 3)
                        eng.wait_ge(S_("xn_made"), b * ST + ST)

                @block.tensor
                def _(eng):
                    eng.wait_ge(S_("consts"), 2)
                    eng.wait_ge(S_("bias_in"), 48)
                    eng.transpose(bank[7][:, 0:BROWS], bias_rows[:, :], ident[0:BROWS, 0:BROWS])\
                       .then_inc(S_("bias_turned"), 1)
                    eng.wait_ge(S_("bias_made"), 1)

                    def turn_ctx(b, c):
                        tiles = list(range(CT * c, min(CT * c + CT, TN)))
                        eng.wait_ge(S_(f"ctx_in{c}"), b * 16 + 16)
                        for k in range(KT):
                            eng.wait_ge(S_("c_lo"), b * 2 * NC + (2 * c - 2 + k + 1 if c else 0))
                            for n in tiles:
                                rows = tile_rows(n)
                                o = (n - tiles[0]) * TP
                                last = eng.transpose(bank[k][:, o:o + rows], ctx_in[0:rows, n, 128 * k:128 * k + 128],
                                                     ident[0:rows, 0:rows])
                            last.then_inc(S_("ctx_tr"), 1)

                    def three(out_ap, lhs, rhs):
                        n = 0
                        for k in range(KT):
                            for a, c in ((0, 0), (0, 1), (1, 0)):
                                last = eng.matmul(out_ap, lhs(a, k), rhs(c, k), start=(n == 0), stop=(n == 3 * KT - 1))
                                n += 1
                        return last

                    def project_k(b, c):
                        cols = slice(c * CW, c * CW + chunk_cols(c) + chunk_cols(c) % 2)
                        w = chunk_cols(c) + chunk_cols(c) % 2
                        eng.wait_ge(S_("c_lo"), b * 2 * NC + 2 * c + 2)
                        for m in range(KT):
                            eng.wait_ge(S_("full_made"), b * NJ + (job_at["k", c - 1] + m + 1 if c else 0))
                            three(bank[2 + m][:, 0:w],
                                  lambda a, k: (w_hi, w_lo)[a][1][:, k, 128 * m:128 * m + 128],
                                  lambda a, k: (cT_hi, cT_lo)[a][:, k, cols]).then_inc(S_("proj_made"), 1)

                    def project_v(b, c):
                        for n in range(CT * c, min(CT * c + CT, TN)):
                            rows = tile_rows(n)
                            eng.wait_ge(S_("v_made"), b * TN + (n - 1 if n > 1 else 0))
                            three(bank[4 + n % 2][0:rows, 0:D],
                                  lambda a, k: (cT_hi, cT_lo)[a][:, k, n * TP:n * TP + rows],
                                  lambda a, k: (w_hi, w_lo)[a][2][:, k, :]).then_inc(S_("v_proj"), 1)

                    eng.wait_ge(S_("pad_zero"), 2)
                    with eng.Fori(0, B) as b:
                        turn_ctx(b, 0)
                        turn_ctx(b, 1)
                        eng.wait_ge(S_("w_lo"), 4)
                        project_k(b, 0)
                        project_v(b, 0)
                        eng.wait_ge(S_("xn_made"), b * ST + ST)
                        for k in range(KT):
                            eng.wait_ge(S_("full_made"), b * NJ)
                            for i in range(ST):
                                last = eng.transpose(bank[6 + k][:, 128 * i:128 * i + 128],
                                                     xn[:, i, 128 * k:128 * k + 128], ident[:, :])
                            last.then_inc(S_("x_tr"), 1)
                        turn_ctx(b, 2)
                        project_k(b, 1)
                        project_v(b, 1)
                        eng.wait_ge(S_("x_lo"), b * KT + KT)
                        for m in range(KT):
                            three(bank[6 + m],
                                  lambda a, k: (w_hi, w_lo)[a][0][:, k, 128 * m:128 * m + 128],
                                  lambda a, k: (xT_hi, xT_lo)[a][:, k, :]).then_inc(S_("proj_made"), 1)
                        turn_ctx(b, 3)
                        project_k(b, 2)
                        project_v(b, 2)
                        project_k(b, 3)
                        project_v(b, 3)

        TILES = NG * TN
        EXPS = TILES * HG
        PR = 4
        UNITS = HG * ST * 2
        MAXES = UNITS + 1

        with ExitStack() as ph:
            def sb1(name, shape, dt=fp32):
                return ph.enter_context(nc.sbuf_tensor(name, shape, dt))

            k_st = [sb1(f"k_st{i}", [128, HG, T], bf16) for i in range(NG)]
            q_st = [sb1(f"q_st{i}", [128, HG, S], bf16) for i in range(NG)]
            v_st = [sb1(f"v_st{i}", [128, TN, HG * STRIP]) for i in range(2)]
            prob = [sb1(f"prob{i}", [128, HG, S]) for i in range(PR)]
            o_sb = sb1("o_sb", [128, S])
            rec = sb1("rec", [128, ST, HG])
            mx2 = sb1("mx2", [128, ST, HG, 2])
            mx = sb1("mx", [128, ST, HG])
            mrest = sb1("mrest", [128, 2, ST, HG])
            mparts = sb1("mparts", [128, ST, HG, 3], bf16)
            mrow = sb1("mrow", [HG * 3, S], bf16)
            slot = [wide[:, 0:1024], wide[:, 1024:2048]]
            m_turned = bank[0].bitcast(bf16)

            def after(b, hg):
                return (b, hg + 1) if hg < NG - 1 else (b + 1, 0)

            with nc.Block() as block:
                @block.sync
                def _(eng):
                    def load_kq(b, hg):
                        for j in range(NB):
                            eng.dma_start(q_st[hg][DK * j:DK * j + DK, :, :],
                                          qd[b, QPARTS[j], hg * HG * DK:(hg + 1) * HG * DK, :]
                                          .rearrange("(h d) s -> d h s", d=DK)).then_inc(S_(f"q_in{hg}"), 16)
                            eng.dma_start(k_st[hg][DK * j:DK * j + DK, :, :],
                                          kd[b, KPARTS[j], hg * HG * DK:(hg + 1) * HG * DK, :]
                                          .rearrange("(h d) t -> d h t", d=DK)).then_inc(S_(f"k_in{hg}"), 16)

                    def load_v(b, hg):
                        cols = TN * HG * STRIP
                        eng.dma_start(v_st[hg % 2][:, :, :].rearrange("p n c -> p (n c)"),
                                      vd[b, :, hg * cols:(hg + 1) * cols]).then_inc(S_(f"v_in{hg % 2}"), 16)

                    def store_max(b, hg):
                        eng.wait_ge(S_("max_read"), (b * NG + hg + 1) * MAXES)
                        for h in range(HG):
                            eng.dma_start(q_st[hg][KS:KM, h, :], mrow[3 * h:3 * h + 3, :])\
                               .then_inc(S_(f"m_in{hg}"), 16)

                    def group(b, hg, last):
                        two = (b, hg + 2) if hg < NG - 2 else (b + 1, hg + 2 - NG)
                        if not (last and hg >= NG - 2):
                            eng.wait_ge(S_("scores_made"), b * EXPS + hg * TN * HG)
                            load_kq(*two)
                        if not (last and hg == NG - 1):
                            store_max(*after(b, hg))
                        if not (last and hg >= NG - 2):
                            eng.wait_ge(S_("pv_tile"), b * TILES + (hg + 1) * TN)
                            load_v(*two)

                    for hg in (0, 1):
                        load_kq(0, hg)
                        load_v(0, hg)
                    store_max(0, 0)
                    with eng.Fori(0, B - 1) as b:
                        for hg in range(NG):
                            group(b, hg, False)
                    for hg in range(NG):
                        group(B - 1, hg, True)

                @block.gpsimd
                def _(eng):
                    for i in range(NG):
                        eng.memset(k_st[i][KS:KM, :, :], -1.0).then_inc(S_("minus_ones"), 1)

                @block.scalar
                def _(eng):
                    def group(b, hg):
                        for n in range(TN):
                            tt, rows = hg * TN + n, tile_rows(n)
                            eng.wait_ge(S_("pv_tile"), b * TILES + (tt - PR + 1 if tt >= PR else 0))
                            for h in range(HG):
                                i = tt * HG + h
                                eng.wait_ge(S_("scores_made"), b * EXPS + i + 1)
                                eng.activation(prob[tt % PR][0:rows, h, :], bank[4 + i % 3][0:rows, :], ACT.Exp,
                                               scale=float(DK) ** -0.5).then_inc(S_("exp_made"), 1)

                    with eng.Fori(0, B) as b:
                        for hg in range(NG):
                            group(b, hg)

                @block.vector
                def _(eng):
                    def maxima(q):
                        for u in range(UNITS):
                            h, st, half = u // (2 * ST), u // 2 % ST, u % 2
                            w = T - HALF if half else HALF
                            eng.wait_ge(S_("max_scores"), q * MAXES + u + 1)
                            eng.tensor_reduce(mx2[:, st, h, half:half + 1], slot[u % 2][:, 0:w], AX.X, ALU.max)\
                               .then_inc(S_("max_read"), 1)
                        eng.wait_ge(S_("max_read"), q * MAXES + UNITS)
                        eng.tensor_reduce(mx[:, :, :], mx2[:, :, :, :], AX.X, ALU.max).then_inc(S_("m_step"), 1)
                        eng.wait_ge(S_("m_step"), q * 6 + 1)
                        eng.tensor_copy(mparts[:, :, :, 0], mx[:, :, :]).then_inc(S_("m_step"), 1)
                        eng.wait_ge(S_("m_step"), q * 6 + 2)
                        eng.tensor_tensor(mrest[:, 0, :, :], mx[:, :, :], mparts[:, :, :, 0], ALU.subtract)\
                           .then_inc(S_("m_step"), 1)
                        eng.wait_ge(S_("m_step"), q * 6 + 3)
                        eng.tensor_copy(mparts[:, :, :, 1], mrest[:, 0, :, :]).then_inc(S_("m_step"), 1)
                        eng.wait_ge(S_("m_step"), q * 6 + 4)
                        eng.tensor_tensor(mrest[:, 1, :, :], mrest[:, 0, :, :], mparts[:, :, :, 1], ALU.subtract)\
                           .then_inc(S_("m_step"), 1)
                        eng.wait_ge(S_("m_step"), q * 6 + 5)
                        eng.tensor_copy(mparts[:, :, :, 2], mrest[:, 1, :, :]).then_inc(S_("m_step"), 1)
                        eng.wait_ge(S_("max_scores"), q * MAXES + MAXES)

                    def rows_out(q):
                        eng.tensor_copy(mrow[:, :], m_turned[0:3 * HG, 0:S]).then_inc(S_("max_read"), 1)

                    def group(b, hg, last):
                        if not last:
                            maxima(b * NG + hg + 1)
                            eng.wait_ge(S_(f"m_in{hg}"), (b + 1) * 16 * HG)
                            rows_out(b * NG + hg + 1)
                        q = b * NG + hg
                        eng.wait_ge(S_("pv_tile"), b * TILES + (hg + 1) * TN)
                        eng.tensor_copy(o_sb[:, :], pv_acc[:, :]).then_inc(S_("o_copied"), 1)
                        eng.wait_ge(S_("o_turned"), q + 1)
                        eng.wait_ge(S_("o_done"), q)
                        turned = pv_acc[:, :].rearrange("p (i h c) -> p i h c", i=ST, h=HG)
                        eng.reciprocal(rec[:, :, :], turned[:, :, :, DK]).then_inc(S_("rec_made"), 1)
                        eng.wait_ge(S_("rec_made"), q + 1)
                        eng.tensor_tensor(
                            attn[:, bass.ds(b * ST, ST), hg * HG * DK:(hg + 1) * HG * DK]
                            .rearrange("p i (h c) -> p i h c", h=HG),
                            turned[:, :, :, 0:DK],
                            rec[:, :, :].rearrange("p i (h a) -> p i h a", a=1).broadcast_to([128, ST, HG, DK]),
                            ALU.mult).then_inc(S_("o_done"), 1)

                    maxima(0)
                    rows_out(0)
                    with eng.Fori(0, B - 1) as b:
                        for hg in range(NG):
                            group(b, hg, False)
                    for hg in range(NG):
                        group(B - 1, hg, hg == NG - 1)

                @block.tensor
                def _(eng):
                    def max_unit(b, hg, u):
                        q = b * NG + hg
                        h, st, half = u // (2 * ST), u // 2 % ST, u % 2
                        if u == 0:
                            eng.wait_ge(S_(f"q_in{hg}"), (b + 1) * 16 * NB)
                            eng.wait_ge(S_(f"k_in{hg}"), (b + 1) * 16 * NB)
                        eng.wait_ge(S_("max_read"), q * MAXES + (u - 1 if u > 1 else 0))
                        lo_, hi_ = (HALF, T) if half else (0, HALF)
                        for o in range(lo_, hi_, 512):
                            w = min(512, hi_ - o)
                            last = eng.matmul(slot[u % 2][:, o - lo_:o - lo_ + w],
                                              q_st[hg][0:KS, h, 128 * st:128 * st + 128],
                                              k_st[hg][0:KS, h, o:o + w], start=True, stop=True)
                        last.then_inc(S_("max_scores"), 1)

                    def turn_max(b, hg):
                        q = b * NG + hg
                        eng.wait_ge(S_("m_step"), q * 6 + 6)
                        eng.wait_ge(S_("max_read"), q * MAXES + UNITS)
                        for i in range(ST):
                            last = eng.transpose(m_turned[0:3 * HG, 128 * i:128 * i + 128],
                                                 mparts[:, i, :, :].rearrange("p h c -> p (h c)"), ident_bf[:, :])
                        last.then_inc(S_("max_scores"), 1)

                    def scores(b, hg, n, h):
                        tt, rows = hg * TN + n, tile_rows(n)
                        i = tt * HG + h
                        eng.wait_ge(S_("exp_made"), b * EXPS + (i - 2 if i > 2 else 0))
                        return eng.matmul(bank[4 + i % 3][0:rows, :], k_st[hg][0:KM, h, n * TP:n * TP + rows],
                                          q_st[hg][0:KM, h, :], start=True, stop=True)\
                                  .then_inc(S_("scores_made"), 1)

                    def weigh_v(b, hg, n):
                        tt, rows = hg * TN + n, tile_rows(n)
                        if n == 0:
                            eng.wait_ge(S_("o_done"), b * NG + hg)
                            eng.wait_ge(S_(f"v_in{hg % 2}"), (b * 2 + hg // 2 + 1) * 16)
                        eng.wait_ge(S_("exp_made"), b * EXPS + tt * HG + HG)
                        for h in range(HG):
                            last = eng.matmul(pv_acc[STRIP * h:STRIP * h + STRIP, :],
                                              v_st[hg % 2][0:rows, n, STRIP * h:STRIP * h + STRIP],
                                              prob[tt % PR][0:rows, h, :], start=(n == 0), stop=(n == TN - 1))
                        last.then_inc(S_("pv_tile"), 1)

                    def group(b, hg, last_group):
                        nxt = after(b, hg)
                        todo = [] if last_group else list(range(UNITS))
                        eng.wait_ge(S_(f"m_in{hg}"), (b + 1) * 16 * HG)

                        def some(k):
                            for _ in range(min(k, len(todo))):
                                max_unit(*nxt, todo.pop(0))

                        for n in range(TN):
                            scores(b, hg, n, 0)
                            some(1)
                            scores(b, hg, n, 1)
                            scores(b, hg, n, 2)
                            if n:
                                weigh_v(b, hg, n - 1)
                            some(1)
                            scores(b, hg, n, 3)
                            some(1 if n % 3 != 2 else 0)
                        if not last_group:
                            some(len(todo))
                            turn_max(*nxt)
                        weigh_v(b, hg, TN - 1)
                        eng.wait_ge(S_("o_copied"), b * NG + hg + 1)
                        for i in range(ST):
                            last = eng.transpose(pv_acc[:, 128 * i:128 * i + 128], o_sb[:, 128 * i:128 * i + 128],
                                                 ident[:, :])
                        last.then_inc(S_("o_turned"), 1)

                    eng.wait_ge(S_("minus_ones"), NG)
                    for u in range(UNITS):
                        max_unit(0, 0, u)
                    turn_max(0, 0)
                    with eng.Fori(0, B - 1) as b:
                        for hg in range(NG):
                            group(b, hg, False)
                    for hg in range(NG):
                        group(B - 1, hg, hg == NG - 1)

        def mix_buffers(ph):
            def sb2(name, shape, dt=fp32):
                return ph.enter_context(nc.sbuf_tensor(name, shape, dt))
            return dict(
                xT_hi=sb2("x2T_hi", [128, KT, NT * 128], f32r), xT_lo=sb2("x2T_lo", [128, KT, NT * 128], f32r),
                logits=sb2("logits", [128, NT, E]),
                w1_raw=sb2("w1_raw", [128, KT, F]), w2_raw=sb2("w2_raw", [128, FT, D]),
                w1=[[sb2(f"w1_{p}{i}", [128, KT, F], f32r) for p in ("hi", "lo")] for i in range(2)],
                w2=[[sb2(f"w2_{p}{i}", [128, FT, D], f32r) for p in ("hi", "lo")] for i in range(2)])

        ph2 = es.enter_context(ExitStack())
        mb = mix_buffers(ph2)
        x2T_hi, x2T_lo, logits = mb["xT_hi"], mb["xT_lo"], mb["logits"]

        with ExitStack() as ph:
            def sb3(name, shape, dt=fp32):
                return ph.enter_context(nc.sbuf_tensor(name, shape, dt))

            a_st = sb3("a_st", [128, ST, D])
            aT_hi = sb3("aT_hi", [128, KT, S], f32r)
            aT_lo = sb3("aT_lo", [128, KT, S], f32r)
            o_bias = sb3("o_bias", [128, ST, D])
            y_st = sb3("y_st", [128, ST, D])
            yT_hi = sb3("yT_hi", [128, KT, S], f32r)
            yT_lo = sb3("yT_lo", [128, KT, S], f32r)

            with nc.Block() as block:
                @block.gpsimd
                def _(eng):
                    with eng.Fori(0, B) as b:
                        wait_apart(eng, S_("stats2_made"), b + 1)
                        wait_apart(eng, S_("rstd2_made"), b)
                        eng.tensor_scalar(vpe[:, :], mv[:, :, 1], EPS, None, ALU.add).then_inc(S_("var2_made"), 1)
                        eng.wait_ge(S_("var2_made"), b + 1)
                        eng.tensor_tensor(rstd[:, :], vpe[:, :], neg_half[:, :], ALU.pow).then_inc(S_("rstd2_made"), 1)

                @block.scalar
                def _(eng):
                    eng.wait_ge(S_("late_in"), 80)
                    eng.activation(tg[:, :], gates_raw[:, :], ACT.Tanh).then_inc(S_("tanh_made"), 1)
                    eng.activation(wr_hi[:, :, :], wr_raw[:, :, :], ACT.Copy).then_inc(S_("wr_hi"), 1)
                    with eng.Fori(0, B) as b:
                        eng.wait_ge(S_("a_turned"), b * KT)
                        eng.activation(a_st[:, :, :], attn[:, bass.ds(b * ST, ST), :], ACT.Copy)\
                           .then_inc(S_("a_copied"), 1)
                        for k in range(KT):
                            eng.wait_ge(S_("a_turned"), b * KT + k + 1)
                            eng.wait_ge(S_("o_proj"), b * ST)
                            eng.activation(aT_hi[:, k, :], bank[k], ACT.Copy).then_inc(S_("a_hi"), 1)
                        for k in range(KT):
                            eng.wait_ge(S_("y_turned"), b * KT + k + 1)
                            eng.wait_ge(S_("y_kept"), b * 2)
                            eng.activation(yT_hi[:, k, :], bank[4 + k], ACT.Copy).then_inc(S_("y_hi"), 1)

                @block.vector
                def _(eng):
                    eng.wait_ge(S_("wr_hi"), 1)
                    eng.tensor_tensor(wr_lo[:, :, :], wr_raw[:, :, :], wr_hi[:, :, :].bitcast(fp32), ALU.subtract)\
                       .then_inc(S_("wr_lo"), 1)
                    eng.wait_ge(S_("tanh_made"), 1)
                    with eng.Fori(0, B) as b:
                        for k in range(KT):
                            eng.wait_ge(S_("a_hi"), b * KT + k + 1)
                            eng.tensor_tensor(aT_lo[:, k, :], bank[k], aT_hi[:, k, :].bitcast(fp32), ALU.subtract)\
                               .then_inc(S_("a_lo"), 1)
                        for j in range(ST // 2):
                            eng.wait_ge(S_("o_proj"), b * ST + 2 * j + 2)
                            eng.tensor_tensor(o_bias[:, 2 * j:2 * j + 2, :],
                                              bank[2 + j].rearrange("p (i d) -> p i d", i=2),
                                              bo_b[:, :].rearrange("p (a d) -> p a d", a=1).broadcast_to([128, 2, D]),
                                              ALU.add).then_inc(S_("o_biased"), 1)
                        eng.wait_ge(S_("o_biased"), b * (ST // 2) + ST // 2)
                        rows = x_all[:, bass.ds(b * ST, ST), :].rearrange("p i d -> p (i d)")
                        eng.scalar_tensor_tensor(rows, o_bias[:, :, :].rearrange("p i d -> p (i d)"), tg[:, 0:1],
                                                 rows, ALU.mult, ALU.add).then_inc(S_("x2_made"), 1)
                        wait_apart(eng, S_("x2_made"), b + 1)
                        for i in range(ST):
                            last = eng.bn_stats(stats[:, i, :], x_all[:, bass.ds(b * ST + i, 1), :]
                                                .rearrange("p a d -> p (a d)"))
                        last.then_inc(S_("bn2_made"), 1)
                        wait_apart(eng, S_("bn2_made"), b + 1)
                        for i in range(ST):
                            last = eng.bn_aggr(mv[:, i, :], stats[:, i, :])
                        last.then_inc(S_("stats2_made"), 1)
                        eng.wait_ge(S_("rstd2_made"), b + 1)
                        eng.wait_ge(S_("y_turned"), b * KT)
                        for i in range(ST):
                            last = eng.tensor_scalar(y_st[:, i, :],
                                                     x_all[:, bass.ds(b * ST + i, 1), :].rearrange("p a d -> p (a d)"),
                                                     mv[:, i, 0:1], rstd[:, i:i + 1], ALU.subtract, ALU.mult)
                        last.then_inc(S_("yn_made"), 1)
                        for k in range(KT):
                            eng.wait_ge(S_("y_hi"), b * KT + k + 1)
                            eng.wait_ge(S_("y_kept"), b * 2)
                            eng.tensor_tensor(yT_lo[:, k, :], bank[4 + k], yT_hi[:, k, :].bitcast(fp32),
                                              ALU.subtract).then_inc(S_("y_lo"), 1)
                        eng.tensor_copy(x2T_hi[:, :, bass.ds(b * S, S)], yT_hi[:, :, :].bitcast(fp32))\
                           .then_inc(S_("y_kept"), 1)
                        eng.wait_ge(S_("y_lo"), b * KT + KT)
                        eng.tensor_copy(x2T_lo[:, :, bass.ds(b * S, S)], yT_lo[:, :, :].bitcast(fp32))\
                           .then_inc(S_("y_kept"), 1)
                        eng.wait_ge(S_("routed"), b + 1)
                        eng.tensor_tensor(logits[:, bass.ds(b * ST, ST), :],
                                          bank[6][:, 0:ST * E].rearrange("p (i e) -> p i e", i=ST),
                                          br_b[:, :].rearrange("p (a e) -> p a e", a=1).broadcast_to([128, ST, E]),
                                          ALU.add).then_inc(S_("logits_made"), 1)
                        eng.wait_ge(S_("yn_made"), b + 1)
                        eng.wait_ge(S_("y_kept"), b * 2 + 2)

                @block.tensor
                def _(eng):
                    def three(out_ap, lhs, rhs):
                        n = 0
                        for k in range(KT):
                            for a, c in ((0, 0), (0, 1), (1, 0)):
                                last = eng.matmul(out_ap, lhs(a, k), rhs(c, k), start=(n == 0), stop=(n == 3 * KT - 1))
                                n += 1
                        return last

                    eng.wait_ge(S_("wr_lo"), 1)
                    with eng.Fori(0, B) as b:
                        eng.wait_ge(S_("a_copied"), b + 1)
                        for k in range(KT):
                            eng.wait_ge(S_("a_lo"), b * KT)
                            for i in range(ST):
                                last = eng.transpose(bank[k][:, 128 * i:128 * i + 128],
                                                     a_st[:, i, 128 * k:128 * k + 128], ident[:, :])
                            last.then_inc(S_("a_turned"), 1)
                        eng.wait_ge(S_("a_lo"), b * KT + KT)
                        eng.wait_ge(S_("o_biased"), b * (ST // 2))
                        for i in range(ST):
                            three(bank[2 + i // 2][:, D * (i % 2):D * (i % 2) + D],
                                  lambda a, k: (aT_hi, aT_lo)[a][:, k, 128 * i:128 * i + 128],
                                  lambda a, k: (wo_hi, wo_lo)[a][:, k, :]).then_inc(S_("o_proj"), 1)
                        eng.wait_ge(S_("yn_made"), b + 1)
                        for k in range(KT):
                            for i in range(ST):
                                last = eng.transpose(bank[4 + k][:, 128 * i:128 * i + 128],
                                                     y_st[:, i, 128 * k:128 * k + 128], ident[:, :])
                            last.then_inc(S_("y_turned"), 1)
                        eng.wait_ge(S_("y_lo"), b * KT + KT)
                        eng.wait_ge(S_("logits_made"), b)
                        for i in range(ST):
                            last = three(bank[6][:, E * i:E * i + E],
                                         lambda a, k: (yT_hi, yT_lo)[a][:, k, 128 * i:128 * i + 128],
                                         lambda a, k: (wr_hi, wr_lo)[a][:, k, :])
                        last.then_inc(S_("routed"), 1)

        with ExitStack() as ph:
            def sb4(name, shape, dt=fp32):
                return ph.enter_context(nc.sbuf_tensor(name, shape, dt))

            HR = 4
            r_sb = [sb4(f"r_sb{i}", [128, TBS]) for i in range(HR)]
            h_hi = [sb4(f"h_hi{i}", [128, TBS], f32r) for i in range(HR)]
            h_lo = [sb4(f"h_lo{i}", [128, TBS], f32r) for i in range(HR)]
            y_sb = sb4("y_sb", [128, ST, D])
            b2_b = [sb4(f"b2_b{i}", [128, D]) for i in range(2)]
            acc = attn
            xs = sb4("xs", [128, NT, E])
            zz = sb4("zz", [128, NT, E])
            z2 = sb4("z2", [128, NT, E])
            gate = sb4("gate", [128, NT, E])
            s4 = sb4("s4", [128, NT, 4])
            s2 = sb4("s2", [128, NT, 2])
            tau = sb4("tau", [128, NT, 1])
            tau_m = sb4("tau_m", [128, NT, 1])
            dm = sb4("dm", [128, NT, 1])
            f_lo = sb4("f_lo", [128, NT, 1])
            f_m = sb4("f_m", [128, NT, 1])
            top = sb4("top", [128, NT, 1])
            neg_one = sb4("neg_one", [128, NT, 1])
            w1_raw, w2_raw, w1, w2 = mb["w1_raw"], mb["w2_raw"], mb["w1"], mb["w2"]
            LAG = 2

            with nc.Block() as block:
                @block.sync
                def _(eng):
                    def load(e, par, first):
                        if not first:
                            eng.wait_ge(S_("w_split"), e * 4)
                        eng.dma_start(w1_raw[:, :, :], W1[e, :, :].rearrange("(k p) f -> p k f", p=128))\
                           .then_inc(S_("w1_in"), 16)
                        eng.dma_start(w2_raw[:, :, :], W2[e, :, :].rearrange("(f p) d -> p f d", p=128))\
                           .then_inc(S_("w2_in"), 16)
                        if not first:
                            eng.wait_ge(S_("y_read"), (e - 1) * NTB * 2)
                        eng.dma_start(b2_b[par][:, :], b2[e, :].rearrange("(a d) -> a d", a=1).broadcast_to([128, D]))\
                           .then_inc(S_(f"b2_in{par}"), 16)

                    load(0, 0, True)
                    load(1, 1, False)
                    with eng.Fori(1, E // 2) as pair:
                        e = pair * 2
                        load(e, 0, False)
                        load(e + 1, 1, False)
                    for t in range(NTB):
                        eng.wait_ge(S_("out_made"), t + 1)
                        eng.dma_start(out[t, :, :].rearrange("(i p) d -> p i d", p=128),
                                      acc[:, ST * t:ST * t + ST, :]).then_inc(S_("out_done"), 16)
                    eng.wait_ge(S_("out_done"), 16 * NTB)

                @block.gpsimd
                def _(eng):
                    def split(e, par, first):
                        if not first:
                            wait_apart(eng, S_("y_made"), (e - 1) * NTB * FT)
                        for j, (raw, pair, name) in enumerate(((w1_raw, w1[par], "w1_in"), (w2_raw, w2[par], "w2_in"))):
                            wait_apart(eng, S_(name), (e + 1) * 16)
                            eng.tensor_copy(pair[0][:, :, :], raw[:, :, :]).then_inc(S_("w_split"), 1)
                            eng.wait_ge(S_("w_split"), e * 4 + 2 * j + 1)
                            eng.tensor_tensor(pair[1][:, :, :], raw[:, :, :], pair[0][:, :, :].bitcast(fp32),
                                              ALU.subtract).then_inc(S_("w_split"), 1)

                    steps = [0]

                    def step(ins):
                        steps[0] += 1
                        ins.then_inc(S_("bisect"), 1)
                        eng.wait_ge(S_("bisect"), steps[0])

                    def wide_(t):
                        return t[:, :, :].broadcast_to([128, NT, E])

                    def total(base, dst, tau_):
                        ops = [
                            lambda: eng.tensor_tensor(zz[:, :, :], xs[:, :, :], wide_(tau_), ALU.subtract),
                            lambda: eng.tensor_scalar(zz[:, :, :], zz[:, :, :], 0.0, None, ALU.max),
                            lambda: eng.tensor_tensor(z2[:, :, :], zz[:, :, :], zz[:, :, :], ALU.mult),
                            lambda: eng.tensor_tensor(s4[:, :, :], z2[:, :, 0:4], z2[:, :, 4:8], ALU.add),
                            lambda: eng.tensor_tensor(s2[:, :, :], s4[:, :, 0:2], s4[:, :, 2:4], ALU.add),
                            lambda: eng.tensor_tensor(dst[:, :, :], s2[:, :, 0:1], s2[:, :, 1:2], ALU.add),
                            lambda: eng.tensor_scalar(dst[:, :, :], dst[:, :, :], -1.0, None, ALU.add)]
                        for i, op in enumerate(ops):
                            op().then_inc(S_("bisect"), 1)
                            wait_apart(eng, S_("bisect"), base + i + 1)
                        return len(ops)

                    split(0, 0, True)
                    split(1, 1, True)
                    eng.wait_ge(S_("top_made"), 1)
                    step(eng.memset(neg_one[:, :, :], -1.0))
                    step(eng.tensor_scalar(tau[:, :, :], top[:, :, :], -1.0, None, ALU.add))
                    step(eng.tensor_scalar(dm[:, :, :], top[:, :, :], -((1.0 / E) ** 0.5), None, ALU.add))
                    step(eng.tensor_tensor(dm[:, :, :], dm[:, :, :], tau[:, :, :], ALU.subtract))
                    steps[0] += total(steps[0], f_lo, tau)
                    base = steps[0]
                    per = 13
                    with eng.Fori(0, BISECT) as i:
                        at = [0]

                        def go(ins):
                            at[0] += 1
                            ins.then_inc(S_("bisect"), 1)
                            wait_apart(eng, S_("bisect"), i * per + (base + at[0]))

                        go(eng.tensor_scalar(dm[:, :, :], dm[:, :, :], 0.5, None, ALU.mult))
                        go(eng.tensor_tensor(tau_m[:, :, :], tau[:, :, :], dm[:, :, :], ALU.add))
                        at[0] += total(i * per + (base + at[0]), f_m, tau_m)
                        go(eng.tensor_tensor(f_m[:, :, :], f_m[:, :, :], f_lo[:, :, :], ALU.mult))
                        go(eng.tensor_scalar(f_m[:, :, :], f_m[:, :, :], 0.0, None, ALU.is_ge))
                        go(eng.tensor_tensor(f_m[:, :, :], f_m[:, :, :], dm[:, :, :], ALU.mult))
                        go(eng.tensor_tensor(tau[:, :, :], tau[:, :, :], f_m[:, :, :], ALU.add))
                        assert at[0] == per
                    steps[0] += per * BISECT
                    step(eng.tensor_tensor(f_m[:, :, :], s2[:, :, 0:1], s2[:, :, 1:2], ALU.add))
                    step(eng.tensor_tensor(f_m[:, :, :], f_m[:, :, :], neg_one[:, :, :], ALU.pow))
                    step(eng.tensor_tensor(z2[:, :, :], z2[:, :, :], wide_(f_m), ALU.mult))
                    step(eng.tensor_scalar(zz[:, :, :], z2[:, :, :], THRESH, None, ALU.is_gt))
                    eng.tensor_tensor(gate[:, :, :], z2[:, :, :], zz[:, :, :], ALU.mult).then_inc(S_("gates_made"), 1)
                    with eng.Fori(1, E // 2) as pair:
                        e = pair * 2
                        split(e, 0, False)
                        split(e + 1, 1, False)

                @block.scalar
                def _(eng):
                    def expert(e):
                        with eng.Fori(0, NTB) as t:
                            blk = e * (NTB * FT) + t * FT
                            for f in range(FT):
                                eng.wait_ge(S_("h_made"), blk + f + 1)
                                eng.wait_ge(S_("y_made"), blk + (f - HR + 1 if f >= HR else 0))
                                bias = b1_c[:, bass.ds(e * FT + f, 1)]
                                eng.activation(r_sb[f % HR][:, :], bank[f % HR], ACT.Relu, bias=bias)
                                eng.activation(h_hi[f % HR][:, :], bank[f % HR], ACT.Relu, bias=bias)\
                                   .then_inc(S_("relu_made"), 1)

                    with eng.Fori(0, E) as e:
                        expert(e)

                @block.vector
                def _(eng):
                    eng.tensor_scalar(xs[:, :, :], logits[:, :, :], 0.5, None, ALU.mult).then_inc(S_("xs_made"), 1)
                    eng.wait_ge(S_("xs_made"), 1)
                    eng.tensor_reduce(top[:, :, :], xs[:, :, :], AX.X, ALU.max).then_inc(S_("top_made"), 1)

                    def token_block(pair, par, t, first):
                        n = (pair * 2 + par) * NTB + t
                        for f in range(FT):
                            eng.wait_ge(S_("relu_made"), n * FT + f + 1)
                            eng.tensor_tensor(h_lo[f % HR][:, :], r_sb[f % HR][:, :], h_hi[f % HR][:, :].bitcast(fp32),
                                              ALU.subtract).then_inc(S_("h_lo"), 1)
                        eng.wait_ge(S_("y_made"), n * FT + FT)
                        eng.wait_ge(S_(f"b2_in{par}"), (pair + 1) * 16)
                        for j in range(ST // 2):
                            dst = acc[:, bass.ds(t * ST + 2 * j, 2), :] if first else y_sb[:, 2 * j:2 * j + 2, :]
                            eng.tensor_tensor(dst, bank[4 + j].rearrange("p (i d) -> p i d", i=2),
                                              b2_b[par][:, :].rearrange("p (a d) -> p a d", a=1)
                                              .broadcast_to([128, 2, D]), ALU.add).then_inc(S_("y_read"), 1)
                        eng.wait_ge(S_("y_read"), n * 2 + 2)

                    def weigh(e, t):
                        for i in range(ST):
                            rows = acc[:, bass.ds(t * ST + i, 1), :].rearrange("p a d -> p (a d)")
                            g = gate[:, bass.ds(t * ST + i, 1), bass.ds(e, 1)].rearrange("p a b -> p (a b)")
                            last = eng.scalar_tensor_tensor(rows, y_sb[:, i, :], g, rows, ALU.mult, ALU.add)
                        last.then_inc(S_("block_done"), 1)

                    with eng.Fori(0, NTB) as t:
                        token_block(0, 0, t, True)
                    eng.wait_ge(S_("gates_made"), 1)
                    for i in range(NT):
                        last = eng.tensor_scalar(acc[:, i, :], acc[:, i, :], gate[:, i, 0:1], None, ALU.mult)
                    last.then_inc(S_("first_weighed"), 1)
                    eng.wait_ge(S_("first_weighed"), 1)
                    with eng.Fori(0, NTB) as t:
                        eng.wait_ge(S_("block_done"), t)
                        token_block(0, 1, t, False)
                        weigh(1, t)
                    with eng.Fori(1, E // 2) as pair:
                        e = pair * 2
                        for par in range(2):
                            with eng.Fori(0, NTB) as t:
                                eng.wait_ge(S_("block_done"), (e + (par - 1)) * NTB + t)
                                token_block(pair, par, t, False)
                                weigh(e + par, t)
                    eng.wait_ge(S_("block_done"), (E - 1) * NTB)
                    for t in range(NTB):
                        rows = acc[:, ST * t:ST * t + ST, :].rearrange("p i d -> p (i d)")
                        eng.scalar_tensor_tensor(rows, rows, tg[:, 1:2],
                                                 x_all[:, ST * t:ST * t + ST, :].rearrange("p i d -> p (i d)"),
                                                 ALU.mult, ALU.add).then_inc(S_("out_made"), 1)

                @block.tensor
                def _(eng):
                    def token_block(e, t, par):
                        n = e * NTB + t

                        def hidden(f):
                            eng.wait_ge(S_("relu_made"), n * FT + (f - HR + 1 if f >= HR else 0))
                            i = 0
                            for k in range(KT):
                                for a, c in ((0, 0), (0, 1), (1, 0)):
                                    last = eng.matmul(bank[f % HR], w1[par][a][:, k, 128 * f:128 * f + 128],
                                                      (x2T_hi, x2T_lo)[c][:, k, bass.ds(t * TBS, TBS)],
                                                      start=(i == 0), stop=(i == 3 * KT - 1))
                                    i += 1
                            last.then_inc(S_("h_made"), 1)

                        def project(f):
                            eng.wait_ge(S_("h_lo"), n * FT + f + 1)
                            if f == 0:
                                eng.wait_ge(S_("y_read"), n * 2)
                            for i in range(ST):
                                for a, c in ((0, 0), (0, 1), (1, 0)):
                                    first = f == 0 and (a, c) == (0, 0)
                                    last = eng.matmul(
                                        bank[4 + i // 2][:, D * (i % 2):D * (i % 2) + D],
                                        (h_hi, h_lo)[a][f % HR][:, 128 * i:128 * i + 128], w2[par][c][:, f, :],
                                        start=(first and i % 2 == 0), stop=(f == FT - 1 and (a, c) == (1, 0)),
                                        skip_group_check=True)
                            last.then_inc(S_("y_made"), 1)

                        for f in range(FT + LAG):
                            if f < FT:
                                hidden(f)
                            if f >= LAG:
                                project(f - LAG)

                    with eng.Fori(0, E // 2) as pair:
                        e = pair * 2
                        for par in range(2):
                            wait_apart(eng, S_("w_split"), (e + (par + 1)) * 4)
                            with eng.Fori(0, NTB) as t:
                                token_block(e + par, t, par)


_INS = ['x', 'ctx_1024', 'g_xattn', 'g_ffn', 'L0_xattn_wq', 'L0_xattn_bq', 'L0_xattn_wk', 'L0_xattn_bk',
        'L0_xattn_wv', 'L0_xattn_bv', 'L0_xattn_wo', 'L0_xattn_bo', 'L0_ffn_Wr', 'L0_ffn_br', 'L0_ffn_W1',
        'L0_ffn_b1', 'L0_ffn_W2', 'L0_ffn_b2']


def kernel(**inputs):
    import numpy as _np
    import concourse.bacc as _bacc
    from concourse import mybir as _mybir
    from concourse.bass_utils import run_bass_kernel_spmd as _run

    nc = _bacc.Bacc("TRN2", target_bir_lowering=False, num_devices=1)
    arrays, args = {}, []
    for name in _INS:
        a = _np.ascontiguousarray(inputs[name])
        arrays[f"in_{name}"] = a
        args.append(nc.dram_tensor(f"in_{name}", a.shape, _mybir.dt.from_np(a.dtype), kind="ExternalInput").ap())
    x = inputs['x']
    out = nc.dram_tensor("out_0", tuple(x.shape), _mybir.dt.from_np(_np.dtype('float32')), kind="ExternalOutput").ap()
    flamingo_block(nc, *args, out)
    r = _run(nc, [arrays], core_ids=[0])
    return r.results[0]["out_0"]
```

```python
import concourse.bass as bass
from concourse import mybir
from contextlib import ExitStack

fp32 = mybir.dt.float32
f32r = mybir.dt.float32r
bf16 = mybir.dt.bfloat16
ALU = mybir.AluOpType
ACT = mybir.ActivationFunctionType
AX = mybir.AxisListType


def flamingo_block(nc, x, ctx, g_xattn, g_ffn, wq, bq, wk, bk, wv, bv, wo, bo,
                   Wr, br, W1, b1, W2, b2, out):
    B, S, D = x.shape
    T = ctx.shape[1]
    H = 16
    DK = D // H
    E, F = b1.shape
    KT = D // 128
    ST = S // 128
    NT = B * ST
    TP = 124
    TN = -(-T // TP)
    CT = 4
    CW = CT * TP
    NC = -(-T // CW)
    HG = 4
    NG = H // HG
    STRIP = 32
    KPARTS = (0, 0, 1, 1, 0, 2)
    QPARTS = (0, 1, 0, 1, 2, 0)
    NB = len(KPARTS)
    KS = NB * DK
    KM = KS + 3
    HALF = (T + 1) // 2
    FT = F // 128
    TBS = S
    NTB = B * S // TBS
    EPS = 1e-5
    BISECT = 25
    THRESH = 1e-9

    def tile_rows(n):
        return min(TP, T - n * TP)

    def chunk_cols(c):
        return min(CW, T - c * CW)

    kd = nc.dram_tensor("k_parts_dram", (B, 3, D, T), bf16).ap()
    qd = nc.dram_tensor("q_parts_dram", (B, 3, D, S), bf16).ap()
    vd = nc.dram_tensor("v_strips_dram", (B, 128, NG * TN * HG * STRIP), fp32).ap()

    with ExitStack() as es:
        def sb(name, shape, dt=fp32):
            return es.enter_context(nc.sbuf_tensor(name, shape, dt))

        def sem(name):
            return es.enter_context(nc.semaphore(name))

        wide = es.enter_context(nc.psum_tensor("wide", [128, 4 * 512], fp32))
        ring = es.enter_context(nc.psum_tensor("ring", [128, 3 * 512], fp32))
        pv_acc = es.enter_context(nc.psum_tensor("pv_acc", [128, 512], fp32))
        bank = [wide[:, 512 * i:512 * i + 512] for i in range(4)] + \
               [ring[:, 512 * i:512 * i + 512] for i in range(3)] + [pv_acc[:, :]]

        ident = sb("ident", [128, 128])
        ident_bf = sb("ident_bf", [128, 128], bf16)
        x_all = sb("x_all", [128, NT, D])
        attn = sb("attn", [128, NT, D])
        BROWS = E * FT + 2 * KT
        bias_rows = sb("bias_rows", [BROWS, 128])
        bias_c = sb("bias_c", [128, BROWS])
        bk_c = bias_c[:, E * FT:E * FT + KT]
        bq_c = bias_c[:, E * FT + KT:BROWS]
        b1_c = bias_c[:, 0:E * FT]
        bv_b = sb("bv_b", [128, D])
        bo_b = sb("bo_b", [128, D])
        br_b = sb("br_b", [128, E])
        wr_raw = sb("wr_raw", [128, KT, E])
        wr_hi = sb("wr_hi", [128, KT, E], f32r)
        wr_lo = sb("wr_lo", [128, KT, E], f32r)
        gates_raw = sb("gates_raw", [128, 2])
        tg = sb("tg", [128, 2])
        stats = sb("stats", [128, ST, 6])
        mv = sb("mv", [128, ST, 2])
        vpe = sb("vpe", [128, ST])
        rstd = sb("rstd", [128, ST])
        neg_half = sb("neg_half", [128, ST])
        wo_hi = sb("wo_hi", [128, KT, D], f32r)
        wo_lo = sb("wo_lo", [128, KT, D], f32r)

        o_sb = sb("o_sb", [128, S])
        rec = sb("rec", [128, ST, HG])
        mx2 = sb("mx2", [128, ST, HG, 2])
        mx = sb("mx", [128, ST, HG])
        mrest = sb("mrest", [128, 2, ST, HG])
        mparts = sb("mparts", [128, ST, HG, 3], bf16)
        mrow = sb("mrow", [HG * 3, S], bf16)

        EARLY = 2

        def stack(i):
            return (nc.sbuf_tensor(f"k_st{i}", [128, HG, T], bf16), nc.sbuf_tensor(f"q_st{i}", [128, HG, S], bf16))

        kq_early = es.enter_context(ExitStack())
        early = [[kq_early.enter_context(t) for t in stack(i)] for i in range(EARLY)]

        sems = {}

        def S_(name):
            if name not in sems:
                sems[name] = sem(name)
            return sems[name]

        ONE = 1
        FROM_ONE = ("rstd_made", "parts_made", "rest_made", "full_made", "c_lo", "v_made",
                    "qp_out", "x_tr", "rstd2_made", "a_turned", "o_proj", "y_kept",
                    "y_turned", "a_lo", "o_biased", "logits_made", "y_read", "relu_made",
                    "y_made", "block_done", "kp_out0", "kp_out1", "attn_made", "v_out_done0",
                    "v_out_done1", "v_out_done2", "v_out_done3")

        def load_kq(eng, k_stack, q_stack, b, hg):
            for j in range(NB):
                eng.dma_start(q_stack[DK * j:DK * j + DK, :, :],
                              qd[b, QPARTS[j], hg * HG * DK:(hg + 1) * HG * DK, :]
                              .rearrange("(h d) s -> d h s", d=DK)).then_inc(S_(f"q_in{hg}"), 16)
                eng.dma_start(k_stack[DK * j:DK * j + DK, :, :],
                              kd[b, KPARTS[j], hg * HG * DK:(hg + 1) * HG * DK, :]
                              .rearrange("(h d) t -> d h t", d=DK)).then_inc(S_(f"k_in{hg}"), 16)

        def wait_apart(eng, semaphore, value):
            if not isinstance(value, int):
                value = eng.snap(eng.to_reg(value))
            eng.wait_ge(S_("consts"), 2)
            eng.wait_ge(semaphore, value)

        with ExitStack() as ph:
            def sb0(name, shape, dt=fp32):
                return ph.enter_context(nc.sbuf_tensor(name, shape, dt))

            w_raw = [sb0(f"w_raw{i}", [128, KT, D]) for i in range(4)]
            w_hi = [sb0(f"w_hi{i}", [128, KT, D], f32r) for i in range(3)] + [wo_hi]
            w_lo = [sb0(f"w_lo{i}", [128, KT, D], f32r) for i in range(3)] + [wo_lo]
            ctx_in = sb0("ctx_in", [128, TN, D])
            cT_hi = sb0("cT_hi", [128, KT, T + 1], f32r)
            cT_lo = sb0("cT_lo", [128, KT, T + 1], f32r)
            xn = sb0("xn", [128, ST, D])
            xT_hi = sb0("xT_hi", [128, KT, S], f32r)
            xT_lo = sb0("xT_lo", [128, KT, S], f32r)
            full = [sb0(f"full{m}", [128, S]) for m in range(KT)]
            rest = [sb0(f"rest{m}", [128, S]) for m in range(KT)]
            kp = [sb0(f"kp{i}", [128, 3, KT, CW], bf16) for i in range(2)]
            qp = sb0("qp", [128, 3, KT, S], bf16)
            v_out = sb0("v_out", [128, NG, TN, HG, STRIP])

            JOBS = [("k", 0), ("k", 1), ("q", 0), ("k", 2), ("k", 3)]
            NJ = 2 * len(JOBS)

            def job_cols(kind, c):
                return chunk_cols(c) if kind == "k" else S

            def job_out(kind, c, part, m):
                return kp[c % 2][:, part, m, 0:chunk_cols(c)] if kind == "k" else qp[:, part, m, :]

            job_at = {job: 2 * i for i, job in enumerate(JOBS)}

            with nc.Block() as block:
                @block.sync
                def _(eng):
                    def load_ctx(b, c):
                        tiles = [n for n in range(CT * c, min(CT * c + CT, TN))]
                        rows = tile_rows(tiles[0])
                        src = ctx[b, c * CW:c * CW + chunk_cols(c), :]
                        eng.dma_start(ctx_in[0:rows, tiles[0]:tiles[-1] + 1, :],
                                      src.rearrange("(n p) d -> p n d", p=rows)).then_inc(S_(f"ctx_in{c}"), 16)

                    def store_k(b, c):
                        for part in range(3):
                            eng.dma_start(
                                kd[b, part, :, c * CW:c * CW + chunk_cols(c)].rearrange("(m p) t -> p m t", p=128),
                                kp[c % 2][:, part, :, 0:chunk_cols(c)]).then_inc(S_(f"kp_out{c % 2}"), 16)

                    def store_v(b, c):
                        tiles = slice(CT * c, min(CT * c + CT, TN))
                        eng.wait_ge(S_("v_made"), ONE + b * TN + tiles.stop)
                        eng.dma_start(vd[b, :, :].rearrange("p (g n e) -> p g n e", g=NG, n=TN)[:, :, tiles, :],
                                      v_out[:, :, tiles, :, :].rearrange("p g n h c -> p g n (h c)"))\
                           .then_inc(S_(f"v_out_done{c}"), 16)

                    def batch(b, load_next):
                        def nxt(c):
                            if load_next:
                                eng.wait_ge(S_("ctx_tr"), b * 2 * NC + 2 * c + 2)
                                load_ctx(b + 1, c)
                        nxt(0)
                        nxt(1)
                        for kind, c in JOBS:
                            eng.wait_ge(S_("parts_made"), ONE + b * NJ + job_at[kind, c] + 2)
                            if kind == "k":
                                store_k(b, c)
                                store_v(b, c)
                                if c in (0, 1):
                                    nxt(c + 2)
                            else:
                                for part in range(3):
                                    eng.dma_start(qd[b, part, :, :].rearrange("(m p) t -> p m t", p=128),
                                                  qp[:, part, :, :]).then_inc(S_("qp_out"), 16)
                    load_ctx(0, 0)
                    for name in FROM_ONE:
                        eng.sem_inc(S_(name), ONE)
                    for i, w in enumerate((wq, wk, wv, wo)):
                        eng.dma_start(w_raw[(0, 1, 2, 3)[i]][:, :, :], w.rearrange("(k p) n -> p k n", p=128))\
                           .then_inc(S_(f"w_in{i}"), 16)
                    eng.dma_start(bias_rows[E * FT:E * FT + KT, :], bk.rearrange("(m p) -> m p", p=128))\
                       .then_inc(S_("bias_in"), 16)
                    eng.dma_start(bias_rows[E * FT + KT:BROWS, :], bq.rearrange("(m p) -> m p", p=128))\
                       .then_inc(S_("bias_in"), 16)
                    eng.dma_start(bias_rows[0:E * FT, :], b1.rearrange("e (f p) -> (e f) p", p=128))\
                       .then_inc(S_("bias_in"), 16)
                    eng.dma_start(bv_b[:, :], bv.rearrange("(a n) -> a n", a=1).broadcast_to([128, D]))\
                       .then_inc(S_("bv_in"), 16)
                    for c in range(1, NC):
                        load_ctx(0, c)
                    for b in range(B):
                        eng.dma_start(x_all[:, ST * b:ST * b + ST, :], x[b, :, :].rearrange("(i p) d -> p i d", p=128))\
                           .then_inc(S_(f"x_in{b}"), 16)
                    eng.dma_start(bo_b[:, :], bo.rearrange("(a n) -> a n", a=1).broadcast_to([128, D]))\
                       .then_inc(S_("late_in"), 16)
                    eng.dma_start(br_b[:, :], br.rearrange("(a n) -> a n", a=1).broadcast_to([128, E]))\
                       .then_inc(S_("late_in"), 16)
                    eng.dma_start(wr_raw[:, :, :], Wr.rearrange("(k p) n -> p k n", p=128)).then_inc(S_("late_in"), 16)
                    for i, g in enumerate((g_xattn, g_ffn)):
                        eng.dma_start(gates_raw[:, i:i + 1], g.rearrange("(a n) -> a n", a=1).broadcast_to([128, 1]))\
                           .then_inc(S_("late_in"), 16)
                    with eng.Fori(0, B - 1) as b:
                        batch(b, True)
                    for i in range(2):
                        eng.wait_ge(S_(f"kp_out{i}"), ONE + 16 * 3 * 2 * (B - 1))
                    eng.wait_ge(S_("qp_out"), ONE + 16 * 3 * (B - 1))
                    for hg in range(EARLY):
                        load_kq(eng, *early[hg], 0, hg)
                    batch(B - 1, False)

                @block.gpsimd
                def _(eng):
                    eng.memset(ident[:, :], 0.0).then_inc(S_("consts"), 1)
                    eng.wait_ge(S_("consts"), 1)
                    eng.affine_select(out=ident[:, :], in_=ident[:, :], compare_op=ALU.not_equal, fill=1.0,
                                      base=0, pattern=[[-1, 128]], channel_multiplier=1).then_inc(S_("consts"), 1)
                    eng.memset(neg_half[:, :], -0.5).then_inc(S_("consts"), 1)
                    eng.wait_ge(S_("consts"), 3)
                    eng.tensor_copy(ident_bf[:, :], ident[:, :]).then_inc(S_("consts"), 1)
                    for t in (cT_hi, cT_lo):
                        eng.memset(t[:, :, T:T + 1].bitcast(fp32), 0.0).then_inc(S_("pad_zero"), 1)
                    eng.memset(v_out[:, :, :, :, :].rearrange("p g n h c -> p (g n h c)"), 0.0)\
                       .then_inc(S_("v_init"), 1)
                    eng.wait_ge(S_("v_init"), 1)
                    eng.memset(v_out[:, :, :, :, DK:DK + 1].rearrange("p g n h c -> p (g n h c)"), 1.0)\
                       .then_inc(S_("v_init"), 1)
                    with eng.Fori(0, B) as b:
                        wait_apart(eng, S_("stats_made"), b + 1)
                        wait_apart(eng, S_("rstd_made"), ONE + b)
                        eng.tensor_scalar(vpe[:, :], mv[:, :, 1], EPS, None, ALU.add).then_inc(S_("var_made"), 1)
                        eng.wait_ge(S_("var_made"), b + 1)
                        eng.tensor_tensor(rstd[:, :], vpe[:, :], neg_half[:, :], ALU.pow).then_inc(S_("rstd_made"), 1)
                        for kind, c in JOBS:
                            for m in range(KT):
                                i, w = job_at[kind, c] + m, job_cols(kind, c)
                                eng.wait_ge(S_("first_made"), b * NJ + i + 1)
                                eng.wait_ge(S_("parts_made"), ONE + b * NJ + max(i - 1, 0))
                                eng.tensor_tensor(rest[m][:, 0:w], full[m][:, 0:w], job_out(kind, c, 0, m),
                                                  ALU.subtract).then_inc(S_("rest_made"), 1)

                @block.scalar
                def _(eng):
                    for i in (1, 2, 0, 3):
                        eng.wait_ge(S_(f"w_in{i}"), 16)
                        eng.activation(w_hi[i][:, :, :], w_raw[i][:, :, :], ACT.Copy).then_inc(S_("w_hi"), 1)
                    eng.wait_ge(S_("bias_turned"), 1)
                    eng.activation(bias_c[:, :], bank[7][:, 0:BROWS], ACT.Copy).then_inc(S_("bias_made"), 1)
                    eng.wait_ge(S_("bias_made"), 1)

                    def hi(b, c, k):
                        eng.wait_ge(S_("ctx_tr"), b * 2 * NC + 2 * c + k + 1)
                        eng.activation(cT_hi[:, k, c * CW:c * CW + chunk_cols(c)], bank[k][:, 0:chunk_cols(c)],
                                       ACT.Copy).then_inc(S_("c_hi"), 1)

                    def job(b, kind, c, m):
                        i, w = job_at[kind, c] + m, job_cols(kind, c)
                        eng.wait_ge(S_("proj_made"), b * NJ + i + 1)
                        eng.wait_ge(S_("rest_made"), ONE + b * NJ + max(i - 1, 0))
                        bias = bk_c if kind == "k" else bq_c
                        src = bank[2 + m] if kind == "k" else bank[6 + m]
                        eng.activation(full[m][:, 0:w], src[:, 0:w], ACT.Identity,
                                       bias=bias[:, m:m + 1]).then_inc(S_("full_made"), 1)

                    with eng.Fori(0, B) as b:
                        for c in (0, 1):
                            for k in range(KT):
                                hi(b, c, k)
                        job(b, "k", 0, 0)
                        job(b, "k", 0, 1)
                        for k in range(KT):
                            eng.wait_ge(S_("x_tr"), ONE + b * KT + k + 1)
                            eng.activation(xT_hi[:, k, :], bank[6 + k], ACT.Copy).then_inc(S_("x_hi"), 1)
                        for k in range(KT):
                            hi(b, 2, k)
                        job(b, "k", 1, 0)
                        job(b, "k", 1, 1)
                        job(b, "q", 0, 0)
                        job(b, "q", 0, 1)
                        for k in range(KT):
                            hi(b, 3, k)
                        for c in (2, 3):
                            job(b, "k", c, 0)
                            job(b, "k", c, 1)

                @block.vector
                def _(eng):
                    for n, i in enumerate((1, 2, 0, 3)):
                        eng.wait_ge(S_("w_hi"), n + 1)
                        eng.tensor_tensor(w_lo[i][:, :, :], w_raw[i][:, :, :], w_hi[i][:, :, :].bitcast(fp32),
                                          ALU.subtract).then_inc(S_("w_lo"), 1)
                    eng.wait_ge(S_("bv_in"), 16)
                    eng.wait_ge(S_("v_init"), 2)
                    for b in range(B):
                        eng.wait_ge(S_(f"x_in{b}"), 16)

                    def lo(b, c, k):
                        cols = slice(c * CW, c * CW + chunk_cols(c))
                        eng.wait_ge(S_("c_hi"), b * 2 * NC + 2 * c + k + 1)
                        eng.tensor_tensor(cT_lo[:, k, cols], bank[k][:, 0:chunk_cols(c)],
                                          cT_hi[:, k, cols].bitcast(fp32), ALU.subtract).then_inc(S_("c_lo"), 1)

                    def first(b, kind, c, m):
                        i, w = job_at[kind, c] + m, job_cols(kind, c)
                        eng.wait_ge(S_("full_made"), ONE + b * NJ + i + 1)
                        if m == 0:
                            if kind == "k":
                                eng.wait_ge(S_(f"kp_out{c % 2}"), ONE + (b * 2 + c // 2) * 48)
                            else:
                                eng.wait_ge(S_("qp_out"), ONE + b * 48)
                        eng.tensor_copy(job_out(kind, c, 0, m), full[m][:, 0:w]).then_inc(S_("first_made"), 1)

                    def others(b, kind, c, m):
                        i, w = job_at[kind, c] + m, job_cols(kind, c)
                        eng.wait_ge(S_("rest_made"), ONE + b * NJ + i + 1)
                        eng.tensor_copy(job_out(kind, c, 1, m), rest[m][:, 0:w]).then_inc(S_("second_made"), 1)
                        eng.wait_ge(S_("second_made"), b * NJ + i + 1)
                        eng.tensor_tensor(job_out(kind, c, 2, m), rest[m][:, 0:w], job_out(kind, c, 1, m),
                                          ALU.subtract).then_inc(S_("parts_made"), 1)

                    def v_rows(b, n):
                        rows = tile_rows(n)
                        if n % CT == 0:
                            eng.wait_ge(S_(f"v_out_done{n // CT}"), ONE + b * 16)
                        eng.wait_ge(S_("v_proj"), b * TN + n + 1)
                        eng.tensor_tensor(v_out[0:rows, :, n, :, 0:DK],
                                          bank[4 + n % 2][0:rows, 0:D].rearrange("p (g h c) -> p g h c", g=NG, h=HG),
                                          bv_b[0:rows, :].rearrange("p (g h c) -> p g h c", g=NG, h=HG),
                                          ALU.add).then_inc(S_("v_made"), 1)

                    def kv(b, c):
                        first(b, "k", c, 0)
                        first(b, "k", c, 1)
                        tiles = list(range(CT * c, min(CT * c + CT, TN)))
                        for m in range(KT):
                            for n in tiles[2 * m:2 * m + 2]:
                                v_rows(b, n)
                            others(b, "k", c, m)

                    with eng.Fori(0, B) as b:
                        lo(b, 0, 0)
                        lo(b, 0, 1)
                        for i in range(ST):
                            eng.bn_stats(stats[:, i, :], x_all[:, bass.ds(b * ST + i, 1), :]
                                         .rearrange("p a d -> p (a d)")).then_inc(S_("bn_made"), 1)
                        lo(b, 1, 0)
                        lo(b, 1, 1)
                        wait_apart(eng, S_("bn_made"), b * ST + ST)
                        for i in range(ST):
                            last = eng.bn_aggr(mv[:, i, :], stats[:, i, :])
                        last.then_inc(S_("stats_made"), 1)
                        eng.wait_ge(S_("rstd_made"), ONE + b + 1)
                        eng.wait_ge(S_("x_tr"), ONE + b * KT)
                        for i in range(ST):
                            eng.tensor_scalar(xn[:, i, :],
                                              x_all[:, bass.ds(b * ST + i, 1), :].rearrange("p a d -> p (a d)"),
                                              mv[:, i, 0:1], rstd[:, i:i + 1], ALU.subtract, ALU.mult)\
                               .then_inc(S_("xn_made"), 1)
                        kv(b, 0)
                        for k in range(KT):
                            eng.wait_ge(S_("x_hi"), b * KT + k + 1)
                            eng.tensor_tensor(xT_lo[:, k, :], bank[6 + k], xT_hi[:, k, :].bitcast(fp32),
                                              ALU.subtract).then_inc(S_("x_lo"), 1)
                        lo(b, 2, 0)
                        lo(b, 2, 1)
                        kv(b, 1)
                        first(b, "q", 0, 0)
                        first(b, "q", 0, 1)
                        lo(b, 3, 0)
                        lo(b, 3, 1)
                        others(b, "q", 0, 0)
                        others(b, "q", 0, 1)
                        kv(b, 2)
                        kv(b, 3)
                        eng.wait_ge(S_("xn_made"), b * ST + ST)

                @block.tensor
                def _(eng):
                    eng.wait_ge(S_("consts"), 2)
                    eng.wait_ge(S_("bias_in"), 48)
                    eng.transpose(bank[7][:, 0:BROWS], bias_rows[:, :], ident[0:BROWS, 0:BROWS])\
                       .then_inc(S_("bias_turned"), 1)
                    eng.wait_ge(S_("bias_made"), 1)

                    def turn_ctx(b, c):
                        tiles = list(range(CT * c, min(CT * c + CT, TN)))
                        eng.wait_ge(S_(f"ctx_in{c}"), b * 16 + 16)
                        for k in range(KT):
                            eng.wait_ge(S_("c_lo"), ONE + b * 2 * NC + (2 * c - 2 + k + 1 if c else 0))
                            for n in tiles:
                                rows = tile_rows(n)
                                o = (n - tiles[0]) * TP
                                last = eng.transpose(bank[k][:, o:o + rows], ctx_in[0:rows, n, 128 * k:128 * k + 128],
                                                     ident[0:rows, 0:rows])
                            last.then_inc(S_("ctx_tr"), 1)

                    def three(out_ap, lhs, rhs):
                        n = 0
                        for k in range(KT):
                            for a, c in ((0, 0), (0, 1), (1, 0)):
                                last = eng.matmul(out_ap, lhs(a, k), rhs(c, k), start=(n == 0), stop=(n == 3 * KT - 1))
                                n += 1
                        return last

                    def project_k(b, c):
                        cols = slice(c * CW, c * CW + chunk_cols(c) + chunk_cols(c) % 2)
                        w = chunk_cols(c) + chunk_cols(c) % 2
                        eng.wait_ge(S_("c_lo"), ONE + b * 2 * NC + 2 * c + 2)
                        for m in range(KT):
                            eng.wait_ge(S_("full_made"), ONE + b * NJ + (job_at["k", c - 1] + m + 1 if c else 0))
                            three(bank[2 + m][:, 0:w],
                                  lambda a, k: (w_hi, w_lo)[a][1][:, k, 128 * m:128 * m + 128],
                                  lambda a, k: (cT_hi, cT_lo)[a][:, k, cols]).then_inc(S_("proj_made"), 1)

                    def project_v(b, c):
                        for n in range(CT * c, min(CT * c + CT, TN)):
                            rows = tile_rows(n)
                            eng.wait_ge(S_("v_made"), ONE + b * TN + (n - 1 if n > 1 else 0))
                            three(bank[4 + n % 2][0:rows, 0:D],
                                  lambda a, k: (cT_hi, cT_lo)[a][:, k, n * TP:n * TP + rows],
                                  lambda a, k: (w_hi, w_lo)[a][2][:, k, :]).then_inc(S_("v_proj"), 1)

                    eng.wait_ge(S_("pad_zero"), 2)
                    with eng.Fori(0, B) as b:
                        turn_ctx(b, 0)
                        turn_ctx(b, 1)
                        eng.wait_ge(S_("w_lo"), 4)
                        project_k(b, 0)
                        project_v(b, 0)
                        eng.wait_ge(S_("xn_made"), b * ST + ST)
                        for k in range(KT):
                            eng.wait_ge(S_("full_made"), ONE + b * NJ)
                            for i in range(ST):
                                last = eng.transpose(bank[6 + k][:, 128 * i:128 * i + 128],
                                                     xn[:, i, 128 * k:128 * k + 128], ident[:, :])
                            last.then_inc(S_("x_tr"), 1)
                        turn_ctx(b, 2)
                        project_k(b, 1)
                        project_v(b, 1)
                        eng.wait_ge(S_("x_lo"), b * KT + KT)
                        for m in range(KT):
                            three(bank[6 + m],
                                  lambda a, k: (w_hi, w_lo)[a][0][:, k, 128 * m:128 * m + 128],
                                  lambda a, k: (xT_hi, xT_lo)[a][:, k, :]).then_inc(S_("proj_made"), 1)
                        turn_ctx(b, 3)
                        project_k(b, 2)
                        project_v(b, 2)
                        project_k(b, 3)
                        project_v(b, 3)

        TILES = NG * TN
        EXPS = TILES * HG
        PR = 4
        LAG_V = 2
        UNITS = HG * ST * 2
        LEAD = 14
        TURN_AT = 3
        O_AT = 8
        ITEMS = UNITS + 2

        with ExitStack() as ph:
            def sb1(name, shape, dt=fp32):
                return ph.enter_context(nc.sbuf_tensor(name, shape, dt))

            stacks = early + [[ph.enter_context(t) for t in stack(i)] for i in range(EARLY, NG)]
            k_st, q_st = [st[0] for st in stacks], [st[1] for st in stacks]
            v_st = [sb1(f"v_st{i}", [128, TN, HG * STRIP]) for i in range(2)]
            prob = [sb1(f"prob{i}", [128, HG, S]) for i in range(PR)]
            slot = [wide[:, 0:1024], wide[:, 1024:2048]]

            def plus(b, hg, k):
                b, hg = b + (hg + k) // NG, (hg + k) % NG
                return None if isinstance(b, int) and b >= B else (b, hg)

            def is_group(b, hg, of_b, of_hg):
                return isinstance(b, int) and (b, hg) == (of_b, of_hg)

            def units(g, first, end):
                return [("unit", g, u) for u in range(first, end)] if g else []

            def head_start(g, g2):
                return units(g2, 0, TURN_AT) + [("turn", g)] + units(g2, TURN_AT, LEAD)

            def slot_items(b, hg):
                g, g2 = plus(b, hg, 1), plus(b, hg, 2)
                items = units(g, LEAD, UNITS) + (head_start(g, g2) if g else [])
                if not is_group(b, hg, 0, 0):
                    items.insert(O_AT, ("output", plus(b, hg, -1)))
                steps = [[] for _ in range(TN)]
                for i, item in enumerate(items):
                    steps[i * TN // ITEMS].append(item)
                if not g:
                    steps = [[], [], []] + [items] + [[] for _ in range(TN - 4)]
                return steps

            PROLOGUE = units((0, 0), 0, UNITS) + head_start((0, 0), (0, 1))

            def slot_base(b, hg):
                if is_group(b, hg, 0, 0):
                    return len(PROLOGUE)
                if is_group(b, hg, B - 1, NG - 1):
                    return slot_base(B - 1, NG - 2) + sum(map(len, slot_items(B - 1, NG - 2)))
                return (b * NG + hg) * ITEMS + (len(PROLOGUE) - 1)

            def slot_of(b, hg, i):
                return (len(PROLOGUE) - (0 if is_group(b, hg, 0, 0) else 1) + i) % 2

            def numbered(b, hg):
                i = 0
                for n, items in enumerate(slot_items(b, hg)):
                    for item in items:
                        yield n, item, slot_base(b, hg) + i, slot_of(b, hg, i)
                        i += 1

            def turn_count(b, hg):
                for _, item, pos, _ in numbered(b, hg):
                    if item[0] == "turn":
                        return pos + 1

            PROLOGUE_TURN = PROLOGUE.index(("turn", (0, 0))) + 1
            LAST_OUTPUT = slot_base(B - 1, NG - 1) + 1

            def over_groups(eng, group):
                group(0, 0)
                with eng.Fori(0, B - 1) as b:
                    for hg in range(1, NG):
                        group(b, hg)
                    group(b + 1, 0)
                for hg in range(1, NG):
                    group(B - 1, hg)

            def not_below_zero(value):
                return max(value, 0) if isinstance(value, int) else value

            with nc.Block() as block:
                @block.sync
                def _(eng):
                    def load_v(b, hg):
                        cols = TN * HG * STRIP
                        eng.dma_start(v_st[hg % 2][:, :, :].rearrange("p n c -> p (n c)"),
                                      vd[b, :, hg * cols:(hg + 1) * cols]).then_inc(S_(f"v_in{hg % 2}"), 16)

                    def store_max(b, hg, count):
                        eng.wait_ge(S_("slot_read"), count)
                        for h in range(HG):
                            eng.dma_start(q_st[hg][KS:KM, h, :], mrow[3 * h:3 * h + 3, :])\
                               .then_inc(S_(f"m_in{hg}"), 16)

                    def group(b, hg):
                        if plus(b, hg, 3):
                            eng.wait_ge(S_("scores_made"), b * EXPS + hg * TN * HG)
                            b3, hg3 = plus(b, hg, 3)
                            load_kq(eng, k_st[hg3], q_st[hg3], b3, hg3)
                        if plus(b, hg, 1):
                            eng.wait_ge(S_("pv_tile"), b * TILES + hg * TN)
                            load_v(*plus(b, hg, 1))
                            store_max(*plus(b, hg, 1), turn_count(b, hg))

                    for i in range(2):
                        eng.wait_ge(S_(f"kp_out{i}"), ONE + 16 * 3 * 2 * B)
                    eng.wait_ge(S_("qp_out"), ONE + 16 * 3 * B)
                    for c in range(NC):
                        eng.wait_ge(S_(f"v_out_done{c}"), ONE + 16 * B)
                    eng.sem_inc(S_("parts_stored"), 1)
                    load_v(0, 0)
                    for hg in range(EARLY, 3):
                        load_kq(eng, k_st[hg], q_st[hg], 0, hg)
                    store_max(0, 0, PROLOGUE_TURN)
                    over_groups(eng, group)

                @block.gpsimd
                def _(eng):
                    for i in range(NG):
                        if i == EARLY:
                            eng.wait_ge(S_("parts_stored"), 1)
                        eng.memset(k_st[i][KS:KM, :, :], -1.0).then_inc(S_("minus_ones"), 1)

                @block.scalar
                def _(eng):
                    def copy_output(q):
                        eng.wait_ge(S_("pv_tile"), q * TN + TN)
                        eng.activation(o_sb[:, :], pv_acc[:, :], ACT.Copy).then_inc(S_("o_copied"), 1)

                    def group(b, hg):
                        for n in range(TN):
                            tt, rows = hg * TN + n, tile_rows(n)
                            eng.wait_ge(S_("pv_tile"), not_below_zero(b * TILES + (tt - PR + 1)))
                            for h in range(HG):
                                i = tt * HG + h
                                eng.wait_ge(S_("scores_made"), b * EXPS + i + 1)
                                eng.activation(prob[tt % PR][0:rows, h, :], bank[4 + i % 3][0:rows, :], ACT.Exp,
                                               scale=float(DK) ** -0.5).then_inc(S_("exp_made"), 1)
                            if n == LAG_V - 2 and not is_group(b, hg, 0, 0):
                                copy_output(b * NG + (hg - 1))

                    over_groups(eng, group)
                    copy_output(B * NG - 1)

                @block.vector
                def _(eng):
                    def maximum(b, hg, u, pos, sl):
                        h, st, half = u // (2 * ST), u // 2 % ST, u % 2
                        w = T - HALF if half else HALF
                        eng.wait_ge(S_("slot_made"), pos + 1)
                        eng.tensor_reduce(mx2[:, st, h, half:half + 1], slot[sl][:, 0:w], AX.X, ALU.max)\
                           .then_inc(S_("slot_read"), 1)
                        if u == UNITS - 1:
                            eng.wait_ge(S_("slot_read"), pos + 1)
                            split_maxima((b * NG + hg) * 6)

                    def split_maxima(count):
                        eng.tensor_reduce(mx[:, :, :], mx2[:, :, :, :], AX.X, ALU.max).then_inc(S_("m_step"), 1)
                        eng.wait_ge(S_("m_step"), count + 1)
                        eng.tensor_copy(mparts[:, :, :, 0], mx[:, :, :]).then_inc(S_("m_step"), 1)
                        eng.wait_ge(S_("m_step"), count + 2)
                        eng.tensor_tensor(mrest[:, 0, :, :], mx[:, :, :], mparts[:, :, :, 0], ALU.subtract)\
                           .then_inc(S_("m_step"), 1)
                        eng.wait_ge(S_("m_step"), count + 3)
                        eng.tensor_copy(mparts[:, :, :, 1], mrest[:, 0, :, :]).then_inc(S_("m_step"), 1)
                        eng.wait_ge(S_("m_step"), count + 4)
                        eng.tensor_tensor(mrest[:, 1, :, :], mrest[:, 0, :, :], mparts[:, :, :, 1], ALU.subtract)\
                           .then_inc(S_("m_step"), 1)
                        eng.wait_ge(S_("m_step"), count + 5)
                        eng.tensor_copy(mparts[:, :, :, 2], mrest[:, 1, :, :]).then_inc(S_("m_step"), 1)

                    def rows_out(b, hg, pos, sl):
                        eng.wait_ge(S_("slot_made"), pos + 1)
                        if not is_group(b, hg, 0, 0):
                            pb, pg = plus(b, hg, -1)
                            eng.wait_ge(S_(f"m_in{pg}"), (pb + 1) * (16 * HG))
                        eng.tensor_copy(mrow[:, :], slot[sl].bitcast(bf16)[0:3 * HG, 0:S])\
                           .then_inc(S_("slot_read"), 1)

                    def normalise(b, hg, pos, sl):
                        q = b * NG + hg
                        eng.wait_ge(S_("slot_made"), pos + 1)
                        turned = slot[sl][:, 0:S].rearrange("p (i h c) -> p i h c", i=ST, h=HG)
                        eng.wait_ge(S_("attn_made"), ONE + q)
                        eng.reciprocal(rec[:, :, :], turned[:, :, :, DK]).then_inc(S_("rec_made"), 1)
                        eng.wait_ge(S_("rec_made"), q + 1)
                        eng.tensor_tensor(
                            attn[:, bass.ds(b * ST, ST), hg * HG * DK:(hg + 1) * HG * DK]
                            .rearrange("p i (h c) -> p i h c", h=HG),
                            turned[:, :, :, 0:DK],
                            rec[:, :, :].rearrange("p i (h a) -> p i h a", a=1).broadcast_to([128, ST, HG, DK]),
                            ALU.mult).then_inc(S_("attn_made"), 1)
                        eng.wait_ge(S_("attn_made"), ONE + q + 1)
                        eng.sem_inc(S_("slot_read"), 1)

                    READ = dict(unit=maximum, turn=rows_out, output=normalise)

                    def group(b, hg):
                        for _, (kind, g, *more), pos, sl in numbered(b, hg):
                            READ[kind](*g, *more, pos, sl)

                    for pos, (kind, g, *more) in enumerate(PROLOGUE):
                        READ[kind](*g, *more, pos, pos % 2)
                    over_groups(eng, group)
                    normalise(B - 1, NG - 1, LAST_OUTPUT, slot_of(B - 1, NG - 1, 1))

                @block.tensor
                def _(eng):
                    def max_unit(b, hg, u, pos, sl):
                        h, st, half = u // (2 * ST), u // 2 % ST, u % 2
                        if u == 0:
                            eng.wait_ge(S_(f"q_in{hg}"), (b + 1) * (16 * NB))
                            eng.wait_ge(S_(f"k_in{hg}"), (b + 1) * (16 * NB))
                        eng.wait_ge(S_("slot_read"), not_below_zero(pos - 1))
                        lo_, hi_ = (HALF, T) if half else (0, HALF)
                        for o in range(lo_, hi_, 512):
                            w = min(512, hi_ - o)
                            last = eng.matmul(slot[sl][:, o - lo_:o - lo_ + w],
                                              q_st[hg][0:KS, h, 128 * st:128 * st + 128],
                                              k_st[hg][0:KS, h, o:o + w], start=True, stop=True)
                        last.then_inc(S_("slot_made"), 1)

                    def turn_max(b, hg, pos, sl):
                        eng.wait_ge(S_("m_step"), (b * NG + hg) * 6 + 6)
                        eng.wait_ge(S_("slot_read"), pos - 1)
                        for i in range(ST):
                            last = eng.transpose(slot[sl].bitcast(bf16)[0:3 * HG, 128 * i:128 * i + 128],
                                                 mparts[:, i, :, :].rearrange("p h c -> p (h c)"), ident_bf[:, :])
                        last.then_inc(S_("slot_made"), 1)

                    def turn_output(b, hg, pos, sl):
                        eng.wait_ge(S_("o_copied"), b * NG + hg + 1)
                        eng.wait_ge(S_("slot_read"), pos - 1)
                        for i in range(ST):
                            last = eng.transpose(slot[sl][:, 128 * i:128 * i + 128], o_sb[:, 128 * i:128 * i + 128],
                                                 ident[:, :])
                        last.then_inc(S_("slot_made"), 1)

                    MAKE = dict(unit=max_unit, turn=turn_max, output=turn_output)

                    def scores(b, hg, n, h):
                        tt, rows = hg * TN + n, tile_rows(n)
                        i = tt * HG + h
                        eng.wait_ge(S_("exp_made"), b * EXPS + (i - 2 if i > 2 else 0))
                        eng.matmul(bank[4 + i % 3][0:rows, :], k_st[hg][0:KM, h, n * TP:n * TP + rows],
                                   q_st[hg][0:KM, h, :], start=True, stop=True).then_inc(S_("scores_made"), 1)

                    def weigh_v(b, hg, n):
                        tt, rows = hg * TN + n, tile_rows(n)
                        if n == 0:
                            eng.wait_ge(S_("o_copied"), b * NG + hg)
                            eng.wait_ge(S_(f"v_in{hg % 2}"), b * 32 + (hg // 2 + 1) * 16)
                        eng.wait_ge(S_("exp_made"), b * EXPS + (tt * HG + HG))
                        for h in range(HG):
                            last = eng.matmul(pv_acc[STRIP * h:STRIP * h + STRIP, :],
                                              v_st[hg % 2][0:rows, n, STRIP * h:STRIP * h + STRIP],
                                              prob[tt % PR][0:rows, h, :], start=(n == 0), stop=(n == TN - 1))
                        last.then_inc(S_("pv_tile"), 1)

                    def group(b, hg):
                        eng.wait_ge(S_(f"m_in{hg}"), (b + 1) * (16 * HG))
                        items = list(numbered(b, hg))
                        for n in range(TN):
                            todo = [it for it in items if it[0] == n]

                            def one():
                                if todo:
                                    _, (kind, g, *more), pos, sl = todo.pop(0)
                                    MAKE[kind](*g, *more, pos, sl)

                            if n >= LAG_V:
                                weigh_v(b, hg, n - LAG_V)
                            elif not is_group(b, hg, 0, 0):
                                weigh_v(*plus(b, hg, -1), TN + n - LAG_V)
                            one()
                            scores(b, hg, n, 0)
                            scores(b, hg, n, 1)
                            one()
                            scores(b, hg, n, 2)
                            scores(b, hg, n, 3)
                            one()
                            assert not todo

                    for pos, (kind, g, *more) in enumerate(PROLOGUE):
                        MAKE[kind](*g, *more, pos, pos % 2)
                    eng.wait_ge(S_("minus_ones"), NG)
                    over_groups(eng, group)
                    for n in range(TN - LAG_V, TN):
                        weigh_v(B - 1, NG - 1, n)
                    turn_output(B - 1, NG - 1, LAST_OUTPUT, slot_of(B - 1, NG - 1, 1))

        kq_early.close()

        def mix_buffers(ph):
            def sb2(name, shape, dt=fp32):
                return ph.enter_context(nc.sbuf_tensor(name, shape, dt))
            return dict(
                xT_hi=sb2("x2T_hi", [128, KT, NT * 128], f32r), xT_lo=sb2("x2T_lo", [128, KT, NT * 128], f32r),
                logits=sb2("logits", [128, NT, E]),
                w1_raw=sb2("w1_raw", [128, KT, F]), w2_raw=sb2("w2_raw", [128, FT, D]),
                w1=[[sb2(f"w1_{p}{i}", [128, KT, F], f32r) for p in ("hi", "lo")] for i in range(2)],
                w2=[[sb2(f"w2_{p}{i}", [128, FT, D], f32r) for p in ("hi", "lo")] for i in range(2)])

        ph2 = es.enter_context(ExitStack())
        mb = mix_buffers(ph2)
        x2T_hi, x2T_lo, logits = mb["xT_hi"], mb["xT_lo"], mb["logits"]

        w1_raw, w2_raw, w1, w2 = mb["w1_raw"], mb["w2_raw"], mb["w1"], mb["w2"]
        b2_b = [es.enter_context(nc.sbuf_tensor(f"b2_b{i}", [128, D], fp32)) for i in range(2)]

        def load_expert(eng, e, par, first):
            if not first:
                eng.wait_ge(S_("w_split"), e * 4)
            eng.dma_start(w1_raw[:, :, :], W1[e, :, :].rearrange("(k p) f -> p k f", p=128))\
               .then_inc(S_("w1_in"), 16)
            eng.dma_start(w2_raw[:, :, :], W2[e, :, :].rearrange("(f p) d -> p f d", p=128))\
               .then_inc(S_("w2_in"), 16)
            if not first:
                eng.wait_ge(S_("y_read"), ONE + (e - 1) * NTB * 2)
            eng.dma_start(b2_b[par][:, :], b2[e, :].rearrange("(a d) -> a d", a=1).broadcast_to([128, D]))\
               .then_inc(S_(f"b2_in{par}"), 16)

        def split_expert(eng, e, par, first):
            if not first:
                wait_apart(eng, S_("y_made"), ONE + (e - 1) * NTB * FT)
            for j, (raw, pair, name) in enumerate(((w1_raw, w1[par], "w1_in"), (w2_raw, w2[par], "w2_in"))):
                wait_apart(eng, S_(name), (e + 1) * 16)
                eng.tensor_copy(pair[0][:, :, :], raw[:, :, :]).then_inc(S_("w_split"), 1)
                eng.wait_ge(S_("w_split"), e * 4 + 2 * j + 1)
                eng.tensor_tensor(pair[1][:, :, :], raw[:, :, :], pair[0][:, :, :].bitcast(fp32),
                                  ALU.subtract).then_inc(S_("w_split"), 1)

        with ExitStack() as ph:
            def sb3(name, shape, dt=fp32):
                return ph.enter_context(nc.sbuf_tensor(name, shape, dt))

            a_st = sb3("a_st", [128, ST, D])
            aT_hi = sb3("aT_hi", [128, KT, S], f32r)
            aT_lo = sb3("aT_lo", [128, KT, S], f32r)
            o_bias = sb3("o_bias", [128, ST, D])
            y_st = sb3("y_st", [128, ST, D])
            yT_hi = sb3("yT_hi", [128, KT, S], f32r)
            yT_lo = sb3("yT_lo", [128, KT, S], f32r)

            with nc.Block() as block:
                @block.gpsimd
                def _(eng):
                    def inverse_deviation(b):
                        wait_apart(eng, S_("stats2_made"), b + 1)
                        wait_apart(eng, S_("rstd2_made"), ONE + b)
                        eng.tensor_scalar(vpe[:, :], mv[:, :, 1], EPS, None, ALU.add).then_inc(S_("var2_made"), 1)
                        eng.wait_ge(S_("var2_made"), b + 1)
                        eng.tensor_tensor(rstd[:, :], vpe[:, :], neg_half[:, :], ALU.pow).then_inc(S_("rstd2_made"), 1)

                    inverse_deviation(0)
                    split_expert(eng, 0, 0, True)
                    with eng.Fori(1, B) as b:
                        inverse_deviation(b)
                    split_expert(eng, 1, 1, True)

                @block.sync
                def _(eng):
                    load_expert(eng, 0, 0, True)
                    load_expert(eng, 1, 1, False)

                @block.scalar
                def _(eng):
                    eng.wait_ge(S_("late_in"), 80)
                    eng.activation(tg[:, :], gates_raw[:, :], ACT.Tanh).then_inc(S_("tanh_made"), 1)
                    eng.activation(wr_hi[:, :, :], wr_raw[:, :, :], ACT.Copy).then_inc(S_("wr_hi"), 1)
                    with eng.Fori(0, B) as b:
                        eng.wait_ge(S_("a_turned"), ONE + b * KT)
                        eng.activation(a_st[:, :, :], attn[:, bass.ds(b * ST, ST), :], ACT.Copy)\
                           .then_inc(S_("a_copied"), 1)
                        for k in range(KT):
                            eng.wait_ge(S_("a_turned"), ONE + b * KT + k + 1)
                            eng.wait_ge(S_("o_proj"), ONE + b * ST)
                            eng.activation(aT_hi[:, k, :], bank[k], ACT.Copy).then_inc(S_("a_hi"), 1)
                        for k in range(KT):
                            eng.wait_ge(S_("y_turned"), ONE + b * KT + k + 1)
                            eng.wait_ge(S_("y_kept"), ONE + b * 2)
                            eng.activation(yT_hi[:, k, :], bank[4 + k], ACT.Copy).then_inc(S_("y_hi"), 1)

                @block.vector
                def _(eng):
                    eng.wait_ge(S_("wr_hi"), 1)
                    eng.tensor_tensor(wr_lo[:, :, :], wr_raw[:, :, :], wr_hi[:, :, :].bitcast(fp32), ALU.subtract)\
                       .then_inc(S_("wr_lo"), 1)
                    eng.wait_ge(S_("tanh_made"), 1)
                    with eng.Fori(0, B) as b:
                        for k in range(KT):
                            eng.wait_ge(S_("a_hi"), b * KT + k + 1)
                            eng.tensor_tensor(aT_lo[:, k, :], bank[k], aT_hi[:, k, :].bitcast(fp32), ALU.subtract)\
                               .then_inc(S_("a_lo"), 1)
                        for j in range(ST // 2):
                            eng.wait_ge(S_("o_proj"), ONE + b * ST + 2 * j + 2)
                            eng.tensor_tensor(o_bias[:, 2 * j:2 * j + 2, :],
                                              bank[2 + j].rearrange("p (i d) -> p i d", i=2),
                                              bo_b[:, :].rearrange("p (a d) -> p a d", a=1).broadcast_to([128, 2, D]),
                                              ALU.add).then_inc(S_("o_biased"), 1)
                        eng.wait_ge(S_("o_biased"), ONE + b * (ST // 2) + ST // 2)
                        rows = x_all[:, bass.ds(b * ST, ST), :].rearrange("p i d -> p (i d)")
                        eng.scalar_tensor_tensor(rows, o_bias[:, :, :].rearrange("p i d -> p (i d)"), tg[:, 0:1],
                                                 rows, ALU.mult, ALU.add).then_inc(S_("x2_made"), 1)
                        wait_apart(eng, S_("x2_made"), b + 1)
                        for i in range(ST):
                            last = eng.bn_stats(stats[:, i, :], x_all[:, bass.ds(b * ST + i, 1), :]
                                                .rearrange("p a d -> p (a d)"))
                        last.then_inc(S_("bn2_made"), 1)
                        wait_apart(eng, S_("bn2_made"), b + 1)
                        for i in range(ST):
                            last = eng.bn_aggr(mv[:, i, :], stats[:, i, :])
                        last.then_inc(S_("stats2_made"), 1)
                        eng.wait_ge(S_("rstd2_made"), ONE + b + 1)
                        eng.wait_ge(S_("y_turned"), ONE + b * KT)
                        for i in range(ST):
                            last = eng.tensor_scalar(y_st[:, i, :],
                                                     x_all[:, bass.ds(b * ST + i, 1), :].rearrange("p a d -> p (a d)"),
                                                     mv[:, i, 0:1], rstd[:, i:i + 1], ALU.subtract, ALU.mult)
                        last.then_inc(S_("yn_made"), 1)
                        for k in range(KT):
                            eng.wait_ge(S_("y_hi"), b * KT + k + 1)
                            eng.wait_ge(S_("y_kept"), ONE + b * 2)
                            eng.tensor_tensor(yT_lo[:, k, :], bank[4 + k], yT_hi[:, k, :].bitcast(fp32),
                                              ALU.subtract).then_inc(S_("y_lo"), 1)
                        eng.tensor_copy(x2T_hi[:, :, bass.ds(b * S, S)], yT_hi[:, :, :].bitcast(fp32))\
                           .then_inc(S_("y_kept"), 1)
                        eng.wait_ge(S_("y_lo"), b * KT + KT)
                        eng.tensor_copy(x2T_lo[:, :, bass.ds(b * S, S)], yT_lo[:, :, :].bitcast(fp32))\
                           .then_inc(S_("y_kept"), 1)
                        eng.wait_ge(S_("routed"), b + 1)
                        eng.tensor_tensor(logits[:, bass.ds(b * ST, ST), :],
                                          bank[6][:, 0:ST * E].rearrange("p (i e) -> p i e", i=ST),
                                          br_b[:, :].rearrange("p (a e) -> p a e", a=1).broadcast_to([128, ST, E]),
                                          ALU.add).then_inc(S_("logits_made"), 1)
                        eng.wait_ge(S_("yn_made"), b + 1)
                        eng.wait_ge(S_("y_kept"), ONE + b * 2 + 2)

                @block.tensor
                def _(eng):
                    def three(out_ap, lhs, rhs):
                        n = 0
                        for k in range(KT):
                            for a, c in ((0, 0), (0, 1), (1, 0)):
                                last = eng.matmul(out_ap, lhs(a, k), rhs(c, k), start=(n == 0), stop=(n == 3 * KT - 1))
                                n += 1
                        return last

                    eng.wait_ge(S_("wr_lo"), 1)
                    with eng.Fori(0, B) as b:
                        eng.wait_ge(S_("a_copied"), b + 1)
                        for k in range(KT):
                            eng.wait_ge(S_("a_lo"), ONE + b * KT)
                            for i in range(ST):
                                last = eng.transpose(bank[k][:, 128 * i:128 * i + 128],
                                                     a_st[:, i, 128 * k:128 * k + 128], ident[:, :])
                            last.then_inc(S_("a_turned"), 1)
                        eng.wait_ge(S_("a_lo"), ONE + b * KT + KT)
                        eng.wait_ge(S_("o_biased"), ONE + b * (ST // 2))
                        for i in range(ST):
                            three(bank[2 + i // 2][:, D * (i % 2):D * (i % 2) + D],
                                  lambda a, k: (aT_hi, aT_lo)[a][:, k, 128 * i:128 * i + 128],
                                  lambda a, k: (wo_hi, wo_lo)[a][:, k, :]).then_inc(S_("o_proj"), 1)
                        eng.wait_ge(S_("yn_made"), b + 1)
                        for k in range(KT):
                            for i in range(ST):
                                last = eng.transpose(bank[4 + k][:, 128 * i:128 * i + 128],
                                                     y_st[:, i, 128 * k:128 * k + 128], ident[:, :])
                            last.then_inc(S_("y_turned"), 1)
                        eng.wait_ge(S_("y_lo"), b * KT + KT)
                        eng.wait_ge(S_("logits_made"), ONE + b)
                        for i in range(ST):
                            last = three(bank[6][:, E * i:E * i + E],
                                         lambda a, k: (yT_hi, yT_lo)[a][:, k, 128 * i:128 * i + 128],
                                         lambda a, k: (wr_hi, wr_lo)[a][:, k, :])
                        last.then_inc(S_("routed"), 1)

        with ExitStack() as ph:
            def sb4(name, shape, dt=fp32):
                return ph.enter_context(nc.sbuf_tensor(name, shape, dt))

            HR = 4
            r_sb = [sb4(f"r_sb{i}", [128, TBS]) for i in range(HR)]
            h_hi = [sb4(f"h_hi{i}", [128, TBS], f32r) for i in range(HR)]
            h_lo = [sb4(f"h_lo{i}", [128, TBS], f32r) for i in range(HR)]
            y_sb = sb4("y_sb", [128, ST, D])
            acc = attn
            xs = sb4("xs", [128, NT, E])
            zz = sb4("zz", [128, NT, E])
            z2 = sb4("z2", [128, NT, E])
            gate = sb4("gate", [128, NT, E])
            tau = sb4("tau", [128, NT, 1])
            tau_m = sb4("tau_m", [128, NT, 1])
            dm = sb4("dm", [128, NT, 1])
            f_lo = sb4("f_lo", [128, NT, 1])
            f_m = sb4("f_m", [128, NT, 1])
            f_s = sb4("f_s", [128, NT, 1])
            top = sb4("top", [128, NT, 1])
            LAG = 2

            with nc.Block() as block:
                @block.sync
                def _(eng):
                    with eng.Fori(1, E // 2) as pair:
                        e = pair * 2
                        load_expert(eng, e, 0, False)
                        load_expert(eng, e + 1, 1, False)
                    for t in range(NTB):
                        eng.wait_ge(S_("out_made"), t + 1)
                        eng.dma_start(out[t, :, :].rearrange("(i p) d -> p i d", p=128),
                                      acc[:, ST * t:ST * t + ST, :]).then_inc(S_("out_done"), 16)
                    eng.wait_ge(S_("out_done"), 16 * NTB)

                @block.gpsimd
                def _(eng):
                    with eng.Fori(1, E // 2) as pair:
                        e = pair * 2
                        split_expert(eng, e, 0, False)
                        split_expert(eng, e + 1, 1, False)

                @block.scalar
                def _(eng):
                    def expert(e):
                        with eng.Fori(0, NTB) as t:
                            blk = e * (NTB * FT) + t * FT
                            for f in range(FT):
                                eng.wait_ge(S_("h_made"), blk + f + 1)
                                eng.wait_ge(S_("y_made"), ONE + blk + (f - HR + 1 if f >= HR else 0))
                                bias = b1_c[:, bass.ds(e * FT + f, 1)]
                                eng.activation(r_sb[f % HR][:, :], bank[f % HR], ACT.Relu, bias=bias)
                                eng.activation(h_hi[f % HR][:, :], bank[f % HR], ACT.Relu, bias=bias)\
                                   .then_inc(S_("relu_made"), 1)

                    with eng.Fori(0, E) as e:
                        expert(e)

                @block.vector
                def _(eng):
                    def chained(count, ops):
                        for i, op in enumerate(ops):
                            op().then_inc(S_("bisect"), 1)
                            wait_apart(eng, S_("bisect"), count + (i + 1))

                    def total(dst, tau_):
                        return [
                            lambda: eng.tensor_tensor(zz[:, :, :], xs[:, :, :],
                                                      tau_[:, :, :].broadcast_to([128, NT, E]), ALU.subtract),
                            lambda: eng.scalar_tensor_tensor(z2[:, :, :], zz[:, :, :], 0.0, zz[:, :, :],
                                                             ALU.max, ALU.mult),
                            lambda: eng.tensor_reduce(dst[:, :, :], z2[:, :, :], AX.X, ALU.add)]

                    START = [
                        lambda: eng.tensor_scalar(xs[:, :, :], logits[:, :, :], 0.5, None, ALU.mult),
                        lambda: eng.tensor_reduce(top[:, :, :], xs[:, :, :], AX.X, ALU.max),
                        lambda: eng.tensor_scalar(tau[:, :, :], top[:, :, :], -1.0, None, ALU.add),
                        lambda: eng.scalar_tensor_tensor(dm[:, :, :], top[:, :, :], -((1.0 / E) ** 0.5), tau[:, :, :],
                                                         ALU.add, ALU.subtract),
                        *total(f_lo, tau),
                        lambda: eng.tensor_scalar(f_lo[:, :, :], f_lo[:, :, :], -1.0, None, ALU.add)]
                    HALVING = [
                        lambda: eng.tensor_scalar(dm[:, :, :], dm[:, :, :], 0.5, None, ALU.mult),
                        lambda: eng.tensor_tensor(tau_m[:, :, :], tau[:, :, :], dm[:, :, :], ALU.add),
                        *total(f_m, tau_m),
                        lambda: eng.scalar_tensor_tensor(f_s[:, :, :], f_m[:, :, :], -1.0, f_lo[:, :, :],
                                                         ALU.add, ALU.mult),
                        lambda: eng.scalar_tensor_tensor(f_s[:, :, :], f_s[:, :, :], 0.0, dm[:, :, :],
                                                         ALU.is_ge, ALU.mult),
                        lambda: eng.tensor_tensor(tau[:, :, :], tau[:, :, :], f_s[:, :, :], ALU.add)]
                    NORMALISE = [
                        lambda: eng.reciprocal(f_m[:, :, :], f_m[:, :, :]),
                        lambda: eng.tensor_tensor(z2[:, :, :], z2[:, :, :],
                                                  f_m[:, :, :].broadcast_to([128, NT, E]), ALU.mult),
                        lambda: eng.scalar_tensor_tensor(gate[:, :, :], z2[:, :, :], THRESH, z2[:, :, :],
                                                         ALU.is_gt, ALU.mult)]
                    PER = BISECT // NTB

                    def token_block(pair, par, t, first):
                        n = (pair * 2 + par) * NTB + t
                        for f in range(FT):
                            eng.wait_ge(S_("relu_made"), ONE + n * FT + f + 1)
                            eng.tensor_tensor(h_lo[f % HR][:, :], r_sb[f % HR][:, :], h_hi[f % HR][:, :].bitcast(fp32),
                                              ALU.subtract).then_inc(S_("h_lo"), 1)
                            if first and f > 0 and f <= PER:
                                chained(t * (PER * len(HALVING)) + (len(START) + (f - 1) * len(HALVING)), HALVING)
                        eng.wait_ge(S_("y_made"), ONE + n * FT + FT)
                        eng.wait_ge(S_(f"b2_in{par}"), (pair + 1) * 16)
                        for j in range(ST // 2):
                            dst = acc[:, bass.ds(t * ST + 2 * j, 2), :] if first else y_sb[:, 2 * j:2 * j + 2, :]
                            eng.tensor_tensor(dst, bank[4 + j].rearrange("p (i d) -> p i d", i=2),
                                              b2_b[par][:, :].rearrange("p (a d) -> p a d", a=1)
                                              .broadcast_to([128, 2, D]), ALU.add).then_inc(S_("y_read"), 1)
                        eng.wait_ge(S_("y_read"), ONE + n * 2 + 2)

                    def weigh(e, t):
                        for i in range(ST):
                            rows = acc[:, bass.ds(t * ST + i, 1), :].rearrange("p a d -> p (a d)")
                            g = gate[:, bass.ds(t * ST + i, 1), bass.ds(e, 1)].rearrange("p a b -> p (a b)")
                            last = eng.scalar_tensor_tensor(rows, y_sb[:, i, :], g, rows, ALU.mult, ALU.add)
                        last.then_inc(S_("block_done"), 1)

                    chained(0, START)
                    with eng.Fori(0, NTB) as t:
                        token_block(0, 0, t, True)
                    done = len(START) + NTB * PER * len(HALVING)
                    for _ in range(NTB * PER, BISECT):
                        chained(done, HALVING)
                        done += len(HALVING)
                    chained(done, NORMALISE)
                    for i in range(NT):
                        last = eng.tensor_scalar(acc[:, i, :], acc[:, i, :], gate[:, i, 0:1], None, ALU.mult)
                    last.then_inc(S_("first_weighed"), 1)
                    eng.wait_ge(S_("first_weighed"), 1)
                    with eng.Fori(0, NTB) as t:
                        eng.wait_ge(S_("block_done"), ONE + t)
                        token_block(0, 1, t, False)
                        weigh(1, t)
                    with eng.Fori(1, E // 2) as pair:
                        e = pair * 2
                        for par in range(2):
                            with eng.Fori(0, NTB) as t:
                                eng.wait_ge(S_("block_done"), ONE + (e + (par - 1)) * NTB + t)
                                token_block(pair, par, t, False)
                                weigh(e + par, t)
                    eng.wait_ge(S_("block_done"), ONE + (E - 1) * NTB)
                    for t in range(NTB):
                        rows = acc[:, ST * t:ST * t + ST, :].rearrange("p i d -> p (i d)")
                        eng.scalar_tensor_tensor(rows, rows, tg[:, 1:2],
                                                 x_all[:, ST * t:ST * t + ST, :].rearrange("p i d -> p (i d)"),
                                                 ALU.mult, ALU.add).then_inc(S_("out_made"), 1)

                @block.tensor
                def _(eng):
                    def token_block(e, t, par):
                        n = e * NTB + t

                        def hidden(f):
                            eng.wait_ge(S_("relu_made"), ONE + n * FT + (f - HR + 1 if f >= HR else 0))
                            i = 0
                            for k in range(KT):
                                for a, c in ((0, 0), (0, 1), (1, 0)):
                                    last = eng.matmul(bank[f % HR], w1[par][a][:, k, 128 * f:128 * f + 128],
                                                      (x2T_hi, x2T_lo)[c][:, k, bass.ds(t * TBS, TBS)],
                                                      start=(i == 0), stop=(i == 3 * KT - 1))
                                    i += 1
                            last.then_inc(S_("h_made"), 1)

                        def project(f):
                            eng.wait_ge(S_("h_lo"), n * FT + f + 1)
                            if f == 0:
                                eng.wait_ge(S_("y_read"), ONE + n * 2)
                            for i in range(ST):
                                for a, c in ((0, 0), (0, 1), (1, 0)):
                                    first = f == 0 and (a, c) == (0, 0)
                                    last = eng.matmul(
                                        bank[4 + i // 2][:, D * (i % 2):D * (i % 2) + D],
                                        (h_hi, h_lo)[a][f % HR][:, 128 * i:128 * i + 128], w2[par][c][:, f, :],
                                        start=(first and i % 2 == 0), stop=(f == FT - 1 and (a, c) == (1, 0)),
                                        skip_group_check=True)
                            last.then_inc(S_("y_made"), 1)

                        for f in range(FT + LAG):
                            if f < FT:
                                hidden(f)
                            if f >= LAG:
                                project(f - LAG)

                    with eng.Fori(0, E // 2) as pair:
                        e = pair * 2
                        for par in range(2):
                            wait_apart(eng, S_("w_split"), (e + (par + 1)) * 4)
                            with eng.Fori(0, NTB) as t:
                                token_block(e + par, t, par)


_INS = ['x', 'ctx_1024', 'g_xattn', 'g_ffn', 'L0_xattn_wq', 'L0_xattn_bq', 'L0_xattn_wk', 'L0_xattn_bk',
        'L0_xattn_wv', 'L0_xattn_bv', 'L0_xattn_wo', 'L0_xattn_bo', 'L0_ffn_Wr', 'L0_ffn_br', 'L0_ffn_W1',
        'L0_ffn_b1', 'L0_ffn_W2', 'L0_ffn_b2']


def kernel(**inputs):
    import numpy as _np
    import concourse.bacc as _bacc
    from concourse import mybir as _mybir
    from concourse.bass_utils import run_bass_kernel_spmd as _run

    nc = _bacc.Bacc("TRN2", target_bir_lowering=False, num_devices=1)
    arrays, args = {}, []
    for name in _INS:
        a = _np.ascontiguousarray(inputs[name])
        arrays[f"in_{name}"] = a
        args.append(nc.dram_tensor(f"in_{name}", a.shape, _mybir.dt.from_np(a.dtype), kind="ExternalInput").ap())
    x = inputs['x']
    out = nc.dram_tensor("out_0", tuple(x.shape), _mybir.dt.from_np(_np.dtype('float32')), kind="ExternalOutput").ap()
    flamingo_block(nc, *args, out)
    r = _run(nc, [arrays], core_ids=[0])
    return r.results[0]["out_0"]
```

```python
import concourse.bass as bass
from concourse import mybir
from contextlib import ExitStack

fp32 = mybir.dt.float32
f32r = mybir.dt.float32r
bf16 = mybir.dt.bfloat16
ALU = mybir.AluOpType
ACT = mybir.ActivationFunctionType
AX = mybir.AxisListType


def flamingo_block(nc, x, ctx, g_xattn, g_ffn, wq, bq, wk, bk, wv, bv, wo, bo,
                   Wr, br, W1, b1, W2, b2, out):
    B, S, D = x.shape
    T = ctx.shape[1]
    H = 16
    DK = D // H
    E, F = b1.shape
    KT = D // 128
    ST = S // 128
    NT = B * ST
    TP = 124
    TN = -(-T // TP)
    CT = 4
    CW = CT * TP
    NC = -(-T // CW)
    HG = 4
    NG = H // HG
    STRIP = 32
    KPARTS = (0, 0, 1, 1, 0, 2)
    QPARTS = (0, 1, 0, 1, 2, 0)
    NB = len(KPARTS)
    KS = NB * DK
    KM = KS + 3
    HALF = (T + 1) // 2
    FT = F // 128
    TBS = S
    NTB = B * S // TBS
    EPS = 1e-5
    BISECT = 25
    THRESH = 1e-9

    def tile_rows(n):
        return min(TP, T - n * TP)

    def chunk_cols(c):
        return min(CW, T - c * CW)

    kd = nc.dram_tensor("k_parts_dram", (B, 3, D, T), bf16).ap()
    qd = nc.dram_tensor("q_parts_dram", (B, 3, D, S), bf16).ap()
    vd = nc.dram_tensor("v_strips_dram", (B, 128, NG * TN * HG * STRIP), fp32).ap()

    with ExitStack() as es:
        def sb(name, shape, dt=fp32):
            return es.enter_context(nc.sbuf_tensor(name, shape, dt))

        def sem(name):
            return es.enter_context(nc.semaphore(name))

        psum = es.enter_context(nc.psum_tensor("psum", [128, 8 * 512], fp32))
        bank = [psum[:, 512 * i:512 * i + 512] for i in range(8)]
        pv_acc = bank[7]

        ident = sb("ident", [128, 128])
        ident_bf = sb("ident_bf", [128, 128], bf16)
        x_all = sb("x_all", [128, NT, D])
        a_st = sb("a_st", [128, ST, D])
        BROWS = E * FT + 2 * KT
        bias_rows = sb("bias_rows", [BROWS, 128])
        bias_c = sb("bias_c", [128, BROWS])
        bk_c = bias_c[:, E * FT:E * FT + KT]
        bq_c = bias_c[:, E * FT + KT:BROWS]
        b1_c = bias_c[:, 0:E * FT]
        bv_b = sb("bv_b", [128, D])
        bo_b = sb("bo_b", [128, D])
        br_b = sb("br_b", [128, E])
        wr_raw = sb("wr_raw", [128, KT, E])
        wr_hi = sb("wr_hi", [128, KT, E], f32r)
        wr_lo = sb("wr_lo", [128, KT, E], f32r)
        gates_raw = sb("gates_raw", [128, 2])
        tg = sb("tg", [128, 2])
        stats = sb("stats", [128, ST, 6])
        mv = sb("mv", [128, ST, 2])
        vpe = sb("vpe", [128, ST])
        rstd = sb("rstd", [128, ST])
        neg_half = sb("neg_half", [128, ST])
        wo_raw = sb("wo_raw", [128, KT, D])
        wo_hi = sb("wo_hi", [128, KT, D], f32r)
        wo_lo = sb("wo_lo", [128, KT, D], f32r)

        o_sb = sb("o_sb", [128, S])
        rec = sb("rec", [128, ST, HG])
        mx2 = sb("mx2", [128, ST, HG, 2])
        mx = sb("mx", [128, ST, HG])
        mrest = sb("mrest", [128, 2, ST, HG])
        mparts = sb("mparts", [128, ST, HG, 3], bf16)
        mrow = sb("mrow", [HG * 3, S], bf16)

        EARLY = 2

        def stack(i):
            return (nc.sbuf_tensor(f"k_st{i}", [128, HG, T + T % 2], bf16),
                    nc.sbuf_tensor(f"q_st{i}", [128, HG, S], bf16))

        early = [[es.enter_context(t) for t in stack(i)] for i in range(EARLY)]

        sems = {}

        def S_(name):
            if name not in sems:
                sems[name] = sem(name)
            return sems[name]

        ONE = 1
        FROM_ONE = ("rstd_made", "parts_made", "rest_made", "full_made", "c_lo", "v_made",
                    "qp_out", "x_tr", "rstd2_made", "y_kept", "y_read", "relu_made",
                    "y_made", "kp_out0", "kp_out1", "attn_made", "v_out_done0", "v_out_done1",
                    "v_out_done2", "v_out_done3")

        def load_kq(eng, k_stack, q_stack, b, hg):
            for j in range(NB):
                eng.dma_start(q_stack[DK * j:DK * j + DK, :, :],
                              qd[b, QPARTS[j], hg * HG * DK:(hg + 1) * HG * DK, :]
                              .rearrange("(h d) s -> d h s", d=DK)).then_inc(S_(f"q_in{hg}"), 16)
                eng.dma_start(k_stack[DK * j:DK * j + DK, :, 0:T],
                              kd[b, KPARTS[j], hg * HG * DK:(hg + 1) * HG * DK, :]
                              .rearrange("(h d) t -> d h t", d=DK)).then_inc(S_(f"k_in{hg}"), 16)

        def again(buf, dtype, n, pattern=None, **sizes):
            flat = buf.rearrange("p a b -> p (a b)")
            if dtype != buf.dtype:
                flat = flat[:, 0:n * 4 // mybir.dt.size(buf.dtype)].bitcast(dtype)
            return flat[:, 0:n].rearrange(pattern, **sizes) if pattern else flat[:, 0:n]

        w1_raw = again(early[0][0][:, :, :], fp32, KT * F, "p (k f) -> p k f", k=KT)
        w2_raw = again(early[1][0][:, :, :], fp32, FT * D, "p (f d) -> p f d", f=FT)

        def load_expert(eng, e):
            eng.dma_start(w1_raw[:, :, :], W1[e, :, :].rearrange("(k p) f -> p k f", p=128)).then_inc(S_("w1_in"), 16)
            eng.dma_start(w2_raw[:, :, :], W2[e, :, :].rearrange("(f p) d -> p f d", p=128)).then_inc(S_("w2_in"), 16)

        def wait_apart(eng, semaphore, value):
            if not isinstance(value, int):
                value = eng.snap(eng.to_reg(value))
            eng.wait_ge(S_("consts"), 2)
            eng.wait_ge(semaphore, value)

        with ExitStack() as ph:
            def sb0(name, shape, dt=fp32):
                return ph.enter_context(nc.sbuf_tensor(name, shape, dt))

            w_raw = [sb0(f"w_raw{i}", [128, KT, D]) for i in range(3)]
            w_hi = [sb0(f"w_hi{i}", [128, KT, D], f32r) for i in range(3)]
            w_lo = [sb0(f"w_lo{i}", [128, KT, D], f32r) for i in range(3)]
            ctx_in = sb0("ctx_in", [128, TN, D])
            cT_hi = sb0("cT_hi", [128, KT, T + 1], f32r)
            cT_lo = sb0("cT_lo", [128, KT, T + 1], f32r)
            xn = sb0("xn", [128, ST, D])
            xT_hi = sb0("xT_hi", [128, KT, S], f32r)
            xT_lo = sb0("xT_lo", [128, KT, S], f32r)
            full = [sb0(f"full{m}", [128, S]) for m in range(KT)]
            rest = [sb0(f"rest{m}", [128, S]) for m in range(KT)]
            kp = [sb0(f"kp{i}", [128, 3, KT, CW], bf16) for i in range(2)]
            qp = sb0("qp", [128, 3, KT, S], bf16)
            v_out = sb0("v_out", [128, NG, TN, HG, STRIP])

            JOBS = [("k", 0), ("k", 1), ("q", 0), ("k", 2), ("k", 3)]
            NJ = 2 * len(JOBS)

            def job_cols(kind, c):
                return chunk_cols(c) if kind == "k" else S

            def job_out(kind, c, part, m):
                return kp[c % 2][:, part, m, 0:chunk_cols(c)] if kind == "k" else qp[:, part, m, :]

            job_at = {job: 2 * i for i, job in enumerate(JOBS)}

            def store_k(eng, b, c):
                for part in range(3):
                    eng.dma_start(
                        kd[b, part, :, c * CW:c * CW + chunk_cols(c)].rearrange("(m p) t -> p m t", p=128),
                        kp[c % 2][:, part, :, 0:chunk_cols(c)]).then_inc(S_(f"kp_out{c % 2}"), 16)

            def store_v(eng, b, c):
                tiles = slice(CT * c, min(CT * c + CT, TN))
                eng.wait_ge(S_("v_made"), ONE + b * TN + tiles.stop)
                eng.dma_start(vd[b, :, :].rearrange("p (g n e) -> p g n e", g=NG, n=TN)[:, :, tiles, :],
                              v_out[:, :, tiles, :, :].rearrange("p g n h c -> p g n (h c)"))\
                   .then_inc(S_(f"v_out_done{c}"), 16)

            def store_last_chunk(eng, b):
                eng.wait_ge(S_("parts_made"), ONE + b * NJ + NJ)
                store_k(eng, b, NC - 1)
                store_v(eng, b, NC - 1)

            def over_batches(eng, batch):
                with eng.Fori(0, B - 1) as b:
                    batch(b, True)
                batch(B - 1, False)

            def v_place(n):
                return bank[4 + n // 2 % 2][0:tile_rows(n), D * (n % 2):D * (n % 2) + D]

            with nc.Block() as block:
                @block.sync
                def _(eng):
                    def load_ctx(b, c):
                        tiles = [n for n in range(CT * c, min(CT * c + CT, TN))]
                        rows = tile_rows(tiles[0])
                        src = ctx[b, c * CW:c * CW + chunk_cols(c), :]
                        eng.dma_start(ctx_in[0:rows, tiles[0]:tiles[-1] + 1, :],
                                      src.rearrange("(n p) d -> p n d", p=rows)).then_inc(S_(f"ctx_in{c}"), 16)

                    def load_x(b):
                        eng.dma_start(x_all[:, bass.ds(b * ST, ST), :],
                                      x[b, :, :].rearrange("(i p) d -> p i d", p=128)).then_inc(S_("x_in"), 16)

                    def batch(b, load_next):
                        def nxt(c):
                            if load_next:
                                eng.wait_ge(S_("ctx_tr"), b * 2 * NC + 2 * c + 2)
                                load_ctx(b + 1, c)
                        nxt(0)
                        if load_next:
                            eng.wait_ge(S_("x_in"), b * 16 + 16)
                            load_x(b + 1)
                        nxt(1)
                        for kind, c in JOBS[:-1]:
                            eng.wait_ge(S_("parts_made"), ONE + b * NJ + job_at[kind, c] + 2)
                            if kind == "k":
                                store_k(eng, b, c)
                                store_v(eng, b, c)
                                if c in (0, 1):
                                    nxt(c + 2)
                            else:
                                for part in range(3):
                                    eng.dma_start(qd[b, part, :, :].rearrange("(m p) t -> p m t", p=128),
                                                  qp[:, part, :, :]).then_inc(S_("qp_out"), 16)
                        if load_next:
                            store_last_chunk(eng, b)
                    def load_w(i):
                        eng.dma_start(w_raw[i][:, :, :], (wq, wk, wv)[i].rearrange("(k p) n -> p k n", p=128))\
                           .then_inc(S_(f"w_in{i}"), 16)

                    load_ctx(0, 0)
                    load_w(1)
                    eng.dma_start(bias_rows[E * FT:E * FT + KT, :], bk.rearrange("(m p) -> m p", p=128))\
                       .then_inc(S_("bias_in"), 16)
                    eng.dma_start(bias_rows[E * FT + KT:BROWS, :], bq.rearrange("(m p) -> m p", p=128))\
                       .then_inc(S_("bias_in"), 16)
                    eng.dma_start(bias_rows[0:E * FT, :], b1.rearrange("e (f p) -> (e f) p", p=128))\
                       .then_inc(S_("bias_in"), 16)
                    for name in FROM_ONE:
                        eng.sem_inc(S_(name), ONE)
                    load_w(0)
                    load_w(2)
                    load_ctx(0, 1)
                    eng.dma_start(bv_b[:, :], bv.rearrange("(a n) -> a n", a=1).broadcast_to([128, D]))\
                       .then_inc(S_("bv_in"), 16)
                    load_x(0)
                    for c in range(2, NC):
                        load_ctx(0, c)
                    eng.dma_start(bo_b[:, :], bo.rearrange("(a n) -> a n", a=1).broadcast_to([128, D]))\
                       .then_inc(S_("late_in"), 16)
                    eng.dma_start(br_b[:, :], br.rearrange("(a n) -> a n", a=1).broadcast_to([128, E]))\
                       .then_inc(S_("late_in"), 16)
                    eng.dma_start(wr_raw[:, :, :], Wr.rearrange("(k p) n -> p k n", p=128)).then_inc(S_("late_in"), 16)
                    eng.dma_start(wo_raw[:, :, :], wo.rearrange("(k p) n -> p k n", p=128)).then_inc(S_("late_in"), 16)
                    for i, g in enumerate((g_xattn, g_ffn)):
                        eng.dma_start(gates_raw[:, i:i + 1], g.rearrange("(a n) -> a n", a=1).broadcast_to([128, 1]))\
                           .then_inc(S_("late_in"), 16)
                    with eng.Fori(0, B - 1) as b:
                        batch(b, True)
                    for i in range(2):
                        eng.wait_ge(S_(f"kp_out{i}"), ONE + 16 * 3 * 2 * (B - 1))
                    eng.wait_ge(S_("qp_out"), ONE + 16 * 3 * (B - 1))
                    for hg in range(EARLY):
                        load_kq(eng, *early[hg], 0, hg)
                    batch(B - 1, False)

                @block.gpsimd
                def _(eng):
                    eng.memset(ident[:, :], 0.0).then_inc(S_("consts"), 1)
                    eng.wait_ge(S_("consts"), 1)
                    eng.affine_select(out=ident[:, :], in_=ident[:, :], compare_op=ALU.not_equal, fill=1.0,
                                      base=0, pattern=[[-1, 128]], channel_multiplier=1).then_inc(S_("consts"), 1)
                    eng.memset(neg_half[:, :], -0.5).then_inc(S_("consts"), 1)
                    eng.wait_ge(S_("consts"), 3)
                    eng.tensor_copy(ident_bf[:, :], ident[:, :]).then_inc(S_("consts"), 1)
                    for t in (cT_hi, cT_lo):
                        eng.memset(t[:, :, T:T + 1].bitcast(fp32), 0.0).then_inc(S_("pad_zero"), 1)
                    eng.memset(v_out[:, :, :, :, :].rearrange("p g n h c -> p (g n h c)"), 0.0)\
                       .then_inc(S_("v_init"), 1)
                    eng.wait_ge(S_("v_init"), 1)
                    eng.memset(v_out[:, :, :, :, DK:DK + 1].rearrange("p g n h c -> p (g n h c)"), 1.0)\
                       .then_inc(S_("v_init"), 1)
                    with eng.Fori(0, B) as b:
                        wait_apart(eng, S_("stats_made"), b + 1)
                        wait_apart(eng, S_("rstd_made"), ONE + b)
                        eng.tensor_scalar(vpe[:, :], mv[:, :, 1], EPS, None, ALU.add).then_inc(S_("var_made"), 1)
                        eng.wait_ge(S_("var_made"), b + 1)
                        eng.tensor_tensor(rstd[:, :], vpe[:, :], neg_half[:, :], ALU.pow).then_inc(S_("rstd_made"), 1)
                        for kind, c in JOBS:
                            for m in range(KT):
                                i, w = job_at[kind, c] + m, job_cols(kind, c)
                                eng.wait_ge(S_("first_made"), b * NJ + i + 1)
                                eng.wait_ge(S_("parts_made"), ONE + b * NJ + max(i - 1, 0))
                                eng.tensor_tensor(rest[m][:, 0:w], full[m][:, 0:w], job_out(kind, c, 0, m),
                                                  ALU.subtract).then_inc(S_("rest_made"), 1)

                @block.scalar
                def _(eng):
                    def weight_hi(i):
                        eng.wait_ge(S_(f"w_in{i}"), 16)
                        eng.activation(w_hi[i][:, :, :], w_raw[i][:, :, :], ACT.Copy).then_inc(S_("w_hi"), 1)

                    weight_hi(1)
                    eng.wait_ge(S_("bias_turned"), 1)
                    eng.activation(bias_c[:, :], bank[7][:, 0:BROWS], ACT.Copy).then_inc(S_("bias_made"), 1)
                    weight_hi(0)
                    weight_hi(2)
                    eng.wait_ge(S_("bias_made"), 1)

                    def hi(b, c, k):
                        eng.wait_ge(S_("ctx_tr"), b * 2 * NC + 2 * c + k + 1)
                        eng.activation(cT_hi[:, k, c * CW:c * CW + chunk_cols(c)], bank[k][:, 0:chunk_cols(c)],
                                       ACT.Copy).then_inc(S_("c_hi"), 1)

                    def job(b, kind, c, m):
                        i, w = job_at[kind, c] + m, job_cols(kind, c)
                        eng.wait_ge(S_("proj_made"), b * NJ + i + 1)
                        eng.wait_ge(S_("rest_made"), ONE + b * NJ + max(i - 1, 0))
                        bias = bk_c if kind == "k" else bq_c
                        src = bank[2 + m] if kind == "k" else bank[6 + m]
                        eng.activation(full[m][:, 0:w], src[:, 0:w], ACT.Identity,
                                       bias=bias[:, m:m + 1]).then_inc(S_("full_made"), 1)

                    def batch(b, more):
                        for k in range(KT):
                            hi(b, 1, k)
                        job(b, "k", 0, 0)
                        job(b, "k", 0, 1)
                        for k in range(KT):
                            eng.wait_ge(S_("x_tr"), ONE + b * KT + k + 1)
                            eng.activation(xT_hi[:, k, :], bank[6 + k], ACT.Copy).then_inc(S_("x_hi"), 1)
                        for k in range(KT):
                            hi(b, 2, k)
                        job(b, "k", 1, 0)
                        job(b, "k", 1, 1)
                        job(b, "q", 0, 0)
                        job(b, "q", 0, 1)
                        for k in range(KT):
                            hi(b, 3, k)
                        for c in (2, 3):
                            if c == 3 and more:
                                for k in range(KT):
                                    hi(b + 1, 0, k)
                            job(b, "k", c, 0)
                            job(b, "k", c, 1)

                    for k in range(KT):
                        hi(0, 0, k)
                    over_batches(eng, batch)

                @block.vector
                def _(eng):
                    for n, i in enumerate((1, 0, 2)):
                        eng.wait_ge(S_("w_hi"), n + 1)
                        eng.tensor_tensor(w_lo[i][:, :, :], w_raw[i][:, :, :], w_hi[i][:, :, :].bitcast(fp32),
                                          ALU.subtract).then_inc(S_("w_lo"), 1)

                    def lo(b, c, k):
                        cols = slice(c * CW, c * CW + chunk_cols(c))
                        eng.wait_ge(S_("c_hi"), b * 2 * NC + 2 * c + k + 1)
                        eng.tensor_tensor(cT_lo[:, k, cols], bank[k][:, 0:chunk_cols(c)],
                                          cT_hi[:, k, cols].bitcast(fp32), ALU.subtract).then_inc(S_("c_lo"), 1)

                    def first(b, kind, c, m):
                        i, w = job_at[kind, c] + m, job_cols(kind, c)
                        eng.wait_ge(S_("full_made"), ONE + b * NJ + i + 1)
                        if m == 0:
                            if kind == "k":
                                eng.wait_ge(S_(f"kp_out{c % 2}"), ONE + (b * 2 + c // 2) * 48)
                            else:
                                eng.wait_ge(S_("qp_out"), ONE + b * 48)
                        eng.tensor_copy(job_out(kind, c, 0, m), full[m][:, 0:w]).then_inc(S_("first_made"), 1)

                    def others(b, kind, c, m):
                        i, w = job_at[kind, c] + m, job_cols(kind, c)
                        eng.wait_ge(S_("rest_made"), ONE + b * NJ + i + 1)
                        eng.tensor_copy(job_out(kind, c, 1, m), rest[m][:, 0:w]).then_inc(S_("second_made"), 1)
                        eng.wait_ge(S_("second_made"), b * NJ + i + 1)
                        eng.tensor_tensor(job_out(kind, c, 2, m), rest[m][:, 0:w], job_out(kind, c, 1, m),
                                          ALU.subtract).then_inc(S_("parts_made"), 1)

                    def v_rows(b, n):
                        rows = tile_rows(n)
                        if n % CT == 0:
                            eng.wait_ge(S_(f"v_out_done{n // CT}"), ONE + b * 16)
                        eng.wait_ge(S_("v_proj"), b * TN + min(n // 2 * 2 + 2, TN))
                        eng.tensor_tensor(v_out[0:rows, :, n, :, 0:DK],
                                          v_place(n).rearrange("p (g h c) -> p g h c", g=NG, h=HG),
                                          bv_b[0:rows, :].rearrange("p (g h c) -> p g h c", g=NG, h=HG),
                                          ALU.add).then_inc(S_("v_made"), 1)

                    def kv(b, c, amid=None):
                        first(b, "k", c, 0)
                        first(b, "k", c, 1)
                        tiles = list(range(CT * c, min(CT * c + CT, TN)))
                        if amid:
                            amid(b)
                        for m in range(KT):
                            for n in tiles[2 * m:2 * m + 2]:
                                v_rows(b, n)
                            others(b, "k", c, m)

                    def normalise_x(b):
                        eng.wait_ge(S_("rstd_made"), ONE + b + 1)
                        eng.wait_ge(S_("x_tr"), ONE + b * KT)
                        for i in range(ST):
                            eng.tensor_scalar(xn[:, i, :],
                                              x_all[:, bass.ds(b * ST + i, 1), :].rearrange("p a d -> p (a d)"),
                                              mv[:, i, 0:1], rstd[:, i:i + 1], ALU.subtract, ALU.mult)\
                               .then_inc(S_("xn_made"), 1)

                    def batch(b, more):
                        wait_apart(eng, S_("x_in"), b * 16 + 16)
                        for i in range(ST):
                            eng.bn_stats(stats[:, i, :], x_all[:, bass.ds(b * ST + i, 1), :]
                                         .rearrange("p a d -> p (a d)")).then_inc(S_("bn_made"), 1)
                        lo(b, 1, 0)
                        lo(b, 1, 1)
                        wait_apart(eng, S_("bn_made"), b * ST + ST)
                        for i in range(ST):
                            last = eng.bn_aggr(mv[:, i, :], stats[:, i, :])
                        last.then_inc(S_("stats_made"), 1)
                        eng.wait_ge(S_("bv_in"), 16)
                        eng.wait_ge(S_("v_init"), 2)
                        kv(b, 0, amid=normalise_x)
                        for k in range(KT):
                            eng.wait_ge(S_("x_hi"), b * KT + k + 1)
                            eng.tensor_tensor(xT_lo[:, k, :], bank[6 + k], xT_hi[:, k, :].bitcast(fp32),
                                              ALU.subtract).then_inc(S_("x_lo"), 1)
                        lo(b, 2, 0)
                        lo(b, 2, 1)
                        kv(b, 1)
                        first(b, "q", 0, 0)
                        first(b, "q", 0, 1)
                        lo(b, 3, 0)
                        lo(b, 3, 1)
                        others(b, "q", 0, 0)
                        others(b, "q", 0, 1)
                        kv(b, 2)
                        if more:
                            lo(b + 1, 0, 0)
                            lo(b + 1, 0, 1)
                        kv(b, 3)
                        eng.wait_ge(S_("xn_made"), b * ST + ST)

                    lo(0, 0, 0)
                    lo(0, 0, 1)
                    over_batches(eng, batch)

                @block.tensor
                def _(eng):
                    eng.wait_ge(S_("consts"), 2)
                    eng.wait_ge(S_("bias_in"), 48)
                    eng.transpose(bank[7][:, 0:BROWS], bias_rows[:, :], ident[0:BROWS, 0:BROWS])\
                       .then_inc(S_("bias_turned"), 1)

                    def turn_ctx(b, c):
                        tiles = list(range(CT * c, min(CT * c + CT, TN)))
                        eng.wait_ge(S_(f"ctx_in{c}"), b * 16 + 16)
                        for k in range(KT):
                            eng.wait_ge(S_("c_lo"), ONE + b * 2 * NC + (2 * c - 2 + k + 1 if c else 0))
                            for n in tiles:
                                rows = tile_rows(n)
                                o = (n - tiles[0]) * TP
                                last = eng.transpose(bank[k][:, o:o + rows], ctx_in[0:rows, n, 128 * k:128 * k + 128],
                                                     ident[0:rows, 0:rows])
                            last.then_inc(S_("ctx_tr"), 1)

                    def three(out_ap, lhs, rhs):
                        n = 0
                        for k in range(KT):
                            for a, c in ((0, 0), (0, 1), (1, 0)):
                                last = eng.matmul(out_ap, lhs(a, k), rhs(c, k), start=(n == 0), stop=(n == 3 * KT - 1))
                                n += 1
                        return last

                    def project_k(b, c):
                        cols = slice(c * CW, c * CW + chunk_cols(c) + chunk_cols(c) % 2)
                        w = chunk_cols(c) + chunk_cols(c) % 2
                        eng.wait_ge(S_("c_lo"), ONE + b * 2 * NC + 2 * c + 2)
                        for m in range(KT):
                            eng.wait_ge(S_("full_made"), ONE + b * NJ + (job_at["k", c - 1] + m + 1 if c else 0))
                            three(bank[2 + m][:, 0:w],
                                  lambda a, k: (w_hi, w_lo)[a][1][:, k, 128 * m:128 * m + 128],
                                  lambda a, k: (cT_hi, cT_lo)[a][:, k, cols]).then_inc(S_("proj_made"), 1)

                    def project_v(b, c):
                        for n in range(CT * c, min(CT * c + CT, TN)):
                            rows = tile_rows(n)
                            if n % 2 == 0:
                                eng.wait_ge(S_("v_made"), ONE + b * TN + (n - 2 if n > 3 else 0))
                            three(v_place(n),
                                  lambda a, k: (cT_hi, cT_lo)[a][:, k, n * TP:n * TP + rows],
                                  lambda a, k: (w_hi, w_lo)[a][2][:, k, :]).then_inc(S_("v_proj"), 1)

                    eng.wait_ge(S_("pad_zero"), 2)
                    def batch(b, more):
                        turn_ctx(b, 1)
                        eng.wait_ge(S_("w_lo"), 1)
                        project_k(b, 0)
                        eng.wait_ge(S_("w_lo"), 3)
                        project_v(b, 0)
                        eng.wait_ge(S_("bias_made"), 1)
                        eng.wait_ge(S_("xn_made"), b * ST + ST)
                        for k in range(KT):
                            eng.wait_ge(S_("full_made"), ONE + b * NJ)
                            for i in range(ST):
                                last = eng.transpose(bank[6 + k][:, 128 * i:128 * i + 128],
                                                     xn[:, i, 128 * k:128 * k + 128], ident[:, :])
                            last.then_inc(S_("x_tr"), 1)
                        turn_ctx(b, 2)
                        project_k(b, 1)
                        project_v(b, 1)
                        eng.wait_ge(S_("x_lo"), b * KT + KT)
                        for m in range(KT):
                            three(bank[6 + m],
                                  lambda a, k: (w_hi, w_lo)[a][0][:, k, 128 * m:128 * m + 128],
                                  lambda a, k: (xT_hi, xT_lo)[a][:, k, :]).then_inc(S_("proj_made"), 1)
                        turn_ctx(b, 3)
                        project_k(b, 2)
                        project_v(b, 2)
                        if more:
                            turn_ctx(b + 1, 0)
                        project_k(b, 3)
                        project_v(b, 3)

                    turn_ctx(0, 0)
                    over_batches(eng, batch)

        x2T_hi, x2T_lo = [es.enter_context(nc.sbuf_tensor(f"x2T_{p}", [128, KT, NT * 128], f32r)) for p in ("hi", "lo")]
        logits = es.enter_context(nc.sbuf_tensor("logits", [128, NT, E], fp32))
        rT_hi, rT_lo = [es.enter_context(nc.sbuf_tensor(f"rT_{p}", [128, KT, S], f32r)) for p in ("hi", "lo")]
        y_st = es.enter_context(nc.sbuf_tensor("y_st", [128, ST, D], fp32))
        slot = [psum[:, 0:1024], psum[:, 1024:2048], psum[:, 3072:4096]]

        def tail_items(g):
            return [(kind, g) for kind in
                    ("attn_turn", "out_proj", "residual", "row_stats", "y_norm", "y_turn", "route")]

        def turn_rows(eng, rows, sl):
            for k in range(KT):
                for i in range(ST):
                    last = eng.transpose(slot[sl][:, S * k + 128 * i:S * k + 128 * i + 128],
                                         rows[:, i, 128 * k:128 * k + 128], ident[:, :])
            return last

        def three_passes(eng, out_ap, lhs, rhs):
            n = 0
            for k in range(KT):
                for a, c in ((0, 0), (0, 1), (1, 0)):
                    last = eng.matmul(out_ap, lhs(a, k), rhs(c, k), start=(n == 0), stop=(n == 3 * KT - 1))
                    n += 1
            return last

        def pe_attn_turn(eng, b, pos, sl):
            eng.wait_ge(S_("attn_made"), ONE + (b + 1) * NG)
            eng.wait_ge(S_("slot_read"), pos - 1)
            turn_rows(eng, a_st, sl).then_inc(S_("slot_made"), 1)

        def pe_out_proj(eng, b, pos, sl):
            eng.wait_ge(S_("rows_lo"), b * 2 + 1)
            eng.wait_ge(S_("wo_lo"), 1)
            eng.wait_ge(S_("slot_read"), pos - 1)
            for i in range(ST):
                last = three_passes(eng, slot[sl][:, D * i:D * i + D],
                                    lambda a, k: (rT_hi, rT_lo)[a][:, k, 128 * i:128 * i + 128],
                                    lambda a, k: (wo_hi, wo_lo)[a][:, k, :])
            last.then_inc(S_("slot_made"), 1)

        def pe_y_turn(eng, b, pos, sl):
            eng.wait_ge(S_("yn_made"), b + 1)
            eng.wait_ge(S_("slot_read"), pos - 1)
            turn_rows(eng, y_st, sl).then_inc(S_("slot_made"), 1)

        def pe_route(eng, b, pos, sl):
            eng.wait_ge(S_("rows_lo"), b * 2 + 2)
            eng.wait_ge(S_("wr_lo"), 1)
            eng.wait_ge(S_("slot_read"), pos - 1)
            for i in range(ST):
                last = three_passes(eng, slot[sl][:, E * i:E * i + E],
                                    lambda a, k: (rT_hi, rT_lo)[a][:, k, 128 * i:128 * i + 128],
                                    lambda a, k: (wr_hi, wr_lo)[a][:, k, :])
            last.then_inc(S_("slot_made"), 1)

        def act_rows_hi(turn):
            def step(eng, b, pos, sl):
                eng.wait_ge(S_("slot_made"), pos + 1)
                if turn == 0:
                    eng.wait_ge(S_("y_kept"), ONE + b * 2)
                eng.activation(rT_hi[:, :, :].rearrange("p k s -> p (k s)"), slot[sl], ACT.Copy)\
                   .then_inc(S_("rows_hi"), 1)
            return step

        def dve_rows_lo(turn):
            def step(eng, b, pos, sl):
                eng.wait_ge(S_("rows_hi"), b * 2 + turn + 1)
                eng.tensor_tensor(rT_lo[:, :, :].rearrange("p k s -> p (k s)"), slot[sl],
                                  rT_hi[:, :, :].rearrange("p k s -> p (k s)").bitcast(fp32),
                                  ALU.subtract).then_inc(S_("rows_lo"), 1)
                eng.wait_ge(S_("rows_lo"), b * 2 + turn + 1)
                eng.sem_inc(S_("slot_read"), 1)
            return step

        def dve_out_proj(eng, b, pos, sl):
            eng.wait_ge(S_("slot_made"), pos + 1)
            eng.tensor_tensor(y_st[:, :, :], slot[sl].rearrange("p (i d) -> p i d", i=ST),
                              bo_b[:, :].rearrange("p (a d) -> p a d", a=1).broadcast_to([128, ST, D]),
                              ALU.add).then_inc(S_("slot_read"), 1)

        def dve_residual(eng, b, pos, sl):
            eng.wait_ge(S_("slot_read"), pos)
            rows = x_all[:, bass.ds(b * ST, ST), :].rearrange("p i d -> p (i d)")
            eng.scalar_tensor_tensor(rows, y_st[:, :, :].rearrange("p i d -> p (i d)"), tg[:, 0:1],
                                     rows, ALU.mult, ALU.add).then_inc(S_("x2_made"), 1)

        def dve_row_stats(eng, b, pos, sl):
            wait_apart(eng, S_("x2_made"), b + 1)
            for i in range(ST):
                last = eng.bn_stats(stats[:, i, :], x_all[:, bass.ds(b * ST + i, 1), :]
                                    .rearrange("p a d -> p (a d)"))
            last.then_inc(S_("bn2_made"), 1)
            wait_apart(eng, S_("bn2_made"), b + 1)
            for i in range(ST):
                last = eng.bn_aggr(mv[:, i, :], stats[:, i, :])
            last.then_inc(S_("stats2_made"), 1)

        def dve_y_norm(eng, b, pos, sl):
            eng.wait_ge(S_("rstd2_made"), ONE + b + 1)
            for i in range(ST):
                last = eng.tensor_scalar(y_st[:, i, :],
                                         x_all[:, bass.ds(b * ST + i, 1), :].rearrange("p a d -> p (a d)"),
                                         mv[:, i, 0:1], rstd[:, i:i + 1], ALU.subtract, ALU.mult)
            last.then_inc(S_("yn_made"), 1)

        def dve_route(eng, b, pos, sl):
            eng.wait_ge(S_("slot_made"), pos + 1)
            eng.tensor_tensor(logits[:, bass.ds(b * ST, ST), :],
                              slot[sl][:, 0:ST * E].rearrange("p (i e) -> p i e", i=ST),
                              br_b[:, :].rearrange("p (a e) -> p a e", a=1).broadcast_to([128, ST, E]),
                              ALU.add).then_inc(S_("slot_read"), 1)

        TAIL_PE = dict(attn_turn=pe_attn_turn, out_proj=pe_out_proj, y_turn=pe_y_turn, route=pe_route)
        TAIL_ACT = dict(attn_turn=act_rows_hi(0), y_turn=act_rows_hi(1))
        TAIL_DVE = dict(attn_turn=dve_rows_lo(0), out_proj=dve_out_proj, residual=dve_residual,
                        row_stats=dve_row_stats, y_norm=dve_y_norm, y_turn=dve_rows_lo(1), route=dve_route)

        def inverse_deviation(eng, b):
            wait_apart(eng, S_("stats2_made"), b + 1)
            eng.tensor_scalar(vpe[:, :], mv[:, :, 1], EPS, None, ALU.add).then_inc(S_("var2_made"), 1)
            eng.wait_ge(S_("var2_made"), b + 1)
            eng.tensor_tensor(rstd[:, :], vpe[:, :], neg_half[:, :], ALU.pow).then_inc(S_("rstd2_made"), 1)

        def keep_rows(eng, b):
            for part, kept, name in ((rT_hi, x2T_hi, "rows_hi"), (rT_lo, x2T_lo, "rows_lo")):
                wait_apart(eng, S_(name), b * 2 + 2)
                eng.tensor_copy(kept[:, :, bass.ds(b * S, S)], part[:, :, :].bitcast(fp32)).then_inc(S_("y_kept"), 1)

        TILES = NG * TN
        EXPS = TILES * HG
        PR = 4
        LAG_V = 2
        UNITS = HG * ST * 2
        TAIL_AT = (10, 15, 17, 20, 25, 28, 33)
        LEAD = 14
        FIRST_LEAD = 8
        TURN_AT = 3
        O_AT = 8
        ITEMS = UNITS + 2

        with ExitStack() as ph:
            def sb1(name, shape, dt=fp32):
                return ph.enter_context(nc.sbuf_tensor(name, shape, dt))

            stacks = early + [[ph.enter_context(t) for t in stack(i)] for i in range(EARLY, NG)]
            k_st, q_st = [st[0] for st in stacks], [st[1] for st in stacks]
            v_st = [sb1(f"v_st{i}", [128, TN, HG * STRIP]) for i in range(2)]
            prob = [sb1(f"prob{i}", [128, HG, S]) for i in range(PR)]

            def plus(b, hg, k):
                b, hg = b + (hg + k) // NG, (hg + k) % NG
                return None if isinstance(b, int) and b >= B else (b, hg)

            def is_group(b, hg, of_b, of_hg):
                return isinstance(b, int) and (b, hg) == (of_b, of_hg)

            def units(g, first, end):
                return [("unit", g, u) for u in range(first, end)] if g else []

            def lead(b, hg):
                return FIRST_LEAD if is_group(b, hg, 0, 1) else LEAD

            def head_start(g, g2):
                return units(g2, 0, TURN_AT) + [("turn", g)] + (units(g2, TURN_AT, lead(*g2)) if g2 else [])

            def slot_items(b, hg):
                g, g2 = plus(b, hg, 1), plus(b, hg, 2)
                items = (units(g, lead(*g), UNITS) + head_start(g, g2)) if g else []
                if not is_group(b, hg, 0, 0):
                    items.insert(O_AT, ("output", plus(b, hg, -1)))
                    if hg == 0:
                        for at, item in zip(TAIL_AT, tail_items(plus(b, hg, -1))):
                            items.insert(at, item)
                if not g:
                    return [[], [], []] + [items] + [[] for _ in range(TN - 4)]
                steps = [[] for _ in range(TN)]
                for i, item in enumerate(items):
                    steps[i * TN // max(ITEMS, len(items))].append(item)
                return steps

            PROLOGUE = units((0, 0), 0, UNITS) + head_start((0, 0), (0, 1))

            def through_slots(items):
                return sum(kind not in TAIL_DVE or kind in TAIL_PE for kind, *_ in items)

            def slot_base(b, hg):
                if is_group(b, hg, 0, 0):
                    return len(PROLOGUE)
                if is_group(b, hg, B - 1, NG - 1):
                    return slot_base(B - 1, NG - 2) + sum(map(through_slots, slot_items(B - 1, NG - 2)))
                tails = b - (1 if hg == 0 else 0)
                return (b * NG + hg) * ITEMS + tails * len(TAIL_PE) + (UNITS + LEAD)

            def slot_of(b, hg, i):
                return (len(PROLOGUE) - (0 if is_group(b, hg, 0, 0) else 1) + i) % 2

            def numbered(b, hg):
                i = 0
                for n, items in enumerate(slot_items(b, hg)):
                    for item in items:
                        yield n, item, slot_base(b, hg) + i, slot_of(b, hg, i)
                        i += through_slots([item])

            def turn_count(b, hg):
                for _, item, pos, _ in numbered(b, hg):
                    if item[0] == "turn":
                        return pos + 1

            PROLOGUE_TURN = PROLOGUE.index(("turn", (0, 0))) + 1
            LAST_OUTPUT = slot_base(B - 1, NG - 1) + 1
            LAST_TAIL, n = [], LAST_OUTPUT + 1
            for kind, g in tail_items((B - 1, NG - 1)):
                LAST_TAIL.append((kind, g, n, slot_of(B - 1, NG - 1, n - slot_base(B - 1, NG - 1))
                                  if kind == "attn_turn" else 2))
                n += kind in TAIL_PE

            def over_groups(eng, group):
                group(0, 0)
                with eng.Fori(0, B - 1) as b:
                    for hg in range(1, NG):
                        group(b, hg)
                    group(b + 1, 0)
                for hg in range(1, NG):
                    group(B - 1, hg)

            def not_below_zero(value):
                return max(value, 0) if isinstance(value, int) else value

            with nc.Block() as block:
                @block.sync
                def _(eng):
                    def load_v(b, hg):
                        cols = TN * HG * STRIP
                        eng.dma_start(v_st[hg % 2][:, :, :].rearrange("p n c -> p (n c)"),
                                      vd[b, :, hg * cols:(hg + 1) * cols]).then_inc(S_(f"v_in{hg % 2}"), 16)

                    def store_max(b, hg, count):
                        eng.wait_ge(S_("slot_read"), count)
                        for h in range(HG):
                            eng.dma_start(q_st[hg][KS:KM, h, :], mrow[3 * h:3 * h + 3, :])\
                               .then_inc(S_(f"m_in{hg}"), 16)

                    def group(b, hg):
                        if plus(b, hg, 3):
                            eng.wait_ge(S_("scores_made"), b * EXPS + hg * TN * HG)
                            b3, hg3 = plus(b, hg, 3)
                            load_kq(eng, k_st[hg3], q_st[hg3], b3, hg3)
                        if plus(b, hg, 1):
                            eng.wait_ge(S_("pv_tile"), b * TILES + hg * TN)
                            load_v(*plus(b, hg, 1))
                            store_max(*plus(b, hg, 1), turn_count(b, hg))

                    store_last_chunk(eng, B - 1)
                    for i in range(2):
                        eng.wait_ge(S_(f"kp_out{i}"), ONE + 16 * 3 * 2 * B)
                    eng.wait_ge(S_("qp_out"), ONE + 16 * 3 * B)
                    for c in range(NC):
                        eng.wait_ge(S_(f"v_out_done{c}"), ONE + 16 * B)
                    eng.sem_inc(S_("parts_stored"), 1)
                    load_v(0, 0)
                    for hg in range(EARLY, 3):
                        load_kq(eng, k_st[hg], q_st[hg], 0, hg)
                    store_max(0, 0, PROLOGUE_TURN)
                    over_groups(eng, group)
                    eng.wait_ge(S_("scores_made"), (B - 1) * EXPS + EARLY * TN * HG)
                    load_expert(eng, 0)

                @block.gpsimd
                def _(eng):
                    for i in range(NG):
                        if i == EARLY:
                            eng.wait_ge(S_("parts_stored"), 1)
                        eng.memset(k_st[i][KS:KM, :, :], -1.0).then_inc(S_("minus_ones"), 1)
                    with eng.Fori(0, B - 1) as b:
                        inverse_deviation(eng, b)
                        keep_rows(eng, b)

                @block.scalar
                def _(eng):
                    def copy_output(q):
                        eng.wait_ge(S_("pv_tile"), q * TN + TN)
                        eng.activation(o_sb[:, :], pv_acc[:, :], ACT.Copy).then_inc(S_("o_copied"), 1)

                    def group(b, hg):
                        items = [it for it in numbered(b, hg) if it[1][0] not in TAIL_DVE or it[1][0] in TAIL_PE]
                        for n in range(TN):
                            tt, rows = hg * TN + n, tile_rows(n)
                            todo = [it for it in items if it[0] == n]

                            def one():
                                if todo:
                                    _, (kind, g, *_), pos, sl = todo.pop(0)
                                    if kind in TAIL_ACT:
                                        TAIL_ACT[kind](eng, g[0], pos, sl)

                            one()
                            eng.wait_ge(S_("pv_tile"), not_below_zero(b * TILES + (tt - PR + 1)))
                            for h in range(HG):
                                i = tt * HG + h
                                eng.wait_ge(S_("scores_made"), b * EXPS + i + 1)
                                eng.activation(prob[tt % PR][0:rows, h, :], bank[4 + i % 3][0:rows, :], ACT.Exp,
                                               scale=float(DK) ** -0.5).then_inc(S_("exp_made"), 1)
                                if h == 1:
                                    one()
                            while todo:
                                one()
                            if n == LAG_V - 2 and not is_group(b, hg, 0, 0):
                                copy_output(b * NG + (hg - 1))

                    eng.wait_ge(S_("late_in"), 96)
                    eng.activation(tg[:, :], gates_raw[:, :], ACT.Tanh).then_inc(S_("tanh_made"), 1)
                    eng.activation(wr_hi[:, :, :], wr_raw[:, :, :], ACT.Copy).then_inc(S_("wr_hi"), 1)
                    eng.activation(wo_hi[:, :, :], wo_raw[:, :, :], ACT.Copy).then_inc(S_("wo_hi"), 1)
                    over_groups(eng, group)
                    copy_output(B * NG - 1)

                @block.vector
                def _(eng):
                    def maximum(b, hg, u, pos, sl):
                        h, st, half = u // (2 * ST), u // 2 % ST, u % 2
                        w = T - HALF if half else HALF
                        eng.wait_ge(S_("slot_made"), pos + 1)
                        eng.tensor_reduce(mx2[:, st, h, half:half + 1], slot[sl][:, 0:w], AX.X, ALU.max)\
                           .then_inc(S_("slot_read"), 1)
                        if u == UNITS - 1:
                            eng.wait_ge(S_("slot_read"), pos + 1)
                            split_maxima((b * NG + hg) * 6)

                    def split_maxima(count):
                        eng.tensor_reduce(mx[:, :, :], mx2[:, :, :, :], AX.X, ALU.max).then_inc(S_("m_step"), 1)
                        eng.wait_ge(S_("m_step"), count + 1)
                        eng.tensor_copy(mparts[:, :, :, 0], mx[:, :, :]).then_inc(S_("m_step"), 1)
                        eng.wait_ge(S_("m_step"), count + 2)
                        eng.tensor_tensor(mrest[:, 0, :, :], mx[:, :, :], mparts[:, :, :, 0], ALU.subtract)\
                           .then_inc(S_("m_step"), 1)
                        eng.wait_ge(S_("m_step"), count + 3)
                        eng.tensor_copy(mparts[:, :, :, 1], mrest[:, 0, :, :]).then_inc(S_("m_step"), 1)
                        eng.wait_ge(S_("m_step"), count + 4)
                        eng.tensor_tensor(mrest[:, 1, :, :], mrest[:, 0, :, :], mparts[:, :, :, 1], ALU.subtract)\
                           .then_inc(S_("m_step"), 1)
                        eng.wait_ge(S_("m_step"), count + 5)
                        eng.tensor_copy(mparts[:, :, :, 2], mrest[:, 1, :, :]).then_inc(S_("m_step"), 1)

                    def rows_out(b, hg, pos, sl):
                        eng.wait_ge(S_("slot_made"), pos + 1)
                        if not is_group(b, hg, 0, 0):
                            pb, pg = plus(b, hg, -1)
                            eng.wait_ge(S_(f"m_in{pg}"), (pb + 1) * (16 * HG))
                        eng.tensor_copy(mrow[:, :], slot[sl].bitcast(bf16)[0:3 * HG, 0:S])\
                           .then_inc(S_("slot_read"), 1)

                    def normalise(b, hg, pos, sl):
                        q = b * NG + hg
                        eng.wait_ge(S_("slot_made"), pos + 1)
                        turned = slot[sl][:, 0:S].rearrange("p (i h c) -> p i h c", i=ST, h=HG)
                        eng.wait_ge(S_("attn_made"), ONE + q)
                        eng.reciprocal(rec[:, :, :], turned[:, :, :, DK]).then_inc(S_("rec_made"), 1)
                        eng.wait_ge(S_("rec_made"), q + 1)
                        eng.tensor_tensor(
                            a_st[:, :, hg * HG * DK:(hg + 1) * HG * DK]
                            .rearrange("p i (h c) -> p i h c", h=HG),
                            turned[:, :, :, 0:DK],
                            rec[:, :, :].rearrange("p i (h a) -> p i h a", a=1).broadcast_to([128, ST, HG, DK]),
                            ALU.mult).then_inc(S_("attn_made"), 1)
                        eng.wait_ge(S_("attn_made"), ONE + q + 1)
                        eng.sem_inc(S_("slot_read"), 1)

                    READ = dict(unit=maximum, turn=rows_out, output=normalise)

                    def group(b, hg):
                        for _, (kind, g, *more), pos, sl in numbered(b, hg):
                            if kind in TAIL_DVE:
                                TAIL_DVE[kind](eng, g[0], pos, sl)
                            else:
                                READ[kind](*g, *more, pos, sl)

                    eng.wait_ge(S_("wr_hi"), 1)
                    eng.tensor_tensor(wr_lo[:, :, :], wr_raw[:, :, :], wr_hi[:, :, :].bitcast(fp32), ALU.subtract)\
                       .then_inc(S_("wr_lo"), 1)
                    eng.wait_ge(S_("wo_hi"), 1)
                    eng.tensor_tensor(wo_lo[:, :, :], wo_raw[:, :, :], wo_hi[:, :, :].bitcast(fp32), ALU.subtract)\
                       .then_inc(S_("wo_lo"), 1)
                    eng.wait_ge(S_("tanh_made"), 1)

                    for pos, (kind, g, *more) in enumerate(PROLOGUE):
                        READ[kind](*g, *more, pos, pos % 2)
                    over_groups(eng, group)
                    normalise(B - 1, NG - 1, LAST_OUTPUT, slot_of(B - 1, NG - 1, 1))

                @block.tensor
                def _(eng):
                    def max_unit(b, hg, u, pos, sl):
                        h, st, half = u // (2 * ST), u // 2 % ST, u % 2
                        if u == 0:
                            eng.wait_ge(S_(f"q_in{hg}"), (b + 1) * (16 * NB))
                            eng.wait_ge(S_(f"k_in{hg}"), (b + 1) * (16 * NB))
                        eng.wait_ge(S_("slot_read"), not_below_zero(pos - 1))
                        lo_, hi_ = (HALF, T) if half else (0, HALF)
                        for o in range(lo_, hi_, 512):
                            w = min(512, hi_ - o)
                            last = eng.matmul(slot[sl][:, o - lo_:o - lo_ + w],
                                              q_st[hg][0:KS, h, 128 * st:128 * st + 128],
                                              k_st[hg][0:KS, h, o:o + w], start=True, stop=True)
                        last.then_inc(S_("slot_made"), 1)

                    def turn_max(b, hg, pos, sl):
                        eng.wait_ge(S_("m_step"), (b * NG + hg) * 6 + 6)
                        eng.wait_ge(S_("slot_read"), pos - 1)
                        for i in range(ST):
                            last = eng.transpose(slot[sl].bitcast(bf16)[0:3 * HG, 128 * i:128 * i + 128],
                                                 mparts[:, i, :, :].rearrange("p h c -> p (h c)"), ident_bf[:, :])
                        last.then_inc(S_("slot_made"), 1)

                    def turn_output(b, hg, pos, sl):
                        eng.wait_ge(S_("o_copied"), b * NG + hg + 1)
                        eng.wait_ge(S_("slot_read"), pos - 1)
                        for i in range(ST):
                            last = eng.transpose(slot[sl][:, 128 * i:128 * i + 128], o_sb[:, 128 * i:128 * i + 128],
                                                 ident[:, :])
                        last.then_inc(S_("slot_made"), 1)

                    MAKE = dict(unit=max_unit, turn=turn_max, output=turn_output)

                    def scores(b, hg, n, h):
                        tt, rows = hg * TN + n, tile_rows(n)
                        i = tt * HG + h
                        eng.wait_ge(S_("exp_made"), b * EXPS + (i - 2 if i > 2 else 0))
                        eng.matmul(bank[4 + i % 3][0:rows, :], k_st[hg][0:KM, h, n * TP:n * TP + rows],
                                   q_st[hg][0:KM, h, :], start=True, stop=True).then_inc(S_("scores_made"), 1)

                    def weigh_v(b, hg, n):
                        tt, rows = hg * TN + n, tile_rows(n)
                        if n == 0:
                            eng.wait_ge(S_("o_copied"), b * NG + hg)
                            eng.wait_ge(S_(f"v_in{hg % 2}"), b * 32 + (hg // 2 + 1) * 16)
                        eng.wait_ge(S_("exp_made"), b * EXPS + (tt * HG + HG))
                        for h in range(HG):
                            last = eng.matmul(pv_acc[STRIP * h:STRIP * h + STRIP, :],
                                              v_st[hg % 2][0:rows, n, STRIP * h:STRIP * h + STRIP],
                                              prob[tt % PR][0:rows, h, :], start=(n == 0), stop=(n == TN - 1))
                        last.then_inc(S_("pv_tile"), 1)

                    def group(b, hg):
                        eng.wait_ge(S_(f"m_in{hg}"), (b + 1) * (16 * HG))
                        items = [it for it in numbered(b, hg) if it[1][0] in MAKE or it[1][0] in TAIL_PE]
                        for n in range(TN):
                            todo = [it for it in items if it[0] == n]

                            def one():
                                if todo:
                                    _, (kind, g, *more), pos, sl = todo.pop(0)
                                    if kind in TAIL_PE:
                                        TAIL_PE[kind](eng, g[0], pos, sl)
                                    else:
                                        MAKE[kind](*g, *more, pos, sl)

                            if n >= LAG_V:
                                weigh_v(b, hg, n - LAG_V)
                            elif not is_group(b, hg, 0, 0):
                                weigh_v(*plus(b, hg, -1), TN + n - LAG_V)
                            one()
                            scores(b, hg, n, 0)
                            scores(b, hg, n, 1)
                            one()
                            scores(b, hg, n, 2)
                            scores(b, hg, n, 3)
                            while todo:
                                one()

                    for pos, (kind, g, *more) in enumerate(PROLOGUE):
                        MAKE[kind](*g, *more, pos, pos % 2)
                    eng.wait_ge(S_("minus_ones"), NG)
                    over_groups(eng, group)
                    for n in range(TN - LAG_V, TN):
                        weigh_v(B - 1, NG - 1, n)
                    turn_output(B - 1, NG - 1, LAST_OUTPUT, slot_of(B - 1, NG - 1, 1))

        w1, w2 = [[[sb(f"{n}_{p}{i}", shape, f32r) for p in ("hi", "lo")] for i in range(2)]
                  for n, shape in (("w1", [128, KT, F]), ("w2", [128, FT, D]))]
        b2_b = [bv_b[:, :], wo_raw[:, 0, :]]

        def load_bias(eng, e, par, first):
            if not first:
                eng.wait_ge(S_("y_read"), ONE + (e - 1) * NTB * 2)
            eng.dma_start(b2_b[par], b2[e, :].rearrange("(a d) -> a d", a=1).broadcast_to([128, D]))\
               .then_inc(S_(f"b2_in{par}"), 16)

        def split_expert(eng, e, par):
            wait_apart(eng, S_("y_made"), ONE + (e - 1) * NTB * FT)
            for j, (raw, pair, name) in enumerate(((w1_raw, w1[par], "w1_in"), (w2_raw, w2[par], "w2_in"))):
                wait_apart(eng, S_(name), (e + 1) * 16)
                eng.tensor_copy(pair[0][:, :, :], raw[:, :, :]).then_inc(S_("w_split"), 1)
                eng.wait_ge(S_("w_split"), e * 4 + 2 * j + 1)
                eng.tensor_tensor(pair[1][:, :, :], raw[:, :, :], pair[0][:, :, :].bitcast(fp32),
                                  ALU.subtract).then_inc(S_("w_split"), 1)

        WEIGHTS = [((w1_raw, w1[par], "w1_in"), (w2_raw, w2[par], "w2_in")) for par in range(2)]

        def weights_hi(eng, e, j):
            raw, parts, name = WEIGHTS[e][j]
            eng.wait_ge(S_(name), 16 * (e + 1))
            eng.activation(parts[0][:, :, :], raw[:, :, :], ACT.Copy).then_inc(S_("w_first_hi"), 1)

        def weights_lo(eng, e, j):
            raw, parts, _ = WEIGHTS[e][j]
            eng.wait_ge(S_("w_first_hi"), 2 * e + j + 1)
            eng.tensor_tensor(parts[1][:, :, :], raw[:, :, :], parts[0][:, :, :].bitcast(fp32),
                              ALU.subtract).then_inc(S_("w_split"), 2)

        def last_tail(steps, eng, kind):
            for k, (b, hg), pos, sl in LAST_TAIL:
                if k == kind:
                    steps[kind](eng, b, pos, sl)

        with ExitStack() as ph:
            def sb2(name, shape, dt=fp32):
                return ph.enter_context(nc.sbuf_tensor(name, shape, dt))

            HR = 4
            r_sb = [again(early[i // 2][1][:, i % 2 * 2:i % 2 * 2 + 2, :], fp32, TBS) for i in range(HR)]
            h_hi, h_lo = [[sb2(f"h_{p}{i}", [128, TBS], f32r)[:, :] for i in range(HR)] for p in ("hi", "lo")]
            y_sb = y_st
            acc = sb2("acc", [128, NT, D])
            xs, zz, z2, gate = [o_sb[:, NT * E * i:NT * E * i + NT * E].rearrange("p (n e) -> p n e", n=NT)
                                for i in range(4)]
            tau = sb2("tau", [128, NT, 1])
            tau_m = sb2("tau_m", [128, NT, 1])
            dm = sb2("dm", [128, NT, 1])
            f_lo = sb2("f_lo", [128, NT, 1])
            f_m = sb2("f_m", [128, NT, 1])
            f_s = sb2("f_s", [128, NT, 1])
            top = sb2("top", [128, NT, 1])
            LAG = 3
            TURN_F = FT - 2

            def rest_of_hidden(eng, n, f, wait=None):
                (wait or eng.wait_ge)(S_("relu_made"), ONE + n * FT + f + 1)
                eng.tensor_tensor(h_lo[f % HR], r_sb[f % HR], h_hi[f % HR].bitcast(fp32),
                                  ALU.subtract).then_inc(S_("h_lo"), 1)

            with nc.Block() as block:
                @block.sync
                def _(eng):
                    load_bias(eng, 0, 0, True)
                    load_bias(eng, 1, 1, True)
                    eng.wait_ge(S_("w_split"), 4)
                    load_expert(eng, 1)
                    with eng.Fori(1, E // 2) as pair:
                        e = pair * 2
                        for par in range(2):
                            eng.wait_ge(S_("w_split"), (e + par) * 4)
                            load_expert(eng, e + par)
                            load_bias(eng, e + par, par, False)
                    for t in range(NTB):
                        eng.wait_ge(S_("out_made"), t + 1)
                        eng.dma_start(out[t, :, :].rearrange("(i p) d -> p i d", p=128),
                                      acc[:, ST * t:ST * t + ST, :]).then_inc(S_("out_done"), 16)
                    eng.wait_ge(S_("out_done"), 16 * NTB)

                @block.gpsimd
                def _(eng):
                    inverse_deviation(eng, B - 1)
                    for j in range(2):
                        weights_lo(eng, 1, j)
                    with eng.Fori(1, NTB + 1) as t:
                        for f in range(FT):
                            rest_of_hidden(eng, t, f, lambda semaphore, value: wait_apart(eng, semaphore, value))
                    with eng.Fori(1, E // 2) as pair:
                        e = pair * 2
                        split_expert(eng, e, 0)
                        split_expert(eng, e + 1, 1)

                @block.scalar
                def _(eng):
                    def block_of(e, t, also=None):
                        blk = e * (NTB * FT) + t * FT
                        for f in range(FT):
                            if also:
                                also(f)
                            eng.wait_ge(S_("h_made"), blk + f + 1)
                            eng.wait_ge(S_("y_made"), ONE + blk + (f - HR + 1 if f >= HR else 0))
                            bias = b1_c[:, bass.ds(e * FT + f, 1)]
                            eng.activation(r_sb[f % HR], bank[f % HR], ACT.Relu, bias=bias)
                            eng.activation(h_hi[f % HR], bank[f % HR], ACT.Relu, bias=bias)\
                               .then_inc(S_("relu_made"), 1)

                    def also(f):
                        if f == TURN_F:
                            last_tail(TAIL_ACT, eng, "y_turn")
                            eng.wait_ge(S_("rows_hi"), B * 2)
                            eng.activation(x2T_hi[:, :, S * (B - 1):S * B], rT_hi[:, :, :].bitcast(fp32), ACT.Copy)\
                               .then_inc(S_("y_kept"), 1)
                        elif f == TURN_F + 1:
                            weights_hi(eng, 1, 0)

                    last_tail(TAIL_ACT, eng, "attn_turn")
                    for j in range(2):
                        weights_hi(eng, 0, j)
                    block_of(0, 0, also)
                    weights_hi(eng, 1, 1)
                    with eng.Fori(1, NTB) as t:
                        block_of(0, t)
                    with eng.Fori(1, E) as e:
                        with eng.Fori(0, NTB) as t:
                            block_of(e, t)

                @block.vector
                def _(eng):
                    def chained(count, ops, together=()):
                        for i, op in enumerate(ops):
                            op().then_inc(S_("bisect"), 1)
                            if i not in together:
                                wait_apart(eng, S_("bisect"), count + (i + 1))

                    def total(dst, tau_):
                        return [
                            lambda: eng.tensor_tensor(zz[:, :, :], xs[:, :, :],
                                                      tau_[:, :, :].broadcast_to([128, NT, E]), ALU.subtract),
                            lambda: eng.scalar_tensor_tensor(z2[:, :, :], zz[:, :, :], 0.0, zz[:, :, :],
                                                             ALU.max, ALU.mult),
                            lambda: eng.tensor_reduce(dst[:, :, :], z2[:, :, :], AX.X, ALU.add)]

                    START = [
                        lambda: eng.tensor_scalar(xs[:, :, :], logits[:, :, :], 0.5, None, ALU.mult),
                        lambda: eng.tensor_reduce(top[:, :, :], xs[:, :, :], AX.X, ALU.max),
                        lambda: eng.tensor_scalar(tau[:, :, :], top[:, :, :], -1.0, None, ALU.add),
                        lambda: eng.scalar_tensor_tensor(dm[:, :, :], top[:, :, :], -((1.0 / E) ** 0.5), tau[:, :, :],
                                                         ALU.add, ALU.subtract),
                        *total(f_lo, tau),
                        lambda: eng.tensor_scalar(f_lo[:, :, :], f_lo[:, :, :], -1.0, None, ALU.add),
                        lambda: eng.tensor_scalar(dm[:, :, :], dm[:, :, :], 0.5, None, ALU.mult)]
                    HALVING = [
                        lambda: eng.tensor_tensor(tau_m[:, :, :], tau[:, :, :], dm[:, :, :], ALU.add),
                        *total(f_m, tau_m),
                        lambda: eng.scalar_tensor_tensor(f_s[:, :, :], f_m[:, :, :], -1.0, f_lo[:, :, :],
                                                         ALU.add, ALU.mult),
                        lambda: eng.scalar_tensor_tensor(f_s[:, :, :], f_s[:, :, :], 0.0, dm[:, :, :],
                                                         ALU.is_ge, ALU.mult),
                        lambda: eng.tensor_tensor(tau[:, :, :], tau[:, :, :], f_s[:, :, :], ALU.add),
                        lambda: eng.tensor_scalar(dm[:, :, :], dm[:, :, :], 0.5, None, ALU.mult)]
                    TOGETHER = (len(HALVING) - 2,)
                    NORMALISE = [
                        lambda: eng.reciprocal(f_m[:, :, :], f_m[:, :, :]),
                        lambda: eng.tensor_tensor(z2[:, :, :], z2[:, :, :],
                                                  f_m[:, :, :].broadcast_to([128, NT, E]), ALU.mult),
                        lambda: eng.scalar_tensor_tensor(gate[:, :, :], z2[:, :, :], THRESH, z2[:, :, :],
                                                         ALU.is_gt, ALU.mult)]
                    PER = 7

                    def halvings_from(k, n=1):
                        for i in range(n):
                            chained((k + i) * len(HALVING) + len(START), HALVING, TOGETHER)

                    def hidden_rest(n):
                        for f in range(FT):
                            rest_of_hidden(eng, n, f)

                    def outputs(pair, par, t, first):
                        n = (pair * 2 + par) * NTB + t
                        eng.wait_ge(S_("y_made"), ONE + n * FT + FT)
                        eng.wait_ge(S_(f"b2_in{par}"), (pair + 1) * 16)
                        for j in range(ST // 2):
                            dst = acc[:, bass.ds(t * ST + 2 * j, 2), :] if first else y_sb[:, 2 * j:2 * j + 2, :]
                            eng.tensor_tensor(dst, bank[4 + j].rearrange("p (i d) -> p i d", i=2),
                                              b2_b[par].rearrange("p (a d) -> p a d", a=1)
                                              .broadcast_to([128, 2, D]), ALU.add).then_inc(S_("y_read"), 1)
                        eng.wait_ge(S_("y_read"), ONE + n * 2 + 2)

                    def weigh(e, t):
                        for i in range(ST):
                            rows = acc[:, bass.ds(t * ST + i, 1), :].rearrange("p a d -> p (a d)")
                            g = gate[:, bass.ds(t * ST + i, 1), bass.ds(e, 1)].rearrange("p a b -> p (a b)")
                            last = eng.scalar_tensor_tensor(rows, y_sb[:, i, :], g, rows, ALU.mult, ALU.add)
                        last.then_inc(S_("block_done"), 1)

                    AFTER = {1: ("residual",), 2: ("row_stats",), 4: ("y_norm",), TURN_F - 1: ("y_turn",)}
                    last_tail(TAIL_DVE, eng, "attn_turn")
                    weights_lo(eng, 0, 0)
                    last_tail(TAIL_DVE, eng, "out_proj")
                    weights_lo(eng, 0, 1)
                    for f in range(FT):
                        rest_of_hidden(eng, 0, f)
                        for kind in AFTER.get(f, ()):
                            last_tail(TAIL_DVE, eng, kind)
                            if kind == "y_turn":
                                eng.wait_ge(S_("rows_lo"), B * 2)
                                eng.tensor_copy(x2T_lo[:, :, S * (B - 1):S * B], rT_lo[:, :, :].bitcast(fp32))\
                                   .then_inc(S_("y_kept"), 1)
                    outputs(0, 0, 0, True)
                    last_tail(TAIL_DVE, eng, "route")
                    eng.wait_ge(S_("slot_read"), LAST_TAIL[-1][2] + 1)
                    chained(0, START)
                    with eng.Fori(1, NTB) as t:
                        halvings_from(t * PER - PER, PER)
                        outputs(0, 0, t, True)

                    def expert(pair, par, last=False):
                        e = pair * 2 + par
                        with eng.Fori(0, NTB) as t:
                            eng.wait_ge(S_("block_done"), (e - 1) * NTB + t)
                            hidden_rest(e * NTB + t)
                            outputs(pair, par, t, False)
                            weigh(e, t)
                            if last:
                                add_to_x(t)

                    def add_to_x(t):
                        eng.wait_ge(S_("block_done"), (E - 2) * NTB + t + 1)
                        rows = acc[:, bass.ds(t * ST, ST), :].rearrange("p i d -> p (i d)")
                        eng.scalar_tensor_tensor(rows, rows, tg[:, 1:2],
                                                 x_all[:, bass.ds(t * ST, ST), :].rearrange("p i d -> p (i d)"),
                                                 ALU.mult, ALU.add).then_inc(S_("out_made"), 1)

                    done = PER * (NTB - 1)
                    halvings_from(done, BISECT - done)
                    chained(len(START) + BISECT * len(HALVING), NORMALISE)
                    for i in range(NT):
                        last = eng.tensor_scalar(acc[:, i, :], acc[:, i, :], gate[:, i, 0:1], None, ALU.mult)
                    last.then_inc(S_("first_weighed"), 1)
                    eng.wait_ge(S_("first_weighed"), 1)
                    outputs(0, 1, 0, False)
                    weigh(1, 0)
                    with eng.Fori(1, NTB) as t:
                        eng.wait_ge(S_("block_done"), t)
                        hidden_rest(NTB + t)
                        outputs(0, 1, t, False)
                        weigh(1, t)
                    with eng.Fori(1, E // 2 - 1) as pair:
                        for par in range(2):
                            expert(pair, par)
                    expert(E // 2 - 1, 0)
                    expert(E // 2 - 1, 1, last=True)

                @block.tensor
                def _(eng):
                    def token_block(e, t, par, before={}):
                        n = e * NTB + t

                        def hidden(f):
                            eng.wait_ge(S_("relu_made"), ONE + n * FT + (f - HR + 1 if f >= HR else 0))
                            i = 0
                            for k in range(KT):
                                for a, c in ((0, 0), (0, 1), (1, 0)):
                                    last = eng.matmul(bank[f % HR], w1[par][a][:, k, 128 * f:128 * f + 128],
                                                      (x2T_hi, x2T_lo)[c][:, k, bass.ds(t * TBS, TBS)],
                                                      start=(i == 0), stop=(i == 3 * KT - 1))
                                    i += 1
                            last.then_inc(S_("h_made"), 1)

                        def project(f):
                            eng.wait_ge(S_("h_lo"), n * FT + f + 1)
                            if f == 0:
                                eng.wait_ge(S_("y_read"), ONE + n * 2)
                            for i in range(ST):
                                for a, c in ((0, 0), (0, 1), (1, 0)):
                                    first = f == 0 and (a, c) == (0, 0)
                                    last = eng.matmul(
                                        bank[4 + i // 2][:, D * (i % 2):D * (i % 2) + D],
                                        (h_hi, h_lo)[a][f % HR][:, 128 * i:128 * i + 128], w2[par][c][:, f, :],
                                        start=(first and i % 2 == 0), stop=(f == FT - 1 and (a, c) == (1, 0)),
                                        skip_group_check=True)
                            last.then_inc(S_("y_made"), 1)

                        for f in range(FT + LAG):
                            if f in before:
                                before[f]()
                            if f < FT:
                                hidden(f)
                            if f >= LAG:
                                project(f - LAG)

                    def w2_there():
                        eng.wait_ge(S_("w_split"), 4)

                    last_tail(TAIL_PE, eng, "attn_turn")
                    last_tail(TAIL_PE, eng, "out_proj")
                    eng.wait_ge(S_("w_split"), 2)
                    token_block(0, 0, 0, {LAG: w2_there,
                                          TURN_F: lambda: last_tail(TAIL_PE, eng, "y_turn")})
                    token_block(0, 1, 0, {0: lambda: last_tail(TAIL_PE, eng, "route")})
                    token_block(0, 2, 0)
                    eng.wait_ge(S_("y_kept"), ONE + B * 2)
                    token_block(0, 3, 0)
                    eng.wait_ge(S_("w_split"), 8)
                    for t in range(NTB):
                        token_block(1, t, 1)
                    with eng.Fori(1, E // 2) as pair:
                        e = pair * 2
                        for par in range(2):
                            wait_apart(eng, S_("w_split"), (e + (par + 1)) * 4)
                            for t in range(NTB):
                                token_block(e + par, t, par)


_INS = ['x', 'ctx_1024', 'g_xattn', 'g_ffn', 'L0_xattn_wq', 'L0_xattn_bq', 'L0_xattn_wk', 'L0_xattn_bk',
        'L0_xattn_wv', 'L0_xattn_bv', 'L0_xattn_wo', 'L0_xattn_bo', 'L0_ffn_Wr', 'L0_ffn_br', 'L0_ffn_W1',
        'L0_ffn_b1', 'L0_ffn_W2', 'L0_ffn_b2']


def kernel(**inputs):
    import numpy as _np
    import concourse.bacc as _bacc
    from concourse import mybir as _mybir
    from concourse.bass_utils import run_bass_kernel_spmd as _run

    nc = _bacc.Bacc("TRN2", target_bir_lowering=False, num_devices=1)
    arrays, args = {}, []
    for name in _INS:
        a = _np.ascontiguousarray(inputs[name])
        arrays[f"in_{name}"] = a
        args.append(nc.dram_tensor(f"in_{name}", a.shape, _mybir.dt.from_np(a.dtype), kind="ExternalInput").ap())
    x = inputs['x']
    out = nc.dram_tensor("out_0", tuple(x.shape), _mybir.dt.from_np(_np.dtype('float32')), kind="ExternalOutput").ap()
    flamingo_block(nc, *args, out)
    r = _run(nc, [arrays], core_ids=[0])
    return r.results[0]["out_0"]
```
